# Optimizing a Trainium2 kernel written in Bass

```python
import numpy as np
import jax
import jax.numpy as jnp

def _softmax(x, axis=-1):
    return jax.nn.softmax(x, axis=axis)

def _gelu(x):
    return jax.nn.gelu(x, approximate=True)

def _silu(x):
    return jax.nn.silu(x)

def _sigmoid(x):
    return jax.nn.sigmoid(x)

def _layernorm(x, axis=-1, eps=1e-05):
    m = jnp.mean(x, axis=axis, keepdims=True)
    v = jnp.var(x, axis=axis, keepdims=True)
    return (x - m) / jnp.sqrt(v + eps)

def _scatter_add(tgt, idx, src, axis=0):
    return tgt.at[idx].add(src)

def _segment_sum(src, seg, n):
    return jax.ops.segment_sum(src, seg, n)
kernel_name = 'mk_flamingo_gated_d2_seqx_r4_7ecab4'

def setup_inputs(seed: int=0):
    np.random.seed(seed)
    _w = jnp.asarray

    def _rec_inputs():
        import jax
        import jax.numpy as jnp
        _rk = jax.random.key(seed)
        x = -0.0002928 + 1 * jax.random.normal(jax.random.fold_in(_rk, 1), (16, 112, 256), jnp.float32)
        _lenS = 112 - jax.random.randint(jax.random.fold_in(_rk, 7), (16,), 0, max(1, 112 // 4) + 1, jnp.int32)
        _lenS2 = 375 - jax.random.randint(jax.random.fold_in(_rk, 8), (16,), 0, max(1, 375 // 4) + 1, jnp.int32)
        _ctx_1024P = jax.random.normal(jax.random.fold_in(_rk, 11), (16, 16, 256), jnp.float32)
        _ctx_1024c = jax.random.dirichlet(jax.random.fold_in(_rk, 511), 0.3 * jnp.ones((16,), jnp.float32), (16, 375))
        _ctx_1024t = jnp.einsum('bsk,bkd->bsd', _ctx_1024c, _ctx_1024P)
        _ctx_1024t = _ctx_1024t * jax.lax.rsqrt(jnp.mean(jnp.square(_ctx_1024t)) + 1e-12) * 0.953939
        ctx_1024 = -1.39393e-06 + 0.999914 * (_ctx_1024t + 0.3 * jax.random.normal(jax.random.fold_in(_rk, 611), (16, 375, 256), jnp.float32))
        _validS = jnp.arange(112)[None, :] < _lenS[:, None]
        _validS2 = jnp.arange(375)[None, :] < _lenS2[:, None]
        _causal = jnp.tril(jnp.ones((112, 112), dtype=bool))
        mask_BxSxS2_ff1 = jnp.where(jnp.ones((16, 112, 375), dtype=bool), 1.0, 0.0).astype(jnp.float32)
        mask_BxS2_bk0 = jnp.logical_not(jnp.broadcast_to(_validS2[:, :], (16, 375)))
        _g = jax.random.normal(jax.random.fold_in(_rk, 9001), (2, 2), jnp.float32)
        _g = jnp.sign(_g) * jnp.maximum(jnp.abs(_g), 1.0) + (_g == 0) * 1.0
        g_xattn = _g[0]
        g_ffn = _g[1]
        return (x, ctx_1024, mask_BxSxS2_ff1, mask_BxS2_bk0, g_xattn, g_ffn)
    x, ctx_1024, mask_BxSxS2_ff1, mask_BxS2_bk0, g_xattn, g_ffn = _rec_inputs()

    def _L0_xattn_setup():
        import jax, jax.numpy as jnp
        import numpy as np
        HIDDEN = 256
        NUM_HEADS = 16
        HEAD_DIM = HIDDEN // NUM_HEADS
        B, LQ, LK = (2, 512, 512)

        def _split_heads(x):
            b, l, _ = x.shape
            return x.reshape(b, l, NUM_HEADS, HEAD_DIM).transpose(0, 2, 1, 3)
        key = jax.random.key(seed)
        ks = jax.random.split(key, 9)
        s = 1.0 / np.sqrt(HIDDEN)
        return {'hidden_states_query': jax.random.normal(ks[0], (B, LQ, HIDDEN), jnp.float32), 'hidden_states_key': jax.random.normal(ks[1], (B, LK, HIDDEN), jnp.float32), 'attention_mask': jnp.ones((B, LQ, LK), jnp.float32), 'Wq': jax.random.normal(ks[2], (HIDDEN, HIDDEN), jnp.float32) * s, 'bq': jax.random.normal(ks[3], (HIDDEN,), jnp.float32) * s, 'Wk': jax.random.normal(ks[4], (HIDDEN, HIDDEN), jnp.float32) * s, 'bk': jax.random.normal(ks[5], (HIDDEN,), jnp.float32) * s, 'Wv': jax.random.normal(ks[6], (HIDDEN, HIDDEN), jnp.float32) * s, 'bv': jax.random.normal(ks[7], (HIDDEN,), jnp.float32) * s}
    _L0_xattn_all = _L0_xattn_setup()
    _L0_xattn_in = {k: v for k, v in _L0_xattn_all.items() if k in ('Wq', 'bq', 'Wk', 'bk', 'Wv', 'bv')}
    del _L0_xattn_all

    def _L0_ffn_setup():
        import jax, jax.numpy as jnp
        import numpy as np
        B, S, D_IN, D_OUT, E, K = (2, 512, 256, 256, 8, 2)
        key = jax.random.key(seed)
        k1, k2, k3, k4 = jax.random.split(key, 4)
        scale = 1.0 / np.sqrt(D_IN)
        return {'inputs': jax.random.normal(k1, (B, S, D_IN), dtype=jnp.float32), 'Wg': jax.random.normal(k2, (E, D_IN), dtype=jnp.float32) * scale, 'We': jax.random.normal(k3, (E, D_OUT, D_IN), dtype=jnp.float32) * scale, 'be': jax.random.normal(k4, (E, D_OUT), dtype=jnp.float32) * scale}
    _L0_ffn_all = _L0_ffn_setup()
    _L0_ffn_in = {k: v for k, v in _L0_ffn_all.items() if k in ('Wg', 'We', 'be')}
    del _L0_ffn_all

    def _L1_xattn_setup():
        import jax, jax.numpy as jnp
        import numpy as np
        EPS = 1e-05

        def layer_norm(x, g, b):
            mu = jnp.mean(x, axis=-1, keepdims=True)
            var = jnp.mean((x - mu) ** 2, axis=-1, keepdims=True)
            return (x - mu) * jax.lax.rsqrt(var + EPS) * g + b
        key = jax.random.key(seed)
        ks = jax.random.split(key, 8)
        b, n, l, D = (8, 1024, 64, 256)
        heads, dim_head = (16, 64)
        inner = heads * dim_head
        x = jax.random.normal(ks[0], (b, n, D), dtype=jnp.float32)
        latents = jax.random.normal(ks[1], (b, l, D), dtype=jnp.float32)
        mask = jax.random.randint(ks[2], (b, n), 0, 2) > 0
        Wq = jax.random.normal(ks[3], (D, inner), dtype=jnp.float32) * D ** (-0.5)
        Wkv = jax.random.normal(ks[4], (D, 2 * inner), dtype=jnp.float32) * D ** (-0.5)
        Wout = jax.random.normal(ks[5], (inner, D), dtype=jnp.float32) * inner ** (-0.5)
        g1 = jnp.ones((D,), jnp.float32)
        b1 = jnp.zeros((D,), jnp.float32)
        g2 = jnp.ones((D,), jnp.float32)
        b2 = jnp.zeros((D,), jnp.float32)
        return {'x': x, 'latents': latents, 'mask': mask, 'g1': g1, 'b1': b1, 'g2': g2, 'b2': b2, 'Wq': Wq, 'Wkv': Wkv, 'Wout': Wout}
    _L1_xattn_all = _L1_xattn_setup()
    _L1_xattn_in = {k: v for k, v in _L1_xattn_all.items() if k in ('g1', 'b1', 'g2', 'b2', 'Wq', 'Wkv', 'Wout')}
    del _L1_xattn_all

    def _L1_ffn_setup():
        import jax, jax.numpy as jnp
        import numpy as np
        D = 256
        H = 512
        E = 8
        K = 2
        B, T = (4, 512)
        key = jax.random.key(seed)
        ks = jax.random.split(key, 7)
        s = 0.02
        return {'x': jax.random.normal(ks[0], (B, T, D), dtype=jnp.float32), 'W1': jax.random.normal(ks[1], (E, D, 2 * H), dtype=jnp.float32) * s, 'b1': jnp.zeros((E, 2 * H), dtype=jnp.float32), 'W2': jax.random.normal(ks[2], (E, H, D), dtype=jnp.float32) * s, 'b2': jnp.zeros((E, D), dtype=jnp.float32), 'Wr': jax.random.normal(ks[3], (D, E), dtype=jnp.float32) * s, 'br': jnp.zeros((E,), dtype=jnp.float32)}
    _L1_ffn_all = _L1_ffn_setup()
    _L1_ffn_in = {k: v for k, v in _L1_ffn_all.items() if k in ('W1', 'b1', 'W2', 'b2', 'Wr', 'br')}
    del _L1_ffn_all
    return {'x': x, 'ctx_1024': ctx_1024, 'mask_BxSxS2_ff1': mask_BxSxS2_ff1, 'mask_BxS2_bk0': mask_BxS2_bk0, 'g_xattn': g_xattn, 'g_ffn': g_ffn, 'L0_xattn_Wq': _L0_xattn_in['Wq'], 'L0_xattn_bq': _L0_xattn_in['bq'], 'L0_xattn_Wk': _L0_xattn_in['Wk'], 'L0_xattn_bk': _L0_xattn_in['bk'], 'L0_xattn_Wv': _L0_xattn_in['Wv'], 'L0_xattn_bv': _L0_xattn_in['bv'], 'L0_ffn_Wg': _L0_ffn_in['Wg'], 'L0_ffn_We': _L0_ffn_in['We'], 'L0_ffn_be': _L0_ffn_in['be'], 'L1_xattn_g1': _L1_xattn_in['g1'], 'L1_xattn_b1': _L1_xattn_in['b1'], 'L1_xattn_g2': _L1_xattn_in['g2'], 'L1_xattn_b2': _L1_xattn_in['b2'], 'L1_xattn_Wq': _L1_xattn_in['Wq'], 'L1_xattn_Wkv': _L1_xattn_in['Wkv'], 'L1_xattn_Wout': _L1_xattn_in['Wout'], 'L1_ffn_W1': _L1_ffn_in['W1'], 'L1_ffn_b1': _L1_ffn_in['b1'], 'L1_ffn_W2': _L1_ffn_in['W2'], 'L1_ffn_b2': _L1_ffn_in['b2'], 'L1_ffn_Wr': _L1_ffn_in['Wr'], 'L1_ffn_br': _L1_ffn_in['br']}

def reference(x, ctx_1024, mask_BxSxS2_ff1, mask_BxS2_bk0, g_xattn, g_ffn, L0_xattn_Wq, L0_xattn_bq, L0_xattn_Wk, L0_xattn_bk, L0_xattn_Wv, L0_xattn_bv, L0_ffn_Wg, L0_ffn_We, L0_ffn_be, L1_xattn_g1, L1_xattn_b1, L1_xattn_g2, L1_xattn_b2, L1_xattn_Wq, L1_xattn_Wkv, L1_xattn_Wout, L1_ffn_W1, L1_ffn_b1, L1_ffn_W2, L1_ffn_b2, L1_ffn_Wr, L1_ffn_br):
    import jax
    import jax.numpy as jnp

    def _L0_xattn_ref(hidden_states_query, hidden_states_key, attention_mask, Wq, bq, Wk, bk, Wv, bv):
        import jax, jax.numpy as jnp
        import numpy as np
        HIDDEN = 256
        NUM_HEADS = 16
        HEAD_DIM = HIDDEN // NUM_HEADS
        B, LQ, LK = (2, 512, 512)

        def _split_heads(x):
            b, l, _ = x.shape
            return x.reshape(b, l, NUM_HEADS, HEAD_DIM).transpose(0, 2, 1, 3)
        q = _split_heads(hidden_states_query @ Wq.T + bq)
        k = _split_heads(hidden_states_key @ Wk.T + bk)
        v = _split_heads(hidden_states_key @ Wv.T + bv)
        scale = 1.0 / np.sqrt(HEAD_DIM)
        scores = jnp.einsum('bhqd,bhkd->bhqk', q * scale, k)
        scores = scores + ((1.0 - attention_mask) * -10000.0)[:, None, :, :]
        probs = jax.nn.softmax(scores, axis=-1)
        ctx = jnp.einsum('bhqk,bhkd->bhqd', probs, v)
        b, h, lq, d = ctx.shape
        return ctx.transpose(0, 2, 1, 3).reshape(b, lq, h * d)

    def _L0_ffn_ref(inputs, Wg, We, be):
        import jax, jax.numpy as jnp
        import numpy as np
        B, S, D_IN, D_OUT, E, K = (2, 512, 256, 256, 8, 2)
        logits = jnp.einsum('bsd,ed->bse', inputs, Wg)
        topw, sel = jax.lax.top_k(logits, K)
        topw = jax.nn.softmax(topw.astype(jnp.float32), axis=-1).astype(inputs.dtype)
        cw = jnp.sum(jax.nn.one_hot(sel, E, dtype=topw.dtype) * topw[..., None], axis=-2)
        y = jnp.einsum('bsd,eod->bseo', inputs, We) + be
        return jnp.einsum('bseo,bse->bso', y, cw)

    def _L1_xattn_ref(x, latents, mask, g1, b1, g2, b2, Wq, Wkv, Wout):
        import jax, jax.numpy as jnp
        import numpy as np
        EPS = 1e-05

        def layer_norm(x, g, b):
            mu = jnp.mean(x, axis=-1, keepdims=True)
            var = jnp.mean((x - mu) ** 2, axis=-1, keepdims=True)
            return (x - mu) * jax.lax.rsqrt(var + EPS) * g + b
        heads, dim_head = (16, 64)
        b, n, D = x.shape
        l = latents.shape[1]
        xn = layer_norm(x, g1, b1)
        ln_lat = layer_norm(latents, g2, b2)
        q = ln_lat @ Wq
        kv = jnp.concatenate([xn, ln_lat], axis=1) @ Wkv
        k, v = jnp.split(kv, 2, axis=-1)

        def to_heads(t):
            return t.reshape(t.shape[0], t.shape[1], heads, dim_head).transpose(0, 2, 1, 3)
        q, k, v = (to_heads(q), to_heads(k), to_heads(v))
        scale = 1.0 / np.sqrt(np.sqrt(dim_head)).astype(np.float32)
        weight = jnp.einsum('bhld,bhnd->bhln', q * scale, k * scale)
        full_mask = jnp.concatenate([mask, jnp.ones((b, l), dtype=bool)], axis=1)
        neg = -jnp.finfo(weight.dtype).max
        weight = jnp.where(full_mask[:, None, None, :], weight, neg)
        weight = jax.nn.softmax(weight.astype(jnp.float32), axis=-1).astype(q.dtype)
        out = jnp.einsum('bhln,bhnd->bhld', weight, v)
        out = out.transpose(0, 2, 1, 3).reshape(b, l, heads * dim_head)
        return out @ Wout

    def _L1_ffn_ref(x, W1, b1, W2, b2, Wr, br):
        import jax, jax.numpy as jnp
        import numpy as np
        D = 256
        H = 512
        E = 8
        K = 2
        B, T = (4, 512)
        Bb, Tt, Dd = x.shape
        xf = x.reshape(-1, Dd)
        logits = xf @ Wr + br
        topk_val, topk_idx = jax.lax.top_k(logits, K)
        scores = jax.nn.softmax(topk_val, axis=-1)
        h = jnp.einsum('nd,edh->enh', xf, W1) + b1[:, None, :]
        a, g = jnp.split(h, 2, axis=-1)
        act = jax.nn.silu(a) * g
        out_e = jnp.einsum('enh,ehd->end', act, W2) + b2[:, None, :]
        out_ne = out_e.transpose(1, 0, 2)
        gathered = jnp.take_along_axis(out_ne, topk_idx[:, :, None], axis=1)
        out = jnp.sum(gathered * scores[:, :, None], axis=1)
        return out.reshape(Bb, Tt, Dd)
    x = x + jnp.tanh(g_xattn[0]) * _L0_xattn_ref(_layernorm(x, axis=-1), ctx_1024, mask_BxSxS2_ff1, L0_xattn_Wq, L0_xattn_bq, L0_xattn_Wk, L0_xattn_bk, L0_xattn_Wv, L0_xattn_bv)
    x = x + jnp.tanh(g_ffn[0]) * _L0_ffn_ref(_layernorm(x, axis=-1), L0_ffn_Wg, L0_ffn_We, L0_ffn_be)
    x = x + jnp.tanh(g_xattn[1]) * _L1_xattn_ref(ctx_1024, _layernorm(x, axis=-1), mask_BxS2_bk0, L1_xattn_g1, L1_xattn_b1, L1_xattn_g2, L1_xattn_b2, L1_xattn_Wq, L1_xattn_Wkv, L1_xattn_Wout)
    x = x + jnp.tanh(g_ffn[1]) * _L1_ffn_ref(_layernorm(x, axis=-1), L1_ffn_W1, L1_ffn_b1, L1_ffn_W2, L1_ffn_b2, L1_ffn_Wr, L1_ffn_br)
    return x

_drawn_inputs = setup_inputs


def setup_inputs(seed=0):
    import zlib

    import numpy as np

    out = dict(_drawn_inputs(seed))
    spreads = {'g_ffn': (-1.0, 0.6),
     'L1_xattn_g1': (1.0, 0.2),
     'L1_xattn_b1': (0.0, 0.287),
     'L1_xattn_g2': (1.0, 0.2),
     'L1_xattn_b2': (0.0, 0.1),
     'L1_ffn_b1': (0.0, 0.8),
     'L1_ffn_b2': (0.0, 0.349),
     'L1_ffn_br': (0.0, 0.318)}
    factors = {'L0_xattn_bk': 64.0, 'L1_ffn_W1': 4.6, 'L1_ffn_W2': 4.602}
    for name, (base, spread) in spreads.items():
        noise = np.random.default_rng([zlib.crc32(name.encode()), seed]).standard_normal(out[name].shape)
        drawn = base * np.exp(spread * noise) if base else spread * noise
        out[name] = jnp.asarray(drawn.astype(out[name].dtype))
    for name, factor in factors.items():
        out[name] = (out[name] * factor).astype(out[name].dtype)
    return out
```

```python
from contextlib import ExitStack

import concourse.bass as bass
from concourse import mybir

ALU = mybir.AluOpType
ACT = mybir.ActivationFunctionType
F32 = mybir.dt.float32
F16 = mybir.dt.float16
U32 = mybir.dt.uint32
U8 = mybir.dt.uint8

B = 16
T = 112
C = 375
D = 256
KT = D // 128
E = 8
H = 16
EPS = 1e-5
HI, LO = 0, 1
PASSES = ((HI, HI), (HI, LO), (LO, HI))

D0 = D // H
KB0, NB0 = 125, 3
SCALE0 = D0 ** -0.5
GROUPS = 4

IDENT, HEADMASK, IOTA, BATCHMASK, NCONST = 0, 128, 132, 140, 156

def need(eng, sem, per, batch, count, met=None):
    need_all(eng, met, (sem, per, batch, count))

def need_all(eng, met, *conditions):
    values = [(sem, batch * per + count) for sem, per, batch, count in conditions]
    values = [(sem, v) for sem, v in values if not isinstance(v, int) or v > 0]
    if met and any(not isinstance(v, int) for _, v in values):
        values = [(sem, v if isinstance(v, int) else eng.to_reg(v)) for sem, v in values]
        eng.wait_ge(*met)
    for sem, v in values:
        eng.wait_ge(sem, v)

def run_batches(eng, body):
    body(0, 0)
    with eng.Fori(0, (B - 2) // 2) as i:
        body(i * 2 + 1, 1)
        body(i * 2 + 2, 0)
    body(B - 1, 1)

def phase_attention_small_heads(nc, x, ctxT, mask, g_xattn, g_ffn, wq, wk, wv, bq, bk, bv, wg, we, be, consts, x2_dram):
    with ExitStack() as ctx:
        sb = lambda name, shape, dt: ctx.enter_context(nc.sbuf_tensor("a_" + name, shape, dt))
        sem = lambda name: ctx.enter_context(nc.semaphore("a_" + name))
        bank = lambda name: ctx.enter_context(nc.psum_tensor("a_" + name, [128, 512], F32))

        const = sb("const", [128, NCONST], F32)
        ident = const[:, IDENT:IDENT + 128]
        neg_half = sb("neg_half", [128, 1], F32)
        wqkv_f = sb("wqkv_f", [128, KT, 512 + 512 + E], F32)
        wqkv = sb("wqkv", [128, 2, KT, 512 + 512 + E], F16)
        we_f = sb("we_f", [128, KT, E * D], F32)
        we_s = sb("we_s", [128, 2, KT, E * D], F16)
        be_f = sb("be_f", [128, D], F32)
        be_s = sb("be_s", [128, 2, D], F16)
        wq_s = wqkv[:, :, :, 0:512].rearrange("p s k (g m) -> p s k g m", g=GROUPS)
        wk_s = wqkv[:, :, :, 512:768]
        wv_s = wqkv[:, :, :, 768:1024]
        wg_s = wqkv[:, :, :, 1024:1024 + E]
        bq_c = sb("bq_c", [128, GROUPS], F32)
        bk_c = sb("bk_c", [128, KT], F32)
        bv_r = sb("bv_r", [128, D], F32)
        gates = sb("gates", [128, 4], F32)
        tanhs = sb("tanhs", [128, 4], F32)

        x_in = sb("x_in", [T, D], F32)
        ctx_f = sb("ctx_f", [128, KT, C], F32)
        ctx_s = sb("ctx_s", [128, 2, KT, C], F16)
        keep = [sb(f"keep{i}", [T, C], F32) for i in range(2)]
        bns = sb("bns", [T, 6], F32)
        mv = sb("mv", [T, 2], F32)
        var = sb("var", [T, 1], F32)
        rstd = sb("rstd", [T, 1], F32)
        xn = sb("xn", [T, D], F32)
        xT = sb("xT", [128, 2, KT, T], F16)
        q_f = sb("q_f", [128, GROUPS * T], F32)
        q_s = sb("q_s", [128, 2, GROUPS * T], F16)
        q_masked = [sb(f"q_masked{i}", [128, 2, 4, GROUPS * T], F16) for i in range(2)]
        k_s = sb("k_s", [128, 2, 2, C], F16)
        k_stack = [sb(f"k_stack{i}", [128, GROUPS, C], F16) for i in range(2)]
        v_s = [sb(f"v_s{i}", [128, NB0, H, 2, D0], F16) for i in range(2)]

        RING = 4
        prob = sb("prob", [T, RING, C], F32)
        top = sb("top", [T, RING], F32)
        sums = [sb(f"sums{i}", [T, H], F32) for i in range(2)]
        pT = sb("pT", [128, 2, 2, NB0, 128], F16)

        x_res = sb("x_res", [T, D], F32)
        o_lo = sb("o_lo", [T, H, D0], F32)
        rsum = sb("rsum", [T, H], F32)
        o_f = sb("o_f", [T, H, D0], F32)
        o_n = sb("o_n", [T, H, D0], F32)
        o_b = sb("o_b", [T, D], F32)
        x1 = sb("x1", [T, D], F32)
        bns1 = sb("bns1", [T, 6], F32)
        mv1 = sb("mv1", [T, 2], F32)
        var1 = sb("var1", [T, 1], F32)
        rstd1 = sb("rstd1", [T, 1], F32)
        xn1 = sb("xn1", [T, D], F32)
        x1T = sb("x1T", [128, 2, KT, T], F16)
        logit = sb("logit", [T, E], F32)
        best = sb("best", [T, 8], F32)
        place = sb("place", [T, 8], U32)
        place_f = sb("place_f", [T, 8], F32)
        gap = sb("gap", [T, 1], F32)
        ratio = sb("ratio", [T, 1], F32)
        norm = sb("norm", [T, 1], F32)
        share = sb("share", [T, 1], F32)
        w_top = sb("w_top", [T, 2], F32)
        picked = sb("picked", [T, 2, E], F32)
        cw = sb("cw", [T, 128], F32)
        cwT = sb("cwT", [128, 2, T], F16)
        acc = sb("acc", [T, D], F32)

        ps_s = [bank(f"ps_s{i}") for i in range(2)]
        ps_t = [bank(f"ps_t{i}") for i in range(2)]
        ps_o = bank("ps_o")
        ps_p = bank("ps_p")
        ps_d = [bank(f"ps_d{i}") for i in range(2)]

        s_setup = sem("setup")
        s_wload = sem("wload")
        s_zero = sem("zero")
        s_wsplit = sem("wsplit")
        s_wesplit = sem("wesplit")
        s_tanh = sem("tanh")
        s_xload = sem("xload")
        s_cload = sem("cload")
        s_mload = sem("mload")
        s_rload = sem("rload")
        s_keep = sem("keep")
        s_csplit = sem("csplit")
        s_stats = sem("stats")
        s_var = sem("var")
        s_rstd = sem("rstd")
        s_xn = sem("xn")
        s_item = sem("item")
        s_ihi = sem("ihi")
        s_ifree = sem("ifree")
        s_qhi = sem("qhi")
        s_qlo = sem("qlo")
        s_qmask = sem("qmask")
        s_kstack = sem("kstack")
        s_score = sem("score")
        s_max = sem("max")
        s_exp = sem("exp")
        s_tr = sem("tr")
        s_phi = sem("phi")
        s_plo = sem("plo")
        s_pv = sem("pv")
        s_olo = sem("olo")
        s_rsum = sem("rsum")
        s_oread = sem("oread")
        s_on = sem("on")
        s_ob = sem("ob")
        s_x1 = sem("x1")
        s_stats1 = sem("stats1")
        s_var1 = sem("var1")
        s_rstd1 = sem("rstd1")
        s_xn1 = sem("xn1")
        s_ditem = sem("ditem")
        s_dhi = sem("dhi")
        s_dfree = sem("dfree")
        s_route = sem("route")
        s_ratio = sem("ratio")
        s_acc = sem("acc")
        s_store = sem("store")

        PI = 7
        P_XT, P_K, P_Q, P_V = 0, 1, 3, 4
        DI = 8
        D_XT, D_GATE, D_CWT, D_PAIR, D_BIAS = 0, 1, 2, 3, 7
        ROUTE = 9
        PSLOT = {3: [P_XT], 4: [P_K], 5: [P_K + 1], 6: [P_Q], 7: [P_V], 8: [P_V + 1], 10: [P_V + 2]}
        DSLOT = {6: [D_XT], 7: [D_GATE], 10: [D_CWT, D_PAIR], 11: [D_PAIR + 1], 12: [D_PAIR + 2],
                 13: [D_PAIR + 3], 14: [D_BIAS]}

        def heads(s, lag, b, par):
            h = s - lag
            return (b, par, h) if h >= 0 else (b - 1, 1 - par, h + H)

        block = ctx.enter_context(nc.Block())

        @block.sync
        def _(sp):
            sp.dma_start(const[:, :], consts).then_inc(s_setup, 16)
            sp.dma_start(wqkv_f[:, :, 0:512], wq).then_inc(s_setup, 16)
            sp.dma_start(wqkv_f[:, :, 512:768], wk).then_inc(s_setup, 16)
            sp.dma_start(wqkv_f[:, :, 768:1024], wv).then_inc(s_setup, 16)
            sp.dma_start(wqkv_f[:, :, 1024:1024 + E], wg).then_inc(s_setup, 16)
            sp.dma_start(bq_c[:, :], bq).then_inc(s_setup, 16)
            sp.dma_start(bk_c[:, :], bk).then_inc(s_setup, 16)
            sp.dma_start(bv_r[:, :], bv.partition_broadcast(128)).then_inc(s_setup, 16)
            sp.dma_start(gates[:, 0:2], g_xattn.partition_broadcast(128)).then_inc(s_setup, 16)
            sp.dma_start(gates[:, 2:4], g_ffn.partition_broadcast(128)).then_inc(s_setup, 16)
            sp.wait_ge(s_zero, 1)
            sp.dma_start(be_f[0:E, :], be).then_inc(s_setup, 16)

            settled = (s_zero, 1)

            def load(c, par):
                need(sp, s_xn, 1, c, 0, settled)
                sp.dma_start(x_in[:, :], x[c]).then_inc(s_xload, 16)
                need(sp, s_csplit, 2, c, 0, settled)
                sp.dma_start(ctx_f[:, :, :], ctxT[c]).then_inc(s_cload, 16)
                need_all(sp, settled, (s_max, H, c - 1, 0), (s_keep, 1, c, 0))
                sp.dma_start(keep[par][:, :], mask[c]).then_inc(s_mload, 16)

            def stack_keys(c, par):
                need_all(sp, settled, (s_ihi, 6, c, 3), (s_ifree, PI, c, P_K + 2), (s_score, H, c - 1, 1))
                for a in range(2):
                    for part in (HI, LO):
                        sp.dma_start(k_stack[par][64 * part:64 * part + 64, a::2, :],
                                     k_s[64 * a:64 * a + 64, part, :, :]).then_inc(s_kstack, 16)

            def body(b, par):
                if not (isinstance(b, int) and b == B - 1):
                    load(b + 1, 1 - par)
                if not (isinstance(b, int) and b == 0):
                    need(sp, s_x1, 1, b - 1, 0, settled)
                    sp.dma_start(x_res[:, :], x[b - 1]).then_inc(s_rload, 16)
                if not (isinstance(b, int) and b == B - 1):
                    stack_keys(b + 1, 1 - par)
                if not (isinstance(b, int) and b == 0):
                    store(b - 1)

            def store(c):
                need(sp, s_dfree, DI, c, DI, settled)
                sp.dma_start(x2_dram[c], acc[:, :]).then_inc(s_store, 16)

            load(0, 0)
            sp.dma_start(we_f[:, :, :], we).then_inc(s_wload, 16)
            stack_keys(0, 0)
            run_batches(sp, body)
            need(sp, s_x1, 1, B - 1, 0, settled)
            sp.dma_start(x_res[:, :], x[B - 1]).then_inc(s_rload, 16)
            store(B - 1)
            sp.wait_ge(s_store, 16 * B)

        @block.gpsimd
        def _(pool):
            pool.memset(be_f[:, :], 0.0).then_inc(s_zero, 1)
            pool.memset(neg_half[:, :], -0.5).then_inc(s_zero, 1)
            pool.memset(cw[:, :], 0.0).then_inc(s_zero, 1)
            pool.memset(pT[:, :, :, :, :], 0.0).then_inc(s_zero, 1)
            pool.wait_ge(s_setup, 16 * 11)
            pool.tensor_copy(wqkv[:, HI, :, :], wqkv_f[:, :, :]).then_inc(s_wsplit, 1)
            pool.tensor_copy(be_s[:, HI, :], be_f[:, :]).then_inc(s_wsplit, 1)
            pool.wait_ge(s_wsplit, 2)
            pool.tensor_tensor(wqkv[:, LO, :, :], wqkv_f[:, :, :], wqkv[:, HI, :, :], ALU.subtract).then_inc(s_wsplit, 1)
            pool.tensor_tensor(be_s[:, LO, :], be_f[:, :], be_s[:, HI, :], ALU.subtract).then_inc(s_wsplit, 1)

            settled = (s_zero, 4)

            def split_context(c):
                need(pool, s_cload, 16, c, 16)
                need(pool, s_item, PI, c, 0, settled)
                pool.tensor_copy(ctx_s[:, HI, :, :], ctx_f[:, :, :]).then_inc(s_csplit, 1)
                need(pool, s_csplit, 2, c, 1)
                pool.tensor_tensor(ctx_s[:, LO, :, :], ctx_f[:, :, :], ctx_s[:, HI, :, :], ALU.subtract).then_inc(s_csplit, 1)

            def deviation(c, s_in, s_mid, s_out, stat, mid, out):
                need(pool, s_in, 2, c, 2, settled)
                pool.tensor_scalar(mid[:, :], stat[:, 1:2], 1.0, EPS, ALU.mult, ALU.add).then_inc(s_mid, 1)
                need(pool, s_mid, 1, c, 1)
                pool.tensor_tensor(out[:, :], mid[:, :], neg_half[0:T, :], ALU.pow).then_inc(s_out, 1)

            def mask_bias(c, par):
                need(pool, s_mload, 16, c, 16, settled)
                pool.tensor_scalar(keep[par][:, :], keep[par][:, :], -1.0, 10000.0 / SCALE0, ALU.add, ALU.mult).then_inc(s_keep, 1)

            def queries(c, par):
                need(pool, s_ifree, PI, c, P_Q + 1, settled)
                pool.tensor_copy(q_s[:, HI, :], q_f[:, :]).then_inc(s_qhi, 1)
                need(pool, s_qhi, 1, c, 1)
                pool.tensor_tensor(q_s[:, LO, :], q_f[:, :], q_s[:, HI, :], ALU.subtract).then_inc(s_qlo, 1)
                need(pool, s_qlo, 1, c, 1)
                need(pool, s_score, H, c - 1, 0)
                for part in (HI, LO):
                    pool.tensor_tensor(q_masked[par][:, part, :, :],
                                       q_s[:, part, :].unsqueeze(1).to_broadcast([128, 4, GROUPS * T]),
                                       const[:, HEADMASK:HEADMASK + 4].unsqueeze(2).to_broadcast([128, 4, GROUPS * T]),
                                       ALU.mult).then_inc(s_qmask, 1)

            def project(c, par):
                deviation(c, s_stats, s_var, s_rstd, mv, var, rstd)
                split_context(c)
                mask_bias(c, par)
                queries(c, par)

            def body(b, par):
                if not (isinstance(b, int) and b == B - 1):
                    deviation(b + 1, s_stats, s_var, s_rstd, mv, var, rstd)
                    split_context(b + 1)
                    mask_bias(b + 1, 1 - par)
                if not (isinstance(b, int) and b == 0):
                    deviation(b - 1, s_stats1, s_var1, s_rstd1, mv1, var1, rstd1)
                if not (isinstance(b, int) and b == B - 1):
                    queries(b + 1, 1 - par)

            project(0, 0)
            pool.wait_ge(s_wload, 16)
            pool.tensor_copy(we_s[:, HI, :, :], we_f[:, :, :]).then_inc(s_wesplit, 1)
            pool.wait_ge(s_wesplit, 1)
            pool.tensor_tensor(we_s[:, LO, :, :], we_f[:, :, :], we_s[:, HI, :, :], ALU.subtract).then_inc(s_wesplit, 1)
            run_batches(pool, body)
            deviation(B - 1, s_stats1, s_var1, s_rstd1, mv1, var1, rstd1)

        @block.tensor
        def _(pe):
            def product(out, sta, mov):
                for k in range(KT):
                    for n, (a, m) in enumerate(PASSES):
                        last = pe.matmul(out, sta(a, k), mov(m, k), start=(k == 0 and n == 0),
                                         stop=(k == KT - 1 and n == 2))
                return last

            def item(c, par, k):
                need(pe, s_ifree, PI, c, k)
                if k == P_XT:
                    need(pe, s_xn, 1, c, 1)
                    for t in range(KT):
                        last = pe.transpose(ps_p[:, t * T:(t + 1) * T], xn[:, t * 128:(t + 1) * 128], ident[0:T, 0:T])
                elif P_K <= k < P_Q:
                    j = k - P_K
                    need(pe, s_csplit, 2, c, 2)
                    last = product(ps_p[:, 0:C], lambda a, t: wk_s[:, a, t, j * 128:(j + 1) * 128],
                                   lambda a, t: ctx_s[:, a, t, :])
                elif k == P_Q:
                    need(pe, s_ihi, 6, c, 1)
                    need(pe, s_ifree, PI, c, P_XT + 1)
                    for g in range(GROUPS):
                        last = product(ps_p[:, g * T:(g + 1) * T], lambda a, t: wq_s[:, a, t, g, :],
                                       lambda a, t: xT[:, a, t, :])
                else:
                    j = k - P_V
                    last = product(ps_p[0:KB0, 0:D], lambda a, t: ctx_s[:, a, t, j * KB0:(j + 1) * KB0],
                                   lambda a, t: wv_s[:, a, t, :])
                last.then_inc(s_item, 1)

            def ditem(c, k):
                ps = ps_d[k % 2]
                need(pe, s_dfree, DI, c, max(k - 1, 0))
                if k == D_XT:
                    need(pe, s_xn1, 1, c, 1)
                    for t in range(KT):
                        last = pe.transpose(ps[:, t * T:(t + 1) * T], xn1[:, t * 128:(t + 1) * 128], ident[0:T, 0:T])
                elif k == D_GATE:
                    need(pe, s_dhi, 2, c, 1)
                    need(pe, s_dfree, DI, c, D_XT + 1)
                    last = product(ps[0:T, 0:E], lambda a, t: x1T[:, a, t, :], lambda a, t: wg_s[:, a, t, :])
                elif k == D_CWT:
                    need(pe, s_route, ROUTE, c, ROUTE)
                    last = pe.transpose(ps[:, 0:T], cw[:, :], ident[0:T, 0:T])
                elif k == D_BIAS:
                    need(pe, s_dhi, 2, c, 2)
                    need(pe, s_dfree, DI, c, D_CWT + 1)
                    for n, (a, m) in enumerate(PASSES):
                        last = pe.matmul(ps[0:T, 0:D], cwT[:, a, :], be_s[:, m, :], start=(n == 0), stop=(n == 2))
                else:
                    j = k - D_PAIR
                    last = product(ps[0:T, :], lambda a, t: x1T[:, a, t, :],
                                   lambda a, t: we_s[:, a, t, j * 512:(j + 1) * 512])
                last.then_inc(s_ditem, 1)

            def scores(b, par, h):
                g, m = h // 4, h % 4
                if h == 0:
                    need(pe, s_qmask, 2, b, 2)
                    need(pe, s_kstack, 64, b, 64)
                need(pe, s_max, H, b, h - 1)
                for part in (HI, LO):
                    last = pe.matmul(ps_s[h % 2][0:T, 0:C], q_masked[par][:, part, m, g * T:(g + 1) * T],
                                     k_stack[par][:, g, :], start=(part == HI), stop=(part == LO))
                last.then_inc(s_score, 1)

            def transposes(b, h):
                need(pe, s_exp, H, b, h + 1)
                need(pe, s_plo, H, b, h - 1)
                for j in range(NB0):
                    last = pe.transpose(ps_t[h % 2][0:KB0, j * T:(j + 1) * T],
                                        prob[:, h % RING, j * KB0:(j + 1) * KB0], ident[0:T, 0:T])
                last.then_inc(s_tr, 1)

            def values(b, par, h):
                need(pe, s_phi, H, b, h + 1)
                need(pe, s_plo, H, b, h + 1)
                if h == 0:
                    need(pe, s_oread, 1, b, 0)
                    need(pe, s_ihi, 6, b, 6)
                    need(pe, s_ifree, PI, b, PI)
                for j in range(NB0):
                    for part in (HI, LO):
                        last = pe.matmul(ps_o[:, 32 * h:32 * h + 32], pT[0:KB0, h % 2, part, j, :],
                                         v_s[par][0:KB0, j, h, :, :], start=(h == 0 and j == 0 and part == HI),
                                         stop=(j == NB0 - 1 and part == LO), skip_group_check=True)
                last.then_inc(s_pv, 1)

            def drain(b, par):
                for s in range(3):
                    for lag, stage in ((2, transposes), (3, values)):
                        h = H + s - lag
                        if h < H:
                            stage(b, h) if lag == 2 else stage(b, par, h)

            def body(b, par):
                for s in range(H):
                    scores(b, par, s)
                    if not (isinstance(b, int) and b == 0 and s < 2):
                        c, _, h = heads(s, 2, b, par)
                        transposes(c, h)
                    if not (isinstance(b, int) and b == 0 and s < 3):
                        values(*heads(s, 3, b, par))
                    if not (isinstance(b, int) and b == B - 1):
                        for k in PSLOT.get(s, []):
                            item(b + 1, 1 - par, k)
                    if not (isinstance(b, int) and b == 0):
                        for k in DSLOT.get(s, []):
                            ditem(b - 1, k)

            pe.wait_ge(s_setup, 16 * 11)
            pe.wait_ge(s_zero, 4)
            pe.wait_ge(s_wsplit, 4)
            for k in range(PI):
                item(0, 0, k)
            pe.wait_ge(s_wesplit, 2)
            run_batches(pe, body)
            drain(B - 1, 1)
            for k in range(DI):
                ditem(B - 1, k)

        @block.scalar
        def _(act):
            def item(c, par, k):
                if k == P_Q:
                    return
                need(act, s_item, PI, c, k + 1)
                if k == P_XT:
                    act.activation(xT[:, HI, :, :], ps_p[:, 0:KT * T].rearrange("p (t n) -> p t n", t=KT), ACT.Copy).then_inc(s_ihi, 1)
                elif k < P_Q:
                    j = k - P_K
                    if j == 0:
                        need(act, s_kstack, 64, c, 0)
                    act.activation(k_s[:, HI, j, :], ps_p[:, 0:C], ACT.Identity, bias=bk_c[:, j:j + 1]).then_inc(s_ihi, 1)
                else:
                    j = k - P_V
                    need(act, s_pv, H, c - 1, 0)
                    act.activation(v_s[par][0:KB0, j, :, HI, :],
                                   ps_p[0:KB0, 0:D].rearrange("p (h d) -> p h d", h=H), ACT.Copy).then_inc(s_ihi, 1)

            def ditem(c, k):
                if k == D_XT:
                    need(act, s_ditem, DI, c, 1)
                    act.activation(x1T[:, HI, :, :], ps_d[0][:, 0:KT * T].rearrange("p (t n) -> p t n", t=KT), ACT.Copy).then_inc(s_dhi, 1)
                elif k == D_CWT:
                    need(act, s_ditem, DI, c, D_CWT + 1)
                    act.activation(cwT[:, HI, :], ps_d[D_CWT % 2][:, 0:T], ACT.Copy).then_inc(s_dhi, 1)

            def exps(b, par, h):
                need(act, s_max, H, b, h + 1)
                act.activation(prob[:, h % RING, :], prob[:, h % RING, :], ACT.Exp, bias=top[:, h % RING:h % RING + 1],
                               scale=-1.0, accum_out=sums[par][:, h:h + 1]).then_inc(s_exp, 1)

            def phi(b, h):
                need(act, s_tr, H, b, h + 1)
                need(act, s_pv, H, b, h - 1)
                act.activation(pT[0:KB0, h % 2, HI, :, 0:T],
                               ps_t[h % 2][0:KB0, 0:NB0 * T].rearrange("p (j n) -> p j n", j=NB0), ACT.Copy).then_inc(s_phi, 1)

            def out_lo(c):
                need(act, s_pv, H, c, H)
                act.activation(o_lo[:, :, :], ps_o[0:T, :].rearrange("p (h s d) -> p h s d", h=H, s=2)[:, :, LO, :], ACT.Copy).then_inc(s_olo, 1)

            def weigh(c):
                need(act, s_route, ROUTE, c, 4)
                act.activation(ratio[:, :], gap[:, :], ACT.Exp).then_inc(s_ratio, 1)

            def body(b, par):
                for s in range(H):
                    if not (isinstance(b, int) and b == B - 1):
                        for k in PSLOT.get(s - 1, []):
                            item(b + 1, 1 - par, k)
                    if not (isinstance(b, int) and b == 0):
                        if s == 3:
                            out_lo(b - 1)
                        if s == 9:
                            weigh(b - 1)
                        for k in DSLOT.get(s - 1, []):
                            ditem(b - 1, k)
                    if not (isinstance(b, int) and b == 0 and s < 1):
                        exps(*heads(s, 1, b, par))
                    if not (isinstance(b, int) and b == 0 and s < 2):
                        c, _, h = heads(s, 2, b, par)
                        phi(c, h)

            act.wait_ge(s_setup, 16 * 11)
            act.activation(tanhs[:, :], gates[:, :], ACT.Tanh).then_inc(s_tanh, 1)
            for k in range(PI):
                item(0, 0, k)
            run_batches(act, body)
            exps(B - 1, 1, H - 1)
            phi(B - 1, H - 2)
            phi(B - 1, H - 1)
            out_lo(B - 1)
            ditem(B - 1, D_XT)
            weigh(B - 1)
            ditem(B - 1, D_CWT)

        @block.vector
        def _(dve):
            settled = (s_zero, 4)

            def stats_x(c):
                need(dve, s_xload, 16, c, 16)
                dve.bn_stats(bns[:, :], x_in[:, :]).then_inc(s_stats, 1)
                need(dve, s_stats, 2, c, 1, settled)
                dve.bn_aggr(mv[:, :], bns[:, :]).then_inc(s_stats, 1)

            def norm_x(c):
                need(dve, s_rstd, 1, c, 1)
                need(dve, s_item, PI, c - 1, 1)
                dve.tensor_scalar(xn[:, :], x_in[:, :], mv[:, 0:1], rstd[:, 0:1], ALU.subtract, ALU.mult).then_inc(s_xn, 1)

            def item(c, par, k):
                if k == P_Q:
                    need(dve, s_item, PI, c, k + 1)
                    need(dve, s_qlo, 1, c, 0)
                    dve.tensor_tensor(q_f[:, :].rearrange("p (g n) -> p g n", g=GROUPS),
                                      ps_p[:, 0:GROUPS * T].rearrange("p (g n) -> p g n", g=GROUPS),
                                      bq_c[:, :].unsqueeze(2).to_broadcast([128, GROUPS, T]), ALU.add).then_inc(s_ifree, 1)
                    return
                need(dve, s_ihi, 6, c, k + 1 if k < P_Q else k)
                if k == P_XT:
                    dve.tensor_tensor(xT[:, LO, :, :], ps_p[:, 0:KT * T].rearrange("p (t n) -> p t n", t=KT), xT[:, HI, :, :], ALU.subtract).then_inc(s_ifree, 1)
                elif k < P_Q:
                    j = k - P_K
                    dve.scalar_tensor_tensor(k_s[:, LO, j, :], ps_p[:, 0:C], bk_c[:, j:j + 1], k_s[:, HI, j, :],
                                             ALU.add, ALU.subtract).then_inc(s_ifree, 1)
                else:
                    j = k - P_V
                    dve.tensor_tensor(v_s[par][0:KB0, j, :, LO, :],
                                      ps_p[0:KB0, 0:D].rearrange("p (h d) -> p h d", h=H),
                                      v_s[par][0:KB0, j, :, HI, :], ALU.subtract).then_inc(s_ifree, 1)

            def maxima(b, par, h):
                need_all(dve, settled, (s_score, H, b, h + 1), (s_tr, H, b, h - RING + 1), *([(s_keep, 1, b, 1)] if h == 0 else []))
                dve.tensor_tensor_reduce(prob[:, h % RING, :], ps_s[h % 2][0:T, 0:C], keep[par][:, :], -SCALE0, 3e38,
                                         ALU.add, ALU.min, top[:, h % RING:h % RING + 1]).then_inc(s_max, 1)

            def plo(b, h):
                need(dve, s_phi, H, b, h + 1)
                dve.tensor_tensor(pT[0:KB0, h % 2, LO, :, 0:T],
                                  ps_t[h % 2][0:KB0, 0:NB0 * T].rearrange("p (j n) -> p j n", j=NB0),
                                  pT[0:KB0, h % 2, HI, :, 0:T], ALU.subtract).then_inc(s_plo, 1)

            def out_x1(c, par):
                need(dve, s_exp, H, c, H)
                dve.reciprocal(rsum[:, :], sums[par][:, :]).then_inc(s_rsum, 1)
                need(dve, s_olo, 1, c, 1)
                dve.tensor_tensor(o_f[:, :, :], ps_o[0:T, :].rearrange("p (h s d) -> p h s d", h=H, s=2)[:, :, HI, :],
                                  o_lo[:, :, :], ALU.add).then_inc(s_oread, 1)
                need(dve, s_oread, 1, c, 1)
                dve.tensor_tensor(o_n[:, :, :], o_f[:, :, :], rsum[:, :].unsqueeze(2).to_broadcast([T, H, D0]), ALU.mult).then_inc(s_on, 1)
                need(dve, s_on, 1, c, 1)
                dve.tensor_tensor(o_b[:, :], o_n[:, :, :].rearrange("p h d -> p (h d)"), bv_r[0:T, :], ALU.add).then_inc(s_ob, 1)
                need(dve, s_ob, 1, c, 1)
                need(dve, s_rload, 16, c, 16)
                dve.scalar_tensor_tensor(x1[:, :], o_b[:, :], tanhs[0:T, 0:1], x_res[:, :], ALU.mult, ALU.add).then_inc(s_x1, 1)
                need(dve, s_x1, 1, c, 1)
                dve.bn_stats(bns1[:, :], x1[:, :]).then_inc(s_stats1, 1)
                need(dve, s_stats1, 2, c, 1, settled)
                dve.bn_aggr(mv1[:, :], bns1[:, :]).then_inc(s_stats1, 1)

            def norm_x1(c):
                need(dve, s_rstd1, 1, c, 1)
                dve.tensor_scalar(xn1[:, :], x1[:, :], mv1[:, 0:1], rstd1[:, 0:1], ALU.subtract, ALU.mult).then_inc(s_xn1, 1)

            def ditem(c, k):
                ps = ps_d[k % 2]
                if k == D_XT:
                    need(dve, s_dhi, 2, c, 1)
                    dve.tensor_tensor(x1T[:, LO, :, :], ps[:, 0:KT * T].rearrange("p (t n) -> p t n", t=KT), x1T[:, HI, :, :], ALU.subtract).then_inc(s_dfree, 1)
                elif k == D_GATE:
                    need(dve, s_ditem, DI, c, k + 1)
                    dve.tensor_copy(logit[:, :], ps[0:T, 0:E]).then_inc(s_dfree, 1)
                    need(dve, s_dfree, DI, c, k + 1, settled)
                    dve.max(best[:, :], logit[:, :]).then_inc(s_route, 1)
                    need(dve, s_route, ROUTE, c, 1, settled)
                    dve.max_index(place[:, :], best[:, :], logit[:, :]).then_inc(s_route, 1)
                    need(dve, s_route, ROUTE, c, 2)
                    dve.tensor_copy(place_f[:, :], place[:, :]).then_inc(s_route, 1)
                    dve.tensor_tensor(gap[:, :], best[:, 1:2], best[:, 0:1], ALU.subtract).then_inc(s_route, 1)
                elif k == D_CWT:
                    need(dve, s_dhi, 2, c, 2)
                    dve.tensor_tensor(cwT[:, LO, :], ps[:, 0:T], cwT[:, HI, :], ALU.subtract).then_inc(s_dfree, 1)
                elif k == D_BIAS:
                    need(dve, s_ditem, DI, c, k + 1)
                    need(dve, s_dfree, DI, c, k)
                    dve.tensor_tensor(acc[:, :], ps[0:T, 0:D], acc[:, :], ALU.add).then_inc(s_dfree, 1)
                else:
                    j = k - D_PAIR
                    need(dve, s_ditem, DI, c, k + 1)
                    if j == 0:
                        need(dve, s_route, ROUTE, c, ROUTE)
                        need(dve, s_store, 16, c, 0)
                    need(dve, s_dfree, DI, c, k)
                    dve.scalar_tensor_tensor(acc[:, :], ps[0:T, 0:D], cw[:, 2 * j:2 * j + 1], (acc if j else x1)[:, :],
                                             ALU.mult, ALU.add).then_inc(s_acc, 1)
                    need(dve, s_acc, E // 2, c, j + 1)
                    dve.scalar_tensor_tensor(acc[:, :], ps[0:T, D:2 * D], cw[:, 2 * j + 1:2 * j + 2], acc[:, :],
                                             ALU.mult, ALU.add).then_inc(s_dfree, 1)

            def combine_weights(c):
                need(dve, s_ratio, 1, c, 1)
                dve.tensor_scalar(norm[:, :], ratio[:, :], 1.0, None, ALU.add).then_inc(s_route, 1)
                need(dve, s_route, ROUTE, c, 5)
                dve.reciprocal(share[:, :], norm[:, :]).then_inc(s_route, 1)
                need(dve, s_route, ROUTE, c, 6)
                dve.tensor_scalar(w_top[:, 0:1], share[:, :], tanhs[0:T, 2:3], None, ALU.mult)
                dve.tensor_scalar(w_top[:, 1:2], share[:, :], tanhs[0:T, 2:3], ratio[:, 0:1], ALU.mult, ALU.mult).then_inc(s_route, 1)
                need(dve, s_route, ROUTE, c, 7)
                for n in range(2):
                    last = dve.tensor_scalar(picked[:, n, :], const[0:T, IOTA:IOTA + E], place_f[:, n:n + 1], w_top[:, n:n + 1],
                                             ALU.is_equal, ALU.mult)
                last.then_inc(s_route, 1)
                need(dve, s_route, ROUTE, c, 8)
                dve.tensor_tensor(cw[:, 0:E], picked[:, 0, :], picked[:, 1, :], ALU.add).then_inc(s_route, 1)

            def body(b, par):
                for s in range(H):
                    if not (isinstance(b, int) and b == B - 1):
                        if s == 2:
                            stats_x(b + 1)
                        if s == 3:
                            norm_x(b + 1)
                        for k in PSLOT.get(s - 1, []):
                            item(b + 1, 1 - par, k)
                    if not (isinstance(b, int) and b == 0):
                        if s == 3:
                            out_x1(b - 1, 1 - par)
                        if s == 5:
                            norm_x1(b - 1)
                        if s == 10:
                            combine_weights(b - 1)
                        for k in DSLOT.get(s - 1, []):
                            ditem(b - 1, k)
                    maxima(b, par, s)
                    if not (isinstance(b, int) and b == 0 and s < 2):
                        c, _, h = heads(s, 2, b, par)
                        plo(c, h)

            dve.wait_ge(s_setup, 16 * 11)
            dve.wait_ge(s_zero, 4)
            dve.wait_ge(s_tanh, 1)
            stats_x(0)
            norm_x(0)
            for k in range(PI):
                item(0, 0, k)
            run_batches(dve, body)
            plo(B - 1, H - 2)
            plo(B - 1, H - 1)
            out_x1(B - 1, 1)
            norm_x1(B - 1)
            ditem(B - 1, D_XT)
            ditem(B - 1, D_GATE)
            combine_weights(B - 1)
            for k in range(D_CWT, DI):
                ditem(B - 1, k)

D1 = 64
INNER = H * D1
IT = INNER // 128
NK = C + T
NKP = 488
KB1, NB1 = 122, 4
SCALE1 = D1 ** -0.5
MASKED = 1e30

def phase_attention_large_heads(nc, ctx_tok, mask, g_xattn, g_ffn, g1, b1, g2, b2, wq, wkv, wout, wr, br, consts,
                                x2_dram, x3_dram, x3T_dram, cw_dram):
    with ExitStack() as ctx:
        sb = lambda name, shape, dt: ctx.enter_context(nc.sbuf_tensor("b_" + name, shape, dt))
        sem = lambda name: ctx.enter_context(nc.semaphore("b_" + name))
        bank = lambda name: ctx.enter_context(nc.psum_tensor("b_" + name, [128, 512], F32))

        const = sb("const", [128, NCONST], F32)
        ident = const[:, IDENT:IDENT + 128]
        neg_half = sb("neg_half", [128, 4], F32)
        stage = sb("stage", [128, KT * 2 * INNER], F32)
        wkv_s = sb("wkv_s", [128, 2, KT, 2 * INNER], F16)
        wq_s = sb("wq_s", [128, 2, KT, INNER], F16)
        wout_s = sb("wout_s", [128, 2, IT, D], F16)
        wr_f = sb("wr_f", [128, KT, E], F32)
        wr_s = sb("wr_s", [128, 2, KT, E], F16)
        br_r = sb("br_r", [128, E], F32)
        affine = sb("affine", [128, 4, KT], F32)
        gates = sb("gates", [128, 4], F32)
        tanhs = sb("tanhs", [128, 4], F32)

        ctx_t = sb("ctx_t", [KB0, NB0, D], F32)
        x2_t = sb("x2_t", [T, D], F32)
        bns = sb("bns", [128, 4, 6], F32)
        mv = sb("mv", [128, 4, 2], F32)
        var = sb("var", [128, 4], F32)
        rstd = sb("rstd", [128, 4], F32)
        ctx_n = sb("ctx_n", [KB0, NB0, D], F32)
        x2_n = sb("x2_n", [T, D], F32)
        tok_f = sb("tok_f", [128, KT, NK], F32)
        tok_s = [sb(f"tok_s{i}", [128, 2, KT, NKP], F16) for i in range(2)]
        keep_u = sb("keep_u", [T, C], U8)
        keep = [sb(f"keep{i}", [T, NK], F32) for i in range(2)]

        q_s = sb("q_s", [128, 2, IT, T], F16)
        q_dup = [sb(f"q_dup{i}", [128, 2, H, T], F16) for i in range(2)]
        k_s = sb("k_s", [128, 2, IT, NK], F16)
        k_stack = [sb(f"k_stack{i}", [128, H, NK], F16) for i in range(2)]
        v_s = [sb(f"v_s{i}", [128, 2, NB1, INNER], F16) for i in range(2)]

        RING = 4
        prob = sb("prob", [T, RING, NKP], F32)
        top = sb("top", [T, RING], F32)
        sums = [sb(f"sums{i}", [T, H], F32) for i in range(2)]
        pT = sb("pT", [128, 2, 2, NB1, 128], F16)

        x_res = sb("x_res", [T, D], F32)
        rsum = sb("rsum", [T, H], F32)
        o_n = sb("o_n", [T, H, D1], F32)
        oT = sb("oT", [128, 2, IT, T], F16)
        x3 = sb("x3", [T, D], F32)
        bns3 = sb("bns3", [T, 6], F32)
        mv3 = sb("mv3", [T, 2], F32)
        var3 = sb("var3", [T, 1], F32)
        rstd3 = sb("rstd3", [T, 1], F32)
        xn3 = sb("xn3", [T, D], F32)
        x3T = sb("x3T", [128, 2, KT, T], F16)
        logit = sb("logit", [T, E], F32)
        best = sb("best", [T, 8], F32)
        place = sb("place", [T, 8], U32)
        place_f = sb("place_f", [T, 8], F32)
        gap = sb("gap", [T, 1], F32)
        ratio = sb("ratio", [T, 1], F32)
        norm = sb("norm", [T, 1], F32)
        share = sb("share", [T, 1], F32)
        w_top = sb("w_top", [T, 2], F32)
        picked = sb("picked", [T, 2, E], F32)
        cw = sb("cw", [T, E], F32)

        ps_s = [bank(f"ps_s{i}") for i in range(2)]
        ps_t = [bank(f"ps_t{i}") for i in range(2)]
        ps_o = [bank(f"ps_o{i}") for i in range(2)]
        ps_p = [bank(f"ps_p{i}") for i in range(2)]
        ps_x = ps_o[1]

        s_setup = sem("setup")
        s_wkv = sem("wkv")
        s_wq = sem("wq")
        s_wout = sem("wout")
        s_zero = sem("zero")
        s_wsplit = sem("wsplit")
        s_tanh = sem("tanh")
        s_cload = sem("cload")
        s_xload = sem("xload")
        s_mload = sem("mload")
        s_rload = sem("rload")
        s_keep = sem("keep")
        s_stats = sem("stats")
        s_var = sem("var")
        s_rstd = sem("rstd")
        s_norm = sem("norm")
        s_nitem = sem("nitem")
        s_nfree = sem("nfree")
        s_tsplit = sem("tsplit")
        s_item = sem("item")
        s_ihi = sem("ihi")
        s_ifree = sem("ifree")
        s_kstack = sem("kstack")
        s_qdup = sem("qdup")
        s_score = sem("score")
        s_max = sem("max")
        s_exp = sem("exp")
        s_tr = sem("tr")
        s_phi = sem("phi")
        s_plo = sem("plo")
        s_pv = sem("pv")
        s_rsum = sem("rsum")
        s_oread = sem("oread")
        s_hitem = sem("hitem")
        s_hhi = sem("hhi")
        s_hfree = sem("hfree")
        s_stats3 = sem("stats3")
        s_var3 = sem("var3")
        s_rstd3 = sem("rstd3")
        s_xn3 = sem("xn3")
        s_route = sem("route")
        s_ratio = sem("ratio")
        s_store = sem("store")

        NSETUP = 16 * 11
        P_K, P_Q, P_V, PI = 0, IT, IT + 2, IT + 2 + 2 * NB1
        N_C, N_L, NI = 0, KT, KT + 1
        H_T, H_O, H_X, H_G, HI_ = 0, 2, 3, 4, 5
        ROUTE = 9
        PSLOT, k = {}, 0
        for s, n in enumerate([2, 2, 2, 2, 1, 1, 0, 1, 1, 1, 1, 1, 1, 1, 1]):
            PSLOT[s] = list(range(k, k + n))
            k += n
        assert k == PI
        XSLOT = {3: ("n", 0), 4: ("h", 0), 5: ("h", 1), 6: ("h", 2), 7: ("n", 1), 8: ("h", 3), 9: ("h", 4), 10: ("n", 2)}

        def first(b):
            return isinstance(b, int) and b == 0

        def ahead(b, n):
            return not (isinstance(b, int) and b + n > B - 1)

        def lent_before(s):
            n = [XSLOT[t][0] for t in XSLOT if t < s]
            return n.count("h"), n.count("n")

        def behind(s, lag, b, par):
            h = s - lag
            return (b, par, h) if h >= 0 else (b - 1, 1 - par, h + H)

        def run_bodies(eng, body):
            body(0, 0)
            with eng.Fori(0, (B - 4) // 2) as i:
                body(i * 2 + 1, 1)
                body(i * 2 + 2, 0)
            for b in range(B - 3, B):
                body(b, b % 2)

        block = ctx.enter_context(nc.Block())

        @block.sync
        def _(sp):
            sp.dma_start(const[:, :], consts).then_inc(s_setup, 16)
            for n, v in enumerate((g1, b1, g2, b2)):
                sp.dma_start(affine[:, n, :], v).then_inc(s_setup, 16)
            sp.dma_start(wr_f[:, :, :], wr).then_inc(s_setup, 16)
            sp.dma_start(br_r[:, :], br.partition_broadcast(128)).then_inc(s_setup, 16)
            sp.dma_start(gates[:, 0:2], g_xattn.partition_broadcast(128)).then_inc(s_setup, 16)
            sp.dma_start(gates[:, 2:4], g_ffn.partition_broadcast(128)).then_inc(s_setup, 16)

            settled = (s_zero, 8)

            def load(c):
                need(sp, s_norm, 2, c, 0, settled)
                sp.dma_start(ctx_t[:, :, :], ctx_tok[c].rearrange("(j p) d -> p j d", p=KB0)).then_inc(s_cload, 16)
                sp.dma_start(x2_t[:, :], x2_dram[c]).then_inc(s_xload, 16)
                need(sp, s_keep, 1, c, 0, settled)
                sp.dma_start(keep_u[:, :], mask[c].partition_broadcast(T)).then_inc(s_mload, 16)

            def stack(c, par):
                need_all(sp, settled, (s_ihi, PI, c, P_Q), (s_ifree, PI, c, P_Q), (s_score, H, c - 1, 1))
                for a in range(2):
                    for part in (HI, LO):
                        src = k_s[64 * a:64 * a + 64, part, :, :]
                        rows = part if a == 0 else 1 - part
                        sp.dma_start(k_stack[par][64 * rows:64 * rows + 64, a::2, :], src).then_inc(s_kstack, 16)
                need_all(sp, settled, (s_ihi, PI, c, P_V), (s_ifree, PI, c, P_V))
                for a in range(2):
                    for rows in range(2):
                        for part in (HI, LO):
                            sp.dma_start(q_dup[par][64 * rows:64 * rows + 64, part, a::2, :],
                                         q_s[64 * a:64 * a + 64, part, :, :]).then_inc(s_qdup, 16)

            def residual(c):
                need(sp, s_hfree, HI_, c, 0, settled)
                sp.dma_start(x_res[:, :], x2_dram[c]).then_inc(s_rload, 16)

            def store(c):
                need(sp, s_hfree, HI_, c, H_X + 1, settled)
                sp.dma_start(x3_dram[c], x3[:, :]).then_inc(s_store, 16)
                sp.dma_start(x3T_dram[c], x3T[:, :, :, :]).then_inc(s_store, 16)
                need(sp, s_route, ROUTE, c, ROUTE, settled)
                sp.dma_start(cw_dram[c], cw[:, :]).then_inc(s_store, 16)

            def body(b, par):
                if not first(b):
                    residual(b - 1)
                if ahead(b, 2):
                    load(b + 2)
                if ahead(b, 1):
                    stack(b + 1, 1 - par)
                if not first(b):
                    store(b - 1)

            load(0)
            sp.dma_start(stage[:, :].rearrange("p (k n) -> p k n", k=KT), wkv).then_inc(s_wkv, 16)
            load(1)
            sp.wait_ge(s_wsplit, 4)
            sp.dma_start(stage[:, 0:KT * INNER].rearrange("p (k n) -> p k n", k=KT), wq).then_inc(s_wq, 16)
            sp.dma_start(stage[:, KT * INNER:KT * INNER + IT * D].rearrange("p (k n) -> p k n", k=IT), wout).then_inc(s_wout, 16)
            stack(0, 0)
            run_bodies(sp, body)
            residual(B - 1)
            store(B - 1)
            sp.wait_ge(s_store, 3 * 16 * B)

        @block.gpsimd
        def _(pool):
            pool.memset(neg_half[:, :], -0.5).then_inc(s_zero, 1)
            pool.memset(pT[:, :, :, :, :], 0.0).then_inc(s_zero, 1)
            pool.memset(prob[:, :, :], 0.0).then_inc(s_zero, 1)
            for i in range(2):
                pool.memset(tok_s[i][:, :, :, :], 0.0).then_inc(s_zero, 1)
                pool.memset(keep[i][:, :], 0.0).then_inc(s_zero, 1)
            pool.memset(mv[:, :, :], 0.0).then_inc(s_zero, 1)

            settled = (s_zero, 8)

            def deviation(c):
                need(pool, s_stats, 8, c, 8, settled)
                pool.tensor_scalar(var[:, 0:NB0], mv[:, 0:NB0, 1], 1.0, EPS, ALU.mult, ALU.add).then_inc(s_var, 1)
                pool.tensor_scalar(var[:, NB0:NB0 + 1], mv[:, NB0:NB0 + 1, 1], 1.0 + EPS, EPS * EPS, ALU.mult, ALU.add).then_inc(s_var, 1)
                need(pool, s_var, 2, c, 2)
                pool.tensor_tensor(rstd[:, :], var[:, :], neg_half[:, :], ALU.pow).then_inc(s_rstd, 1)

            def deviation3(c):
                need(pool, s_stats3, 2, c, 2, settled)
                pool.tensor_scalar(var3[:, :], mv3[:, 1:2], 1.0, EPS, ALU.mult, ALU.add).then_inc(s_var3, 1)
                need(pool, s_var3, 1, c, 1)
                pool.tensor_tensor(rstd3[:, :], var3[:, :], neg_half[0:T, 0:1], ALU.pow).then_inc(s_rstd3, 1)

            def mask_bias(c, par):
                need_all(pool, settled, (s_mload, 16, c, 16), (s_max, H, c - 1, 0))
                pool.tensor_scalar(keep[par][:, 0:C], keep_u[:, :], -1.0, MASKED, ALU.add, ALU.mult).then_inc(s_keep, 1)

            def split_tokens(c, par):
                for k in range(KT):
                    need_all(pool, settled, (s_nfree, NI, c, k + 1), *([(s_item, PI, c - 1, 0)] if k == 0 else []))
                    pool.tensor_copy(tok_s[par][:, HI, k, 0:C], tok_f[:, k, 0:C]).then_inc(s_tsplit, 1)
                    need(pool, s_tsplit, 6, c, 2 * k + 1)
                    pool.tensor_tensor(tok_s[par][:, LO, k, 0:C], tok_f[:, k, 0:C], tok_s[par][:, HI, k, 0:C], ALU.subtract).then_inc(s_tsplit, 1)
                need(pool, s_nfree, NI, c, NI, settled)
                pool.tensor_copy(tok_s[par][:, HI, :, C:NK], tok_f[:, :, C:NK]).then_inc(s_tsplit, 1)
                need(pool, s_tsplit, 6, c, 5)
                pool.tensor_tensor(tok_s[par][:, LO, :, C:NK], tok_f[:, :, C:NK], tok_s[par][:, HI, :, C:NK], ALU.subtract).then_inc(s_tsplit, 1)

            def body(b, par):
                if ahead(b, 2):
                    deviation(b + 2)
                if not first(b):
                    deviation3(b - 1)
                if ahead(b, 2):
                    split_tokens(b + 2, par)
                    mask_bias(b + 2, par)

            pool.wait_ge(s_zero, 8)
            deviation(0)
            mask_bias(0, 0)
            split_tokens(0, 0)
            pool.wait_ge(s_setup, 16 * 9)
            pool.tensor_copy(wr_s[:, HI, :, :], wr_f[:, :, :]).then_inc(s_wsplit, 1)
            pool.wait_ge(s_wkv, 16)
            stage_kv = stage[:, :].rearrange("p (k n) -> p k n", k=KT)
            pool.tensor_copy(wkv_s[:, HI, :, :], stage_kv).then_inc(s_wsplit, 1)
            pool.wait_ge(s_wsplit, 2)
            pool.tensor_tensor(wr_s[:, LO, :, :], wr_f[:, :, :], wr_s[:, HI, :, :], ALU.subtract).then_inc(s_wsplit, 1)
            pool.tensor_tensor(wkv_s[:, LO, :, :], stage_kv, wkv_s[:, HI, :, :], ALU.subtract).then_inc(s_wsplit, 1)
            pool.wait_ge(s_wq, 16)
            pool.wait_ge(s_wout, 16)
            stage_q = stage[:, 0:KT * INNER].rearrange("p (k n) -> p k n", k=KT)
            stage_o = stage[:, KT * INNER:KT * INNER + IT * D].rearrange("p (k n) -> p k n", k=IT)
            pool.tensor_copy(wq_s[:, HI, :, :], stage_q).then_inc(s_wsplit, 1)
            pool.tensor_copy(wout_s[:, HI, :, :], stage_o).then_inc(s_wsplit, 1)
            pool.wait_ge(s_wsplit, 6)
            pool.tensor_tensor(wq_s[:, LO, :, :], stage_q, wq_s[:, HI, :, :], ALU.subtract).then_inc(s_wsplit, 1)
            pool.tensor_tensor(wout_s[:, LO, :, :], stage_o, wout_s[:, HI, :, :], ALU.subtract).then_inc(s_wsplit, 1)
            deviation(1)
            mask_bias(1, 1)
            split_tokens(1, 1)
            run_bodies(pool, body)
            deviation3(B - 1)

        @block.tensor
        def _(pe):
            def product(out, sta, mov, tiles=KT):
                for k in range(tiles):
                    for n, (a, m) in enumerate(PASSES):
                        last = pe.matmul(out, sta(a, k), mov(m, k), start=(k == 0 and n == 0),
                                         stop=(k == tiles - 1 and n == 2))
                return last

            def item(c, par, k):
                ps = ps_p[k % 2]
                need(pe, s_ifree, PI, c, max(k - 1, 0))
                if k == 0:
                    need(pe, s_tsplit, 6, c, 6)
                tok = tok_s[par]
                if k < P_Q:
                    last = product(ps[:, 0:NK], lambda a, t: wkv_s[:, a, t, k * 128:(k + 1) * 128],
                                   lambda a, t: tok[:, a, t, 0:NK])
                elif k < P_V:
                    for n in range(4):
                        j = 4 * (k - P_Q) + n
                        last = product(ps[:, n * T:(n + 1) * T], lambda a, t: wq_s[:, a, t, j * 128:(j + 1) * 128],
                                       lambda a, t: tok[:, a, t, C:NK])
                else:
                    j, half = (k - P_V) // 2, (k - P_V) % 2
                    last = product(ps[0:KB1, :], lambda a, t: tok[:, a, t, j * KB1:(j + 1) * KB1],
                                   lambda a, t: wkv_s[:, a, t, INNER + half * 512:INNER + (half + 1) * 512])
                last.then_inc(s_item, 1)

            def nitem(c, k):
                if k == 0:
                    need(pe, s_norm, 2, c, 2)
                if k < N_L:
                    for j in range(NB0):
                        last = pe.transpose(ps_x[:, j * KB0:(j + 1) * KB0], ctx_n[:, j, k * 128:(k + 1) * 128], ident[0:KB0, 0:KB0])
                else:
                    for t in range(KT):
                        last = pe.transpose(ps_x[:, t * T:(t + 1) * T], x2_n[:, t * 128:(t + 1) * 128], ident[0:T, 0:T])
                last.then_inc(s_nitem, 1)

            def hitem(c, k):
                if k < H_O:
                    for n in range(4):
                        j = 4 * k + n
                        last = pe.transpose(ps_x[:, n * T:(n + 1) * T], o_n[:, 2 * j:2 * j + 2, :].rearrange("p h d -> p (h d)"), ident[0:T, 0:T])
                elif k == H_O:
                    need(pe, s_hhi, 3, c, 2)
                    need(pe, s_hfree, HI_, c, 2)
                    last = product(ps_x[0:T, 0:D], lambda a, t: oT[:, a, t, :], lambda a, t: wout_s[:, a, t, :], IT)
                elif k == H_X:
                    need(pe, s_xn3, 1, c, 1)
                    for t in range(KT):
                        last = pe.transpose(ps_x[:, t * T:(t + 1) * T], xn3[:, t * 128:(t + 1) * 128], ident[0:T, 0:T])
                else:
                    need(pe, s_hhi, 3, c, 3)
                    need(pe, s_hfree, HI_, c, H_X + 1)
                    last = product(ps_x[0:T, 0:E], lambda a, t: x3T[:, a, t, :], lambda a, t: wr_s[:, a, t, :])
                last.then_inc(s_hitem, 1)

            def lend(b, s):
                kind, k = XSLOT[s]
                if kind == "h" and first(b) or kind == "n" and not ahead(b, 2):
                    return
                nh, nn = lent_before(s)
                need(pe, s_oread, 2, b, 0)
                if not first(b):
                    need(pe, s_hfree, HI_, b - 1, nh)
                if ahead(b, 2):
                    need(pe, s_nfree, NI, b + 2, nn)
                if kind == "h":
                    hitem(b - 1, k)
                else:
                    nitem(b + 2, k)

            def scores(b, par, h):
                if h == 0:
                    need(pe, s_qdup, 128, b, 128)
                    need(pe, s_kstack, 64, b, 64)
                need(pe, s_max, H, b, h - 1)
                for part in (HI, LO):
                    last = pe.matmul(ps_s[h % 2][0:T, 0:NK], q_dup[par][:, part, h, :], k_stack[par][:, h, :],
                                     start=(part == HI), stop=(part == LO))
                last.then_inc(s_score, 1)

            def transposes(b, h):
                need(pe, s_exp, H, b, h + 1)
                need(pe, s_plo, H, b, h - 1)
                for j in range(NB1):
                    last = pe.transpose(ps_t[h % 2][0:KB1, j * T:(j + 1) * T],
                                        prob[:, h % RING, j * KB1:(j + 1) * KB1], ident[0:T, 0:T])
                last.then_inc(s_tr, 1)

            def values(b, par, h):
                need(pe, s_phi, H, b, h + 1)
                need(pe, s_plo, H, b, h + 1)
                if h == 0:
                    need(pe, s_oread, 2, b, 0)
                    need(pe, s_ihi, PI, b, PI)
                    need(pe, s_ifree, PI, b, PI)
                if h == H // 2:
                    if not first(b):
                        need(pe, s_hfree, HI_, b - 1, HI_)
                    if ahead(b, 2):
                        need(pe, s_nfree, NI, b + 2, NI)
                col = (h % 8) * D1
                for j in range(NB1):
                    for n, (a, m) in enumerate(PASSES):
                        last = pe.matmul(ps_o[h // 8][:, col:col + D1], pT[0:KB1, h % 2, a, j, :],
                                         v_s[par][0:KB1, m, j, h * D1:(h + 1) * D1],
                                         start=(h % 8 == 0 and j == 0 and n == 0),
                                         stop=(j == NB1 - 1 and n == 2), skip_group_check=True)
                last.then_inc(s_pv, 1)

            def body(b, par):
                for s in range(H):
                    scores(b, par, s)
                    if not (first(b) and s < 2):
                        c, _, h = behind(s, 2, b, par)
                        transposes(c, h)
                    if ahead(b, 1):
                        for k in PSLOT.get(s, []):
                            item(b + 1, 1 - par, k)
                    if not (first(b) and s < 3):
                        values(*behind(s, 3, b, par))
                    if s in XSLOT:
                        lend(b, s)

            pe.wait_ge(s_setup, 16 * 9)
            pe.wait_ge(s_zero, 8)
            for k in range(NI):
                need(pe, s_nfree, NI, 0, k)
                nitem(0, k)
            for k in range(NI):
                need(pe, s_nfree, NI, 1, k)
                nitem(1, k)
            pe.wait_ge(s_wsplit, 8)
            for k in range(PI):
                item(0, 0, k)
            run_bodies(pe, body)
            transposes(B - 1, H - 2)
            values(B - 1, 1, H - 3)
            transposes(B - 1, H - 1)
            values(B - 1, 1, H - 2)
            values(B - 1, 1, H - 1)
            need(pe, s_oread, 2, B, 0)
            for k in range(HI_):
                need(pe, s_hfree, HI_, B - 1, k)
                hitem(B - 1, k)

        @block.scalar
        def _(act):
            def item(c, par, k):
                ps = ps_p[k % 2]
                need(act, s_item, PI, c, k + 1)
                if k < P_Q:
                    if k == 0:
                        need(act, s_kstack, 64, c, 0)
                    act.activation(k_s[:, HI, k, :], ps[:, 0:NK], ACT.Copy).then_inc(s_ihi, 1)
                elif k < P_V:
                    j = 4 * (k - P_Q)
                    if j == 0:
                        need(act, s_qdup, 128, c, 0)
                    act.activation(q_s[:, HI, j:j + 4, :], ps[:, 0:4 * T].rearrange("p (j n) -> p j n", j=4), ACT.Copy).then_inc(s_ihi, 1)
                else:
                    j, half = (k - P_V) // 2, (k - P_V) % 2
                    need(act, s_pv, H, c - 1, 0)
                    act.activation(v_s[par][0:KB1, HI, j, half * 512:(half + 1) * 512], ps[0:KB1, :], ACT.Copy).then_inc(s_ihi, 1)

            def hitem(c, k):
                if k < H_O:
                    need(act, s_hitem, HI_, c, k + 1)
                    act.activation(oT[:, HI, 4 * k:4 * k + 4, :], ps_x[:, 0:4 * T].rearrange("p (j n) -> p j n", j=4), ACT.Copy).then_inc(s_hhi, 1)
                elif k == H_X:
                    need(act, s_hitem, HI_, c, k + 1)
                    need(act, s_store, 48, c, 0)
                    act.activation(x3T[:, HI, :, :], ps_x[:, 0:KT * T].rearrange("p (t n) -> p t n", t=KT), ACT.Copy).then_inc(s_hhi, 1)

            def exps(b, par, h):
                need(act, s_max, H, b, h + 1)
                act.activation(prob[:, h % RING, 0:NK], prob[:, h % RING, 0:NK], ACT.Exp, bias=top[:, h % RING:h % RING + 1],
                               scale=-1.0, accum_out=sums[par][:, h:h + 1]).then_inc(s_exp, 1)

            def phi(b, h):
                need(act, s_tr, H, b, h + 1)
                need(act, s_pv, H, b, h - 1)
                act.activation(pT[0:KB1, h % 2, HI, :, 0:T],
                               ps_t[h % 2][0:KB1, 0:NB1 * T].rearrange("p (j n) -> p j n", j=NB1), ACT.Copy).then_inc(s_phi, 1)

            def weigh(c):
                need(act, s_route, ROUTE, c, 4)
                act.activation(ratio[:, :], gap[:, :], ACT.Exp).then_inc(s_ratio, 1)

            def body(b, par):
                for s in range(H):
                    if ahead(b, 1):
                        for k in PSLOT.get(s - 1, []):
                            item(b + 1, 1 - par, k)
                    if not first(b):
                        kind, k = XSLOT.get(s - 1, ("", 0))
                        if kind == "h":
                            hitem(b - 1, k)
                        if s == 11:
                            weigh(b - 1)
                    if not (first(b) and s < 1):
                        exps(*behind(s, 1, b, par))
                    if not (first(b) and s < 2):
                        c, _, h = behind(s, 2, b, par)
                        phi(c, h)

            act.wait_ge(s_setup, 16 * 9)
            act.wait_ge(s_zero, 8)
            act.activation(tanhs[:, :], gates[:, :], ACT.Tanh).then_inc(s_tanh, 1)
            for k in range(PI):
                item(0, 0, k)
            run_bodies(act, body)
            exps(B - 1, 1, H - 1)
            phi(B - 1, H - 2)
            phi(B - 1, H - 1)
            for k in range(HI_):
                hitem(B - 1, k)
            weigh(B - 1)

        @block.vector
        def _(dve):
            settled = (s_zero, 8)

            def stats(c):
                need(dve, s_cload, 16, c, 16)
                for j in range(NB0):
                    dve.bn_stats(bns[0:KB0, j, :], ctx_t[:, j, :]).then_inc(s_stats, 1)
                need(dve, s_xload, 16, c, 16)
                dve.bn_stats(bns[0:T, NB0, :], x2_t[:, :]).then_inc(s_stats, 1)
                need(dve, s_stats, 8, c, 4, settled)
                for j in range(NB0):
                    dve.bn_aggr(mv[0:KB0, j, :], bns[0:KB0, j, :]).then_inc(s_stats, 1)
                dve.bn_aggr(mv[0:T, NB0, :], bns[0:T, NB0, :]).then_inc(s_stats, 1)

            def normalise(c):
                need(dve, s_rstd, 1, c, 1)
                need(dve, s_nitem, NI, c, 0)
                for j in range(NB0):
                    last = dve.tensor_scalar(ctx_n[:, j, :], ctx_t[:, j, :], mv[0:KB0, j, 0:1], rstd[0:KB0, j:j + 1], ALU.subtract, ALU.mult)
                last.then_inc(s_norm, 1)
                dve.tensor_scalar(x2_n[:, :], x2_t[:, :], mv[0:T, NB0, 0:1], rstd[0:T, NB0:NB0 + 1], ALU.subtract, ALU.mult).then_inc(s_norm, 1)

            def nitem(c, k):
                need(dve, s_nitem, NI, c, k + 1)
                if k == 0:
                    need(dve, s_tsplit, 6, c, 0)
                if k < N_L:
                    dve.tensor_scalar(tok_f[:, k, 0:C], ps_x[:, 0:C], affine[:, 0, k:k + 1], affine[:, 1, k:k + 1], ALU.mult, ALU.add).then_inc(s_nfree, 1)
                else:
                    for t in range(KT):
                        last = dve.tensor_scalar(tok_f[:, t, C:NK], ps_x[:, t * T:(t + 1) * T], affine[:, 2, t:t + 1], affine[:, 3, t:t + 1], ALU.mult, ALU.add)
                    last.then_inc(s_nfree, 1)

            def item(c, par, k):
                ps = ps_p[k % 2]
                need(dve, s_ihi, PI, c, k + 1)
                if k < P_Q:
                    dve.tensor_tensor(k_s[:, LO, k, :], ps[:, 0:NK], k_s[:, HI, k, :], ALU.subtract).then_inc(s_ifree, 1)
                elif k < P_V:
                    j = 4 * (k - P_Q)
                    dve.tensor_tensor(q_s[:, LO, j:j + 4, :], ps[:, 0:4 * T].rearrange("p (j n) -> p j n", j=4), q_s[:, HI, j:j + 4, :], ALU.subtract).then_inc(s_ifree, 1)
                else:
                    j, half = (k - P_V) // 2, (k - P_V) % 2
                    cols = slice(half * 512, (half + 1) * 512)
                    dve.tensor_tensor(v_s[par][0:KB1, LO, j, cols], ps[0:KB1, :], v_s[par][0:KB1, HI, j, cols], ALU.subtract).then_inc(s_ifree, 1)

            def maxima(b, par, h):
                need_all(dve, settled, (s_score, H, b, h + 1), (s_tr, H, b, h - RING + 1), *([(s_keep, 1, b, 1)] if h == 0 else []))
                dve.tensor_tensor_reduce(prob[:, h % RING, 0:NK], ps_s[h % 2][0:T, 0:NK], keep[par][:, :], -SCALE1, 3e38,
                                         ALU.add, ALU.min, top[:, h % RING:h % RING + 1]).then_inc(s_max, 1)

            def plo(b, h):
                need(dve, s_phi, H, b, h + 1)
                dve.tensor_tensor(pT[0:KB1, h % 2, LO, :, 0:T],
                                  ps_t[h % 2][0:KB1, 0:NB1 * T].rearrange("p (j n) -> p j n", j=NB1),
                                  pT[0:KB1, h % 2, HI, :, 0:T], ALU.subtract).then_inc(s_plo, 1)

            def out_heads(c, par):
                need(dve, s_exp, H, c, H)
                dve.reciprocal(rsum[:, :], sums[par][:, :]).then_inc(s_rsum, 1)
                need(dve, s_rsum, 1, c, 1)
                need(dve, s_pv, H, c, H)
                need(dve, s_hitem, HI_, c, 0)
                for i in range(2):
                    dve.tensor_tensor(o_n[:, 8 * i:8 * i + 8, :], ps_o[i][0:T, :].rearrange("p (h d) -> p h d", h=8),
                                      rsum[:, 8 * i:8 * i + 8].unsqueeze(2).to_broadcast([T, 8, D1]), ALU.mult).then_inc(s_oread, 1)

            def hitem(c, k):
                if k < H_O:
                    need(dve, s_hhi, 3, c, k + 1)
                    dve.tensor_tensor(oT[:, LO, 4 * k:4 * k + 4, :], ps_x[:, 0:4 * T].rearrange("p (j n) -> p j n", j=4), oT[:, HI, 4 * k:4 * k + 4, :], ALU.subtract).then_inc(s_hfree, 1)
                elif k == H_O:
                    need(dve, s_hitem, HI_, c, k + 1)
                    need(dve, s_rload, 16, c, 16)
                    need(dve, s_store, 48, c, 0)
                    dve.scalar_tensor_tensor(x3[:, :], ps_x[0:T, 0:D], tanhs[0:T, 1:2], x_res[:, :], ALU.mult, ALU.add).then_inc(s_hfree, 1)
                    need(dve, s_hfree, HI_, c, k + 1)
                    dve.bn_stats(bns3[:, :], x3[:, :]).then_inc(s_stats3, 1)
                    need(dve, s_stats3, 2, c, 1, settled)
                    dve.bn_aggr(mv3[:, :], bns3[:, :]).then_inc(s_stats3, 1)
                elif k == H_X:
                    need(dve, s_hhi, 3, c, 3)
                    dve.tensor_tensor(x3T[:, LO, :, :], ps_x[:, 0:KT * T].rearrange("p (t n) -> p t n", t=KT), x3T[:, HI, :, :], ALU.subtract).then_inc(s_hfree, 1)
                else:
                    need(dve, s_hitem, HI_, c, k + 1)
                    dve.tensor_tensor(logit[:, :], ps_x[0:T, 0:E], br_r[0:T, :], ALU.add).then_inc(s_hfree, 1)
                    need(dve, s_hfree, HI_, c, k + 1, settled)
                    dve.max(best[:, :], logit[:, :]).then_inc(s_route, 1)
                    need(dve, s_route, ROUTE, c, 1, settled)
                    dve.max_index(place[:, :], best[:, :], logit[:, :]).then_inc(s_route, 1)
                    need(dve, s_route, ROUTE, c, 2)
                    dve.tensor_copy(place_f[:, :], place[:, :]).then_inc(s_route, 1)
                    dve.tensor_tensor(gap[:, :], best[:, 1:2], best[:, 0:1], ALU.subtract).then_inc(s_route, 1)

            def norm_x3(c):
                need(dve, s_rstd3, 1, c, 1)
                dve.tensor_scalar(xn3[:, :], x3[:, :], mv3[:, 0:1], rstd3[:, 0:1], ALU.subtract, ALU.mult).then_inc(s_xn3, 1)

            def combine_weights(c):
                need(dve, s_ratio, 1, c, 1)
                dve.tensor_scalar(norm[:, :], ratio[:, :], 1.0, None, ALU.add).then_inc(s_route, 1)
                need(dve, s_route, ROUTE, c, 5)
                dve.reciprocal(share[:, :], norm[:, :]).then_inc(s_route, 1)
                need(dve, s_route, ROUTE, c, 6)
                dve.tensor_scalar(w_top[:, 0:1], share[:, :], tanhs[0:T, 3:4], None, ALU.mult)
                dve.tensor_scalar(w_top[:, 1:2], share[:, :], tanhs[0:T, 3:4], ratio[:, 0:1], ALU.mult, ALU.mult).then_inc(s_route, 1)
                need(dve, s_route, ROUTE, c, 7)
                for n in range(2):
                    last = dve.tensor_scalar(picked[:, n, :], const[0:T, IOTA:IOTA + E], place_f[:, n:n + 1], w_top[:, n:n + 1],
                                             ALU.is_equal, ALU.mult)
                last.then_inc(s_route, 1)
                need(dve, s_route, ROUTE, c, 8)
                dve.tensor_tensor(cw[:, :], picked[:, 0, :], picked[:, 1, :], ALU.add).then_inc(s_route, 1)

            def body(b, par):
                for s in range(H):
                    if ahead(b, 1):
                        for k in PSLOT.get(s - 1, []):
                            item(b + 1, 1 - par, k)
                    if not first(b) and s == 3:
                        out_heads(b - 1, 1 - par)
                    kind, k = XSLOT.get(s - 1, ("", 0))
                    if kind == "h" and not first(b):
                        hitem(b - 1, k)
                    if kind == "n" and ahead(b, 2):
                        nitem(b + 2, k)
                    if not first(b):
                        if s == 8:
                            norm_x3(b - 1)
                        if s == 12:
                            combine_weights(b - 1)
                    if ahead(b, 2):
                        if s == 1:
                            stats(b + 2)
                        if s == 2:
                            normalise(b + 2)
                    maxima(b, par, s)
                    if not (first(b) and s < 2):
                        c, _, h = behind(s, 2, b, par)
                        plo(c, h)

            dve.wait_ge(s_setup, 16 * 9)
            dve.wait_ge(s_zero, 8)
            dve.wait_ge(s_tanh, 1)
            for c in range(2):
                stats(c)
                normalise(c)
                for k in range(NI):
                    nitem(c, k)
            for k in range(PI):
                item(0, 0, k)
            run_bodies(dve, body)
            plo(B - 1, H - 2)
            plo(B - 1, H - 1)
            out_heads(B - 1, 1)
            for k in range(H_X):
                hitem(B - 1, k)
            norm_x3(B - 1)
            hitem(B - 1, H_X)
            hitem(B - 1, H_G)
            combine_weights(B - 1)

F = 512
FT = F // 128
W1N, W2N = KT * 2 * F, FT * D
NG = 4
GB = B // NG
G = GB * T

def phase_experts(nc, w_all, b2, consts, x3_dram, x3T_dram, cw_dram, out):
    with ExitStack() as ctx:
        sb = lambda name, shape, dt: ctx.enter_context(nc.sbuf_tensor("c_" + name, shape, dt))
        sem = lambda name: ctx.enter_context(nc.semaphore("c_" + name))
        bank = lambda name: ctx.enter_context(nc.psum_tensor("c_" + name, [128, 512], F32))

        const = sb("const", [128, NCONST], F32)
        ident = const[:, IDENT:IDENT + 128]
        x_T = sb("x_T", [128, B, 2, KT, T], F16)
        x_s = sb("x_s", [128, 2, KT, B, T], F16)
        x3 = sb("x3", [T, B, D], F32)
        acc = sb("acc", [T, B, D], F32)
        cw = sb("cw", [T, B, E], F32)
        cw_e = [sb(f"cw_e{i}", [T, B], F32) for i in range(2)]
        cwT_f = sb("cwT_f", [128, T], F32)
        cwT_s = sb("cwT_s", [128, 2, T], F16)
        cwT_b = sb("cwT_b", [128, 2, B, T], F16)
        b2_f = sb("b2_f", [128, D], F32)
        b2_s = sb("b2_s", [128, 2, D], F16)
        w_f = [sb(f"w_f{i}", [128, W1N + W2N + 8], F32) for i in range(2)]
        w_s = [sb(f"w_s{i}", [128, 2, W1N + W2N], F16) for i in range(2)]
        b1 = [sb(f"b1{i}", [128, 8], F32) for i in range(2)]
        sil = sb("sil", [128, 2, G], F32)
        act_f = sb("act_f", [128, 2, G], F32)
        act_s = sb("act_s", [128, 2, 2, FT, G], F16)

        ps_a = [bank(f"ps_a{i}") for i in range(2)]
        ps_g = [bank(f"ps_g{i}") for i in range(2)]
        ps_y = [bank(f"ps_y{i}") for i in range(GB)]

        s_setup = sem("setup")
        s_xT = sem("xT")
        s_xs = sem("xs")
        s_cw = sem("cw")
        s_cwT = sem("cwT")
        s_cwf = sem("cwf")
        s_cws = sem("cws")
        s_cwb = sem("cwb")
        s_b2 = sem("b2")
        s_bias = sem("bias")
        s_acc = sem("acc")
        s_wload = sem("wload")
        s_wsplit = sem("wsplit")
        s_cwe = sem("cwe")
        s_a = sem("a")
        s_g = sem("g")
        s_sil = sem("sil")
        s_act = sem("act")
        s_ahi = sem("ahi")
        s_alo = sem("alo")
        s_y = sem("y")
        s_yread = sem("yread")
        s_store = sem("store")

        PAIRS = NG * FT

        def run_experts(eng, body):
            body(0, 0)
            body(1, 1)
            with eng.Fori(1, E // 2) as i:
                body(i * 2, 0)
                body(i * 2 + 1, 1)

        block = ctx.enter_context(nc.Block())

        @block.sync
        def _(sp):
            settled = (s_setup, 32)

            def load(e, par):
                sp.dma_start(w_f[par][:, :], w_all[e]).then_inc(s_wload, 16)

            sp.dma_start(const[:, :], consts).then_inc(s_setup, 16)
            sp.dma_start(cw[:, :, :], cw_dram.rearrange("b t e -> t b e")).then_inc(s_cw, 16)
            load(0, 0)
            sp.dma_start(x_T[:, :, :, :, :], x3T_dram.rearrange("b p s k n -> p b s k n")).then_inc(s_xT, 16)
            sp.dma_start(b2_f[:, :], b2).then_inc(s_b2, 16)
            sp.dma_start(x3[:, :, :], x3_dram.rearrange("b t d -> t b d")).then_inc(s_setup, 16)
            need(sp, s_wsplit, 3, 0, 1)
            load(1, 1)
            with sp.Fori(0, E // 2 - 1) as i:
                for par in range(2):
                    need(sp, s_wsplit, 3, i * 2 + par + 1, 1, settled)
                    load(i * 2 + par + 2, par)
            for g in range(NG):
                need(sp, s_yread, B, E - 1, (g + 1) * GB, settled)
                sp.dma_start(out[g * GB:(g + 1) * GB].rearrange("b t d -> t b d"), acc[:, g * GB:(g + 1) * GB, :]).then_inc(s_store, 16)
            sp.wait_ge(s_store, 16 * NG)

        @block.gpsimd
        def _(pool):
            settled = (s_setup, 32)

            def split_weights(e, par):
                need_all(pool, settled, (s_wload, 16, e, 16), (s_y, B, e - 1, 0), (s_act, PAIRS, e - 1, 0))
                pool.tensor_copy(w_s[par][:, HI, :], w_f[par][:, 0:W1N + W2N]).then_inc(s_wsplit, 1)
                need(pool, s_wsplit, 3, e, 1)
                pool.tensor_tensor(w_s[par][:, LO, :], w_f[par][:, 0:W1N + W2N], w_s[par][:, HI, :], ALU.subtract).then_inc(s_wsplit, 1)
                pool.tensor_copy(b1[par][:, :], w_f[par][:, W1N + W2N:]).then_inc(s_wsplit, 1)

            split_weights(0, 0)
            split_weights(1, 1)
            with pool.Fori(0, E // 2 - 1) as i:
                split_weights(i * 2 + 2, 0)
                split_weights(i * 2 + 3, 1)

        @block.tensor
        def _(pe):
            def product(out_, sta, mov, tiles):
                for k in range(tiles):
                    for n, (a, m) in enumerate(PASSES):
                        last = pe.matmul(out_, sta(a, k), mov(m, k), start=(k == 0 and n == 0),
                                         stop=(k == tiles - 1 and n == 2))
                return last

            def hidden(e, par, g, m):
                n = g * FT + m
                w1 = w_s[par][:, :, 0:W1N].rearrange("p s (k n) -> p s k n", k=KT)
                xg = lambda a, t: x_s[:, a, t, g * GB:(g + 1) * GB, :].rearrange("p b n -> p (b n)")
                need(pe, s_sil, PAIRS, e, n - 1)
                product(ps_a[n % 2][:, 0:G], lambda a, t: w1[:, a, t, m * 128:(m + 1) * 128], xg, KT).then_inc(s_a, 1)
                need(pe, s_act, PAIRS, e, n - 1)
                product(ps_g[n % 2][:, 0:G], lambda a, t: w1[:, a, t, F + m * 128:F + (m + 1) * 128], xg, KT).then_inc(s_g, 1)

            def outputs(e, par, g):
                w2 = w_s[par][:, :, W1N:].rearrange("p s (k n) -> p s k n", k=FT)
                need(pe, s_alo, PAIRS, e, (g + 1) * FT)
                for i in range(GB):
                    need(pe, s_yread, B, e, (g - 1) * GB + i + 1)
                    product(ps_y[i][0:T, 0:D], lambda a, t: act_s[:, g % 2, a, t, i * T:(i + 1) * T],
                            lambda a, t: w2[:, a, t, :], FT).then_inc(s_y, 1)

            def body(e, par):
                need(pe, s_wsplit, 3, e, 2)
                for g in range(NG):
                    for m in range(FT):
                        hidden(e, par, g, m)
                        if m == 1 and g > 0:
                            outputs(e, par, g - 1)
                outputs(e, par, NG - 1)

            pe.wait_ge(s_setup, 16)
            pe.wait_ge(s_cw, 16)
            pe.transpose(ps_a[0][:, 0:T], cw[:, :, :].rearrange("t b e -> t (b e)"), ident[0:T, 0:T]).then_inc(s_cwT, 1)
            pe.wait_ge(s_cwb, 2)
            pe.wait_ge(s_b2, 18)
            for b in range(B):
                if b >= GB:
                    pe.wait_ge(s_acc, b - GB + 1)
                for n, (a, m) in enumerate(PASSES):
                    last = pe.matmul(ps_y[b % GB][0:T, 0:D], cwT_b[:, a, b, :], b2_s[:, m, :], start=(n == 0), stop=(n == 2))
                last.then_inc(s_bias, 1)
            pe.wait_ge(s_acc, B)
            pe.wait_ge(s_xs, 2)
            run_experts(pe, body)

        @block.scalar
        def _(act):
            def silu(e, par, n):
                m = n % FT
                if n == 0:
                    need(act, s_wsplit, 3, e, 3)
                need(act, s_a, PAIRS, e, n + 1)
                need(act, s_act, PAIRS, e, n - 1)
                act.activation(sil[:, n % 2, :], ps_a[n % 2][:, 0:G], ACT.Silu, bias=b1[par][:, m:m + 1]).then_inc(s_sil, 1)

            def high(e, n):
                g, m = n // FT, n % FT
                need(act, s_act, PAIRS, e, n + 1)
                if m == 0:
                    need(act, s_y, B, e, (g - 1) * GB)
                act.activation(act_s[:, g % 2, HI, m, :], act_f[:, n % 2, :], ACT.Copy).then_inc(s_ahi, 1)

            def body(e, par):
                for n in range(PAIRS):
                    silu(e, par, n)
                    if n:
                        high(e, n - 1)
                high(e, PAIRS - 1)

            act.wait_ge(s_cwT, 1)
            act.activation(cwT_f[:, :], ps_a[0][:, 0:T], ACT.Copy).then_inc(s_cwf, 1)
            act.wait_ge(s_xT, 16)
            act.activation(x_s[:, HI, :, :, :].rearrange("p k b n -> p b k n"), x_T[:, :, HI, :, :], ACT.Copy).then_inc(s_xs, 1)
            run_experts(act, body)

        @block.vector
        def _(dve):
            def product_act(e, par, n):
                m = n % FT
                need(dve, s_sil, PAIRS, e, n + 1)
                need(dve, s_g, PAIRS, e, n + 1)
                need(dve, s_alo, PAIRS, e, n - 1)
                dve.scalar_tensor_tensor(act_f[:, n % 2, :], ps_g[n % 2][:, 0:G], b1[par][:, FT + m:FT + m + 1], sil[:, n % 2, :],
                                         ALU.add, ALU.mult).then_inc(s_act, 1)

            def low(e, n):
                g, m = n // FT, n % FT
                need(dve, s_ahi, PAIRS, e, n + 1)
                dve.tensor_tensor(act_s[:, g % 2, LO, m, :], act_f[:, n % 2, :], act_s[:, g % 2, HI, m, :], ALU.subtract).then_inc(s_alo, 1)

            def add(e, par, g):
                for i in range(GB):
                    b = g * GB + i
                    need(dve, s_y, B, e, b + 1)
                    need(dve, s_yread, B, e, 0)
                    dve.scalar_tensor_tensor(acc[:, b, :], ps_y[i][0:T, 0:D], cw_e[par][:, b:b + 1], acc[:, b, :],
                                             ALU.mult, ALU.add).then_inc(s_yread, 1)

            def body(e, par):
                need(dve, s_yread, B, e - 1, 0)
                dve.tensor_copy(cw_e[par][:, :], cw[:, :, bass.ds(e, 1)].rearrange("t b o -> t (b o)")).then_inc(s_cwe, 1)
                need(dve, s_cwe, 1, e, 1)
                for n in range(PAIRS):
                    product_act(e, par, n)
                    if n:
                        low(e, n - 1)
                    if n % FT == 2 and n > FT:
                        add(e, par, n // FT - 1)
                low(e, PAIRS - 1)
                add(e, par, NG - 1)

            dve.wait_ge(s_b2, 16)
            dve.tensor_copy(b2_s[:, HI, :], b2_f[:, :]).then_inc(s_b2, 1)
            dve.wait_ge(s_b2, 17)
            dve.tensor_tensor(b2_s[:, LO, :], b2_f[:, :], b2_s[:, HI, :], ALU.subtract).then_inc(s_b2, 1)
            dve.wait_ge(s_cwf, 1)
            dve.tensor_copy(cwT_s[:, HI, :], cwT_f[:, :]).then_inc(s_cws, 1)
            dve.wait_ge(s_cws, 1)
            dve.tensor_tensor(cwT_s[:, LO, :], cwT_f[:, :], cwT_s[:, HI, :], ALU.subtract).then_inc(s_cws, 1)
            dve.wait_ge(s_cws, 2)
            dve.wait_ge(s_setup, 32)
            for part in (HI, LO):
                dve.tensor_tensor(cwT_b[:, part, :, :], cwT_s[:, part, :].unsqueeze(1).to_broadcast([128, B, T]),
                                  const[:, BATCHMASK:BATCHMASK + B].unsqueeze(2).to_broadcast([128, B, T]), ALU.mult).then_inc(s_cwb, 1)
            dve.wait_ge(s_xT, 16)
            dve.tensor_copy(x_s[:, LO, :, :, :].rearrange("p k b n -> p b k n"), x_T[:, :, LO, :, :]).then_inc(s_xs, 1)
            for b in range(B):
                dve.wait_ge(s_bias, b + 1)
                dve.tensor_tensor(acc[:, b, :], ps_y[b % GB][0:T, 0:D], x3[:, b, :], ALU.add).then_inc(s_acc, 1)
            dve.wait_ge(s_acc, B)
            run_experts(dve, body)

def build_program(nc, a, out):
    x2 = nc.dram_tensor("x2", (B, T, D), F32, kind="Internal").ap()
    x3 = nc.dram_tensor("x3", (B, T, D), F32, kind="Internal").ap()
    x3T = nc.dram_tensor("x3T", (B, 128, 2, KT, T), F16, kind="Internal").ap()
    cw = nc.dram_tensor("cw", (B, T, E), F32, kind="Internal").ap()
    phase_attention_small_heads(nc, a["x"], a["ctxT"], a["mask0"], a["g_xattn"], a["g_ffn"], a["wq0"], a["wk0"], a["wv0"],
                                a["bq0"], a["bk0"], a["bv0"], a["wg0"], a["we0"], a["be0"], a["consts"], x2)
    phase_attention_large_heads(nc, a["ctx"], a["mask1"], a["g_xattn"], a["g_ffn"], a["g1"], a["b1"], a["g2"], a["b2"],
                                a["wq1"], a["wkv1"], a["wout1"], a["wr1"], a["br1"], a["consts"], x2, x3, x3T, cw)
    phase_experts(nc, a["w_experts"], a["b2_experts"], a["consts"], x3, x3T, cw, out)

def kernel(x, ctx_1024, mask_BxSxS2_ff1, mask_BxS2_bk0, g_xattn, g_ffn,
           L0_xattn_Wq, L0_xattn_bq, L0_xattn_Wk, L0_xattn_bk, L0_xattn_Wv, L0_xattn_bv,
           L0_ffn_Wg, L0_ffn_We, L0_ffn_be,
           L1_xattn_g1, L1_xattn_b1, L1_xattn_g2, L1_xattn_b2, L1_xattn_Wq, L1_xattn_Wkv, L1_xattn_Wout,
           L1_ffn_W1, L1_ffn_b1, L1_ffn_W2, L1_ffn_b2, L1_ffn_Wr, L1_ffn_br):
    import numpy as np
    import concourse.bacc as bacc
    from concourse.bass_utils import run_bass_kernel_spmd

    rows = lambda w: w.reshape(-1, 128, w.shape[-1]).transpose(1, 0, 2)
    column = lambda v: v.reshape(-1, 128).T
    twice = lambda w: np.concatenate([w, w], -1)

    p = np.arange(128)
    consts = np.zeros((128, NCONST), np.float32)
    consts[:, IDENT:IDENT + 128] = np.eye(128)
    consts[:, HEADMASK:HEADMASK + 4] = (p[:, None] // D0) % 4 == np.arange(4)
    consts[:, IOTA:IOTA + E] = np.arange(E)
    consts[:, BATCHMASK:BATCHMASK + B] = p[:, None] // E == np.arange(B)

    as_np = np.asarray
    experts = [as_np(L1_ffn_W1).reshape(E, KT, 128, 2 * F).transpose(0, 2, 1, 3).reshape(E, 128, W1N),
               as_np(L1_ffn_W2).reshape(E, FT, 128, D).transpose(0, 2, 1, 3).reshape(E, 128, W2N),
               as_np(L1_ffn_b1).reshape(E, 2 * FT, 128).transpose(0, 2, 1)]
    arrays = {
        "x": as_np(x), "ctx": as_np(ctx_1024), "consts": consts,
        "ctxT": as_np(ctx_1024).reshape(B, C, KT, 128).transpose(0, 3, 2, 1),
        "mask0": as_np(mask_BxSxS2_ff1), "mask1": as_np(mask_BxS2_bk0),
        "g_xattn": as_np(g_xattn), "g_ffn": as_np(g_ffn),
        "wq0": rows(twice(as_np(L0_xattn_Wq).T.reshape(D, GROUPS, 64)).reshape(D, 128 * GROUPS)),
        "bq0": twice(as_np(L0_xattn_bq).reshape(GROUPS, 64)).T,
        "wk0": rows(as_np(L0_xattn_Wk).T), "bk0": column(as_np(L0_xattn_bk)),
        "wv0": rows(as_np(L0_xattn_Wv).T), "bv0": as_np(L0_xattn_bv),
        "wg0": rows(as_np(L0_ffn_Wg).T), "we0": rows(as_np(L0_ffn_We).transpose(2, 0, 1).reshape(D, E * D)),
        "be0": as_np(L0_ffn_be),
        "g1": column(as_np(L1_xattn_g1)), "b1": column(as_np(L1_xattn_b1)),
        "g2": column(as_np(L1_xattn_g2)), "b2": column(as_np(L1_xattn_b2)),
        "wq1": rows(as_np(L1_xattn_Wq)), "wkv1": rows(as_np(L1_xattn_Wkv)), "wout1": rows(as_np(L1_xattn_Wout)),
        "wr1": rows(as_np(L1_ffn_Wr)), "br1": as_np(L1_ffn_br),
        "w_experts": np.concatenate(experts, 2), "b2_experts": np.tile(as_np(L1_ffn_b2), (B, 1)),
    }
    nc = bacc.Bacc("TRN2", target_bir_lowering=False, num_devices=1)
    inputs, aps = {}, {}
    for name, array in arrays.items():
        array = np.ascontiguousarray(array)
        inputs[f"in_{name}"] = array
        aps[name] = nc.dram_tensor(f"in_{name}", array.shape, mybir.dt.from_np(array.dtype), kind="ExternalInput").ap()
    out = nc.dram_tensor("out", (B, T, D), F32, kind="ExternalOutput").ap()
    build_program(nc, aps, out)
    result = run_bass_kernel_spmd(nc, [inputs], core_ids=[0])
    return result.results[0]["out"]
```

```python
from contextlib import ExitStack

import concourse.bass as bass
from concourse import mybir

ALU = mybir.AluOpType
ACT = mybir.ActivationFunctionType
F32 = mybir.dt.float32
F16 = mybir.dt.float16
U32 = mybir.dt.uint32
U8 = mybir.dt.uint8

B = 16
T = 112
C = 375
D = 256
KT = D // 128
E = 8
H = 16
EPS = 1e-5
HI, LO = 0, 1
PASSES = ((HI, HI), (HI, LO), (LO, HI))

D0 = D // H
KB0, NB0 = 125, 3
SCALE0 = D0 ** -0.5
GROUPS = 4

IDENT, HEADMASK, IOTA, BATCHMASK, NCONST = 0, 128, 132, 140, 156

def need(eng, sem, per, batch, count, met=None):
    need_all(eng, met, (sem, per, batch, count))

def need_all(eng, met, *conditions):
    values = [(sem, batch * per + count) for sem, per, batch, count in conditions]
    values = [(sem, v) for sem, v in values if not isinstance(v, int) or v > 0]
    if met and any(not isinstance(v, int) for _, v in values):
        values = [(sem, v if isinstance(v, int) else eng.to_reg(v)) for sem, v in values]
        eng.wait_ge(*met)
    for sem, v in values:
        eng.wait_ge(sem, v)

def run_batches(eng, body):
    body(0, 0)
    body(1, 1)
    with eng.Fori(1, B // 2 - 1) as i:
        body(i * 2, 0)
        body(i * 2 + 1, 1)
    body(B - 2, 0)
    body(B - 1, 1)

def first(b):
    return isinstance(b, int) and b == 0

def ahead(b, n):
    return not (isinstance(b, int) and b + n > B - 1)

def phase_attention_small_heads(nc, x, ctxT, mask, g_xattn, g_ffn, wq, wk, wv, bq, bk, bv, wg, we, be, consts,
                                x2_dram, next_w, next_w_dram):
    with ExitStack() as ctx:
        sb = lambda name, shape, dt: ctx.enter_context(nc.sbuf_tensor("a_" + name, shape, dt))
        sem = lambda name: ctx.enter_context(nc.semaphore("a_" + name))
        bank = lambda name: ctx.enter_context(nc.psum_tensor("a_" + name, [128, 512], F32))

        const = sb("const", [128, NCONST], F32)
        ident = const[:, IDENT:IDENT + 128]
        neg_half = sb("neg_half", [128, 1], F32)
        wqkv_f = sb("wqkv_f", [128, KT, 512 + 512 + E], F32)
        wqkv = sb("wqkv", [128, 2, KT, 512 + 512 + E], F16)
        we_f = sb("we_f", [128, KT, E * D], F32)
        we_s = sb("we_s", [128, 2, KT, E * D], F16)
        NEXT = next_w_dram.shape[1] // H
        WE = E * D // (H // 2)
        next_f = sb("next_f", [128, next_w_dram.shape[1]], F32)
        be_f = sb("be_f", [128, D], F32)
        be_s = sb("be_s", [128, 2, D], F16)
        wq_s = wqkv[:, :, :, 0:512].rearrange("p s k (g m) -> p s k g m", g=GROUPS)
        wk_s = wqkv[:, :, :, 512:768]
        wv_s = wqkv[:, :, :, 768:1024]
        wg_s = wqkv[:, :, :, 1024:1024 + E]
        bq_c = sb("bq_c", [128, GROUPS], F32)
        bk_c = sb("bk_c", [128, KT], F32)
        bv_r = sb("bv_r", [128, D], F32)
        bv_t = sb("bv_t", [T, D], F32)
        gates = sb("gates", [128, 4], F32)
        tanhs = sb("tanhs", [128, 4], F32)

        x_in = sb("x_in", [T, D], F32)
        ctx_f = sb("ctx_f", [128, KT, C], F32)
        ctx_s = sb("ctx_s", [128, 2, KT, C], F16)
        keep = [sb(f"keep{i}", [T, C], F32) for i in range(2)]
        bns = sb("bns", [T, 6], F32)
        mv = sb("mv", [T, 2], F32)
        var = sb("var", [T, 1], F32)
        rstd = sb("rstd", [T, 1], F32)
        xn = sb("xn", [T, D], F32)
        xT = sb("xT", [128, 2, KT, T], F16)
        q_f = sb("q_f", [128, GROUPS * T], F32)
        q_s = sb("q_s", [128, 2, GROUPS * T], F16)
        q_masked = [sb(f"q_masked{i}", [128, 2, 4, GROUPS * T], F16) for i in range(2)]
        k_s = sb("k_s", [128, 2, 2, C], F16)
        k_stack = [sb(f"k_stack{i}", [128, GROUPS, C], F16) for i in range(2)]
        v_s = [sb(f"v_s{i}", [128, NB0, H, 2, D0], F16) for i in range(2)]

        RING = 4
        prob = sb("prob", [T, RING, C], F32)
        top = sb("top", [T, RING], F32)
        sums = [sb(f"sums{i}", [T, H], F32) for i in range(2)]
        pT = sb("pT", [128, RING, 2, NB0, 128], F16)

        x_res = sb("x_res", [T, D], F32)
        o_lo = sb("o_lo", [T, H, D0], F32)
        rsum = sb("rsum", [T, H], F32)
        rsum_t = sb("rsum_t", [T, H], F32)
        x_b = sb("x_b", [T, D], F32)
        o_f = sb("o_f", [T, H, D0], F32)
        o_n = sb("o_n", [T, H, D0], F32)
        x1 = sb("x1", [T, D], F32)
        bns1 = sb("bns1", [T, 6], F32)
        mv1 = sb("mv1", [T, 2], F32)
        var1 = sb("var1", [T, 1], F32)
        rstd1 = sb("rstd1", [T, 1], F32)
        xn1 = sb("xn1", [T, D], F32)
        x1T = sb("x1T", [128, 2, KT, T], F16)
        logit = sb("logit", [T, E], F32)
        best = sb("best", [T, 8], F32)
        place = sb("place", [T, 8], U32)
        place_f = sb("place_f", [T, 8], F32)
        gap = sb("gap", [T, 1], F32)
        ratio = sb("ratio", [T, 1], F32)
        norm = sb("norm", [T, 1], F32)
        share = sb("share", [T, 1], F32)
        w_top = sb("w_top", [T, 2], F32)
        picked = sb("picked", [T, 2, E], F32)
        cw = sb("cw", [T, 128], F32)
        cwT = sb("cwT", [128, 2, T], F16)
        acc = sb("acc", [T, D], F32)

        ps_s = [bank(f"ps_s{i}") for i in range(2)]
        ps_t = [bank(f"ps_t{i}") for i in range(2)]
        ps_o = bank("ps_o")
        ps_p = [bank(f"ps_p{i}") for i in range(3)]

        s_setup = sem("setup")
        s_const = sem("const")
        s_wk = sem("wk")
        s_wq = sem("wq")
        s_wv = sem("wv")
        s_wload = sem("wload")
        s_nload = sem("nload")
        s_nhi = sem("nhi")
        s_nlo = sem("nlo")
        s_bvt = sem("bvt")
        s_xb = sem("xb")
        s_zero = sem("zero")
        s_zq = sem("zq")
        s_besplit = sem("besplit")
        s_whi = sem("whi")
        s_wlo = sem("wlo")
        s_wehi = sem("wehi")
        s_welo = sem("welo")
        s_tanh = sem("tanh")
        s_xload = sem("xload")
        s_cload = sem("cload")
        s_mload = sem("mload")
        s_rload = sem("rload")
        s_keep = sem("keep")
        s_csplit = sem("csplit")
        s_stats = sem("stats")
        s_var = sem("var")
        s_rstd = sem("rstd")
        s_xn = sem("xn")
        s_item = sem("item")
        s_ihi = sem("ihi")
        s_ifree = sem("ifree")
        s_qhi = sem("qhi")
        s_qlo = sem("qlo")
        s_qmask = sem("qmask")
        s_kstack = sem("kstack")
        s_score = sem("score")
        s_max = sem("max")
        s_exp = sem("exp")
        s_tr = sem("tr")
        s_phi = sem("phi")
        s_plo = sem("plo")
        s_pv = sem("pv")
        s_olo = sem("olo")
        s_rsum = sem("rsum")
        s_oread = sem("oread")
        s_on = sem("on")
        s_rsumt = sem("rsumt")
        s_x1 = sem("x1")
        s_stats1 = sem("stats1")
        s_var1 = sem("var1")
        s_rstd1 = sem("rstd1")
        s_xn1 = sem("xn1")
        s_ditem = sem("ditem")
        s_dhi = sem("dhi")
        s_dfree = sem("dfree")
        s_route = sem("route")
        s_ratio = sem("ratio")
        s_acc = sem("acc")
        s_store = sem("store")

        PI = 7
        P_K, P_XT, P_Q, P_V = 0, 2, 3, 4
        NSETUP = 16 * 4
        QMASK = 16 * 8
        DI = 8
        D_XT, D_GATE, D_CWT, D_PAIRS, D_BIAS = 0, 1, 3, (2, 4, 5, 6), 7
        ROUTE = 9
        PSLOT = {0: [P_K], 1: [P_K + 1], 2: [P_XT], 4: [P_Q], 5: [P_V], 6: [P_V + 1], 7: [P_V + 2]}
        DSLOT = {7: [D_XT], 8: [D_GATE], 10: [D_PAIRS[0]], 12: [D_CWT, D_PAIRS[1]], 13: [D_PAIRS[2]],
                 14: [D_PAIRS[3], D_BIAS]}
        WPARTS = ((512, 768), (0, 512), (768, 1024 + E))

        def heads(s, lag, b, par):
            h = s - lag
            return (b, par, h) if h >= 0 else (b - 1, 1 - par, h + H)

        ps_i = (ps_p[0], ps_p[1], ps_p[2])
        ps_d = (ps_p[1], ps_p[2], ps_p[0])

        block = ctx.enter_context(nc.Block())

        @block.sync
        def _(sp):
            sp.dma_start(ctx_f[:, :, :], ctxT[0]).then_inc(s_cload, 16)
            sp.dma_start(wqkv_f[:, :, 512:768], wk).then_inc(s_wk, 16)
            sp.dma_start(x_in[:, :], x[0]).then_inc(s_xload, 16)
            sp.dma_start(wqkv_f[:, :, 0:512], wq).then_inc(s_wq, 16)
            sp.dma_start(wqkv_f[:, :, 768:1024], wv).then_inc(s_wv, 16)
            sp.dma_start(wqkv_f[:, :, 1024:1024 + E], wg).then_inc(s_wv, 16)
            sp.dma_start(keep[0][:, :], mask[0]).then_inc(s_mload, 16)
            sp.dma_start(bv_r[:, :], bv.partition_broadcast(128)).then_inc(s_setup, 16)
            sp.dma_start(gates[:, 0:2], g_xattn.partition_broadcast(128)).then_inc(s_setup, 16)
            sp.dma_start(gates[:, 2:4], g_ffn.partition_broadcast(128)).then_inc(s_setup, 16)
            sp.wait_ge(s_zero, 1)
            sp.dma_start(be_f[0:E, :], be).then_inc(s_setup, 16)

            settled = (s_zero, 1)

            def load_tokens(c):
                need(sp, s_xn, 1, c, 0, settled)
                sp.dma_start(x_in[:, :], x[c]).then_inc(s_xload, 16)
                need(sp, s_csplit, 2, c, 0, settled)
                sp.dma_start(ctx_f[:, :, :], ctxT[c]).then_inc(s_cload, 16)

            def load_mask(c, par):
                need_all(sp, settled, (s_max, H, c - 1, 0), (s_keep, 1, c, 0))
                sp.dma_start(keep[par][:, :], mask[c]).then_inc(s_mload, 16)

            def load_residual(c):
                need(sp, s_xb, 1, c, 0, settled)
                sp.dma_start(x_res[:, :], x[c]).then_inc(s_rload, 16)

            def stack_keys(c, par):
                need_all(sp, settled, (s_ihi, 6, c, P_K + 2), (s_ifree, PI, c, P_K + 2), (s_score, H, c - 1, 1))
                for a in range(2):
                    for part in (HI, LO):
                        sp.dma_start(k_stack[par][64 * part:64 * part + 64, a::2, :],
                                     k_s[64 * a:64 * a + 64, part, :, :]).then_inc(s_kstack, 16)

            def mask_queries(c, par):
                need_all(sp, settled, (s_qlo, 1, c, 1), (s_score, H, c - 1, 1))
                for m in range(4):
                    for row in (D0 * m, 64 + D0 * m):
                        sp.dma_start(q_masked[par][row:row + D0, :, m, :], q_s[row:row + D0, :, :]).then_inc(s_qmask, 16)

            def store(c):
                need(sp, s_dfree, DI, c, DI, settled)
                sp.dma_start(x2_dram[c], acc[:, :]).then_inc(s_store, 16)

            def body(b, par):
                if ahead(b, 1):
                    load_mask(b + 1, 1 - par)
                if not first(b):
                    load_residual(b - 1)
                if ahead(b, 2):
                    load_tokens(b + 2)
                if ahead(b, 1):
                    stack_keys(b + 1, 1 - par)
                    mask_queries(b + 1, 1 - par)
                if not first(b):
                    store(b - 1)

            load_tokens(1)
            stack_keys(0, 0)
            sp.wait_ge(s_zq, 2)
            mask_queries(0, 0)
            run_batches(sp, body)
            load_residual(B - 1)
            store(B - 1)
            sp.wait_ge(s_store, 16 * B)

        @block.gpsimd
        def _(pool):
            pool.memset(be_f[:, :], 0.0).then_inc(s_zero, 1)
            pool.memset(neg_half[:, :], -0.5).then_inc(s_zero, 1)
            pool.memset(cw[:, :], 0.0).then_inc(s_zero, 1)
            pool.memset(pT[:, :, :, :, T:128], 0.0).then_inc(s_zero, 1)

            settled = (s_zero, 4)

            def split_context(c):
                need_all(pool, settled, (s_cload, 16, c, 16), (s_item, PI, c, 0))
                pool.tensor_copy(ctx_s[:, HI, :, :], ctx_f[:, :, :]).then_inc(s_csplit, 1)
                need(pool, s_csplit, 2, c, 1)
                pool.tensor_tensor(ctx_s[:, LO, :, :], ctx_f[:, :, :], ctx_s[:, HI, :, :], ALU.subtract).then_inc(s_csplit, 1)

            def deviation(c, s_in, s_mid, s_out, stat, mid, out):
                need(pool, s_in, 2, c, 2, settled)
                pool.tensor_scalar(mid[:, :], stat[:, 1:2], 1.0, EPS, ALU.mult, ALU.add).then_inc(s_mid, 1)
                need(pool, s_mid, 1, c, 1)
                pool.tensor_tensor(out[:, :], mid[:, :], neg_half[0:T, :], ALU.pow).then_inc(s_out, 1)

            def deviation_x(c):
                deviation(c, s_stats, s_var, s_rstd, mv, var, rstd)

            def deviation_x1(c):
                deviation(c, s_stats1, s_var1, s_rstd1, mv1, var1, rstd1)

            def mask_bias(c, par):
                need(pool, s_mload, 16, c, 16, settled)
                pool.tensor_scalar(keep[par][:, :], keep[par][:, :], -1.0, 10000.0 / SCALE0, ALU.add, ALU.mult).then_inc(s_keep, 1)

            def split_queries(c):
                need_all(pool, settled, (s_ifree, PI, c, P_Q + 1), (s_qmask, QMASK, c, 0))
                pool.tensor_copy(q_s[:, HI, :], q_f[:, :]).then_inc(s_qhi, 1)
                need(pool, s_qhi, 1, c, 1)
                pool.tensor_tensor(q_s[:, LO, :], q_f[:, :], q_s[:, HI, :], ALU.subtract).then_inc(s_qlo, 1)

            def residual(c):
                need(pool, s_rload, 16, c, 16)
                pool.tensor_tensor(x_b[:, :], x_res[:, :], bv_t[:, :], ALU.add).then_inc(s_xb, 1)
                need(pool, s_rsumt, 1, c, 1)
                need(pool, s_oread, 1, c, 1)
                pool.tensor_tensor(o_n[:, :, :], o_f[:, :, :], rsum_t[:, :].unsqueeze(2).to_broadcast([T, H, D0]), ALU.mult).then_inc(s_on, 1)
                need(pool, s_on, 1, c, 1)
                need(pool, s_xb, 1, c, 1)
                need(pool, s_dfree, DI, c, 0)
                pool.tensor_tensor(x1[:, :], o_n[:, :, :].rearrange("p h d -> p (h d)"), x_b[:, :], ALU.add).then_inc(s_x1, 1)

            def experts_low(n):
                pool.wait_ge(s_wehi, n + 1)
                cols = slice(n * WE, (n + 1) * WE)
                pool.tensor_tensor(we_s[:, LO, :, cols], we_f[:, :, cols], we_s[:, HI, :, cols], ALU.subtract).then_inc(s_welo, 1)

            def next_low(n):
                pool.wait_ge(s_nhi, n + 1)
                cols = slice(n * NEXT, (n + 1) * NEXT)
                pool.tensor_tensor(next_w[:, LO, cols], next_f[:, cols], next_w[:, HI, cols], ALU.subtract).then_inc(s_nlo, 1)

            def body(b, par):
                last = not ahead(b, 1)
                if ahead(b, 1):
                    deviation_x(b + 1)
                if last:
                    for n in range(3):
                        next_low(n)
                if not first(b):
                    residual(b - 1)
                    deviation_x1(b - 1)
                if ahead(b, 1):
                    mask_bias(b + 1, 1 - par)
                    split_queries(b + 1)
                if ahead(b, 2):
                    split_context(b + 2)
                if first(b):
                    for n in range(H // 2):
                        experts_low(n)
                if last:
                    for n in range(3, H):
                        next_low(n)

            split_context(0)
            mask_bias(0, 0)
            deviation_x(0)
            split_queries(0)
            split_context(1)
            pool.wait_ge(s_setup, NSETUP)
            pool.tensor_copy(be_s[:, HI, :], be_f[:, :]).then_inc(s_besplit, 1)
            pool.wait_ge(s_besplit, 1)
            pool.tensor_tensor(be_s[:, LO, :], be_f[:, :], be_s[:, HI, :], ALU.subtract).then_inc(s_besplit, 1)
            pool.wait_ge(s_bvt, 1)
            run_batches(pool, body)
            residual(B - 1)
            deviation_x1(B - 1)

        @block.tensor
        def _(pe):
            def product(out, sta, mov):
                for k in range(KT):
                    for n, (a, m) in enumerate(PASSES):
                        last = pe.matmul(out, sta(a, k), mov(m, k), start=(k == 0 and n == 0),
                                         stop=(k == KT - 1 and n == 2))
                return last

            def pe_wait_weights(c, n):
                if first(c):
                    pe.wait_ge(s_whi, n)
                    pe.wait_ge(s_wlo, n)

            def item(c, par, k):
                ps = ps_i[k % 3]
                if k < 3 and isinstance(c, int) and c < 3:
                    need(pe, s_ifree, PI, c, 0)
                elif k < 3:
                    need(pe, s_dfree, DI, c - 2, k - 2)
                else:
                    need(pe, s_ifree, PI, c, k - 2)
                if k == P_XT:
                    need(pe, s_xn, 1, c, 1)
                    for t in range(KT):
                        last = pe.transpose(ps[:, t * T:(t + 1) * T], xn[:, t * 128:(t + 1) * 128], ident[0:T, 0:T])
                elif P_K <= k < P_Q:
                    j = k - P_K
                    pe_wait_weights(c, 1)
                    need(pe, s_csplit, 2, c, 2)
                    last = product(ps[:, 0:C], lambda a, t: wk_s[:, a, t, j * 128:(j + 1) * 128],
                                   lambda a, t: ctx_s[:, a, t, :])
                elif k == P_Q:
                    pe_wait_weights(c, 2)
                    need(pe, s_ihi, 6, c, P_XT + 1)
                    need(pe, s_ifree, PI, c, P_XT + 1)
                    for g in range(GROUPS):
                        last = product(ps[:, g * T:(g + 1) * T], lambda a, t: wq_s[:, a, t, g, :],
                                       lambda a, t: xT[:, a, t, :])
                else:
                    j = k - P_V
                    pe_wait_weights(c, 3)
                    last = product(ps[0:KB0, 0:D], lambda a, t: ctx_s[:, a, t, j * KB0:(j + 1) * KB0],
                                   lambda a, t: wv_s[:, a, t, :])
                last.then_inc(s_item, 1)

            def ditem(c, k):
                ps = ps_d[k % 3]
                if k >= 3:
                    need(pe, s_dfree, DI, c, k - 2)
                elif ahead(c, 2):
                    need(pe, s_ifree, PI, c + 2, P_V + 1 + k)
                if k == D_XT:
                    need(pe, s_xn1, 1, c, 1)
                    for t in range(KT):
                        last = pe.transpose(ps[:, t * T:(t + 1) * T], xn1[:, t * 128:(t + 1) * 128], ident[0:T, 0:T])
                elif k == D_GATE:
                    need(pe, s_dhi, 2, c, 1)
                    need(pe, s_dfree, DI, c, D_XT + 1)
                    last = product(ps[0:T, 0:E], lambda a, t: x1T[:, a, t, :], lambda a, t: wg_s[:, a, t, :])
                elif k == D_CWT:
                    need(pe, s_route, ROUTE, c, ROUTE)
                    last = pe.transpose(ps[:, 0:T], cw[:, :], ident[0:T, 0:T])
                elif k == D_BIAS:
                    if first(c):
                        pe.wait_ge(s_besplit, 2)
                    need(pe, s_dhi, 2, c, 2)
                    need(pe, s_dfree, DI, c, D_CWT + 1)
                    for n, (a, m) in enumerate(PASSES):
                        last = pe.matmul(ps[0:T, 0:D], cwT[:, a, :], be_s[:, m, :], start=(n == 0), stop=(n == 2))
                else:
                    j = D_PAIRS.index(k)
                    if first(c):
                        pe.wait_ge(s_welo, H // 2)
                    last = product(ps[0:T, :], lambda a, t: x1T[:, a, t, :],
                                   lambda a, t: we_s[:, a, t, j * 512:(j + 1) * 512])
                last.then_inc(s_ditem, 1)

            def scores(b, par, h):
                g, m = h // 4, h % 4
                if h == 0:
                    need(pe, s_qmask, QMASK, b, QMASK)
                    need(pe, s_kstack, 64, b, 64)
                need(pe, s_max, H, b, h - 1)
                for part in (HI, LO):
                    last = pe.matmul(ps_s[h % 2][0:T, 0:C], q_masked[par][:, part, m, g * T:(g + 1) * T],
                                     k_stack[par][:, g, :], start=(part == HI), stop=(part == LO))
                last.then_inc(s_score, 1)

            def transposes(b, h):
                need(pe, s_exp, H, b, h + 1)
                need(pe, s_plo, H, b, h - 1)
                for j in range(NB0):
                    last = pe.transpose(ps_t[h % 2][0:KB0, j * T:(j + 1) * T],
                                        prob[:, h % RING, j * KB0:(j + 1) * KB0], ident[0:T, 0:T])
                last.then_inc(s_tr, 1)

            def values(b, par, h):
                need(pe, s_phi, H, b, h + 1)
                need(pe, s_plo, H, b, h + 1)
                if h == 0:
                    need(pe, s_oread, 1, b, 0)
                    need(pe, s_ihi, 6, b, 6)
                    need(pe, s_ifree, PI, b, PI)
                for j in range(NB0):
                    for part in (HI, LO):
                        last = pe.matmul(ps_o[:, 32 * h:32 * h + 32], pT[0:KB0, h % RING, part, j, :],
                                         v_s[par][0:KB0, j, h, :, :], start=(h == 0 and j == 0 and part == HI),
                                         stop=(j == NB0 - 1 and part == LO), skip_group_check=True)
                last.then_inc(s_pv, 1)

            def drain(b, par):
                for s in range(4):
                    for lag, stage in ((2, transposes), (4, values)):
                        h = H + s - lag
                        if h < H:
                            stage(b, h) if lag == 2 else stage(b, par, h)

            def body(b, par):
                for s in range(H):
                    scores(b, par, s)
                    if not (first(b) and s < 2):
                        c, _, h = heads(s, 2, b, par)
                        transposes(c, h)
                    if s == 5:
                        values(b, par, 0)
                    if s != 4 and not (first(b) and s < 4):
                        values(*heads(s, 4, b, par))
                    if ahead(b, 1):
                        for k in PSLOT.get(s, []):
                            item(b + 1, 1 - par, k)
                    if not first(b):
                        for k in DSLOT.get(s, []):
                            ditem(b - 1, k)

            pe.wait_ge(s_zero, 4)
            for k in range(PI):
                if k == P_XT:
                    pe.wait_ge(s_const, 48)
                item(0, 0, k)
            run_batches(pe, body)
            drain(B - 1, 1)
            for k in range(DI):
                ditem(B - 1, k)

        @block.scalar
        def _(act):
            def item(c, par, k):
                ps = ps_i[k % 3]
                if k == P_Q:
                    return
                need(act, s_item, PI, c, k + 1)
                if k == P_XT:
                    act.activation(xT[:, HI, :, :], ps[:, 0:KT * T].rearrange("p (t n) -> p t n", t=KT), ACT.Copy).then_inc(s_ihi, 1)
                elif k < P_Q:
                    j = k - P_K
                    if j == 0:
                        need(act, s_kstack, 64, c, 0)
                    act.activation(k_s[:, HI, j, :], ps[:, 0:C], ACT.Identity, bias=bk_c[:, j:j + 1]).then_inc(s_ihi, 1)
                else:
                    j = k - P_V
                    need(act, s_pv, H, c - 1, 0)
                    act.activation(v_s[par][0:KB0, j, :, HI, :],
                                   ps[0:KB0, 0:D].rearrange("p (h d) -> p h d", h=H), ACT.Copy).then_inc(s_ihi, 1)

            def ditem(c, k):
                if k == D_XT:
                    need(act, s_ditem, DI, c, 1)
                    act.activation(x1T[:, HI, :, :], ps_d[0][:, 0:KT * T].rearrange("p (t n) -> p t n", t=KT), ACT.Copy).then_inc(s_dhi, 1)
                elif k == D_CWT:
                    need(act, s_ditem, DI, c, D_CWT + 1)
                    act.activation(cwT[:, HI, :], ps_d[D_CWT % 3][:, 0:T], ACT.Copy).then_inc(s_dhi, 1)

            def exps(b, par, h):
                need(act, s_max, H, b, h + 1)
                act.activation(prob[:, h % RING, :], prob[:, h % RING, :], ACT.Exp, bias=top[:, h % RING:h % RING + 1],
                               scale=-1.0, accum_out=sums[par][:, h:h + 1]).then_inc(s_exp, 1)

            def phi(b, h):
                need(act, s_tr, H, b, h + 1)
                need(act, s_pv, H, b, h - RING + 1)
                act.activation(pT[0:KB0, h % RING, HI, :, 0:T],
                               ps_t[h % 2][0:KB0, 0:NB0 * T].rearrange("p (j n) -> p j n", j=NB0), ACT.Copy).then_inc(s_phi, 1)

            def out_lo(c):
                need(act, s_pv, H, c, H)
                act.activation(o_lo[:, :, :], ps_o[0:T, :].rearrange("p (h s d) -> p h s d", h=H, s=2)[:, :, LO, :], ACT.Copy).then_inc(s_olo, 1)

            def experts_high(n):
                act.wait_ge(s_wload, 16)
                act.activation(we_s[:, HI, :, n * WE:(n + 1) * WE], we_f[:, :, n * WE:(n + 1) * WE], ACT.Copy).then_inc(s_wehi, 1)

            def next_high(n):
                act.wait_ge(s_nload, 16)
                act.activation(next_w[:, HI, n * NEXT:(n + 1) * NEXT], next_f[:, n * NEXT:(n + 1) * NEXT], ACT.Copy).then_inc(s_nhi, 1)

            def weigh(c):
                need(act, s_route, ROUTE, c, 4)
                act.activation(ratio[:, :], gap[:, :], ACT.Exp).then_inc(s_ratio, 1)

            def body(b, par):
                for s in range(H):
                    if ahead(b, 1):
                        for k in PSLOT.get(s - 1, []):
                            item(b + 1, 1 - par, k)
                    if not first(b):
                        if s == 4:
                            out_lo(b - 1)
                        if s == 10:
                            weigh(b - 1)
                        for k in DSLOT.get(s - 1, []):
                            ditem(b - 1, k)
                    if first(b) and s >= H // 2:
                        experts_high(s - H // 2)
                    if isinstance(b, int) and b == 1 and s == 0:
                        act.dma_start(next_f[:, :], next_w_dram).then_inc(s_nload, 16)
                    if not ahead(b, 1):
                        next_high(s)
                    if not (first(b) and s < 1):
                        exps(*heads(s, 1, b, par))
                    if not (first(b) and s < 2):
                        c, _, h = heads(s, 2, b, par)
                        phi(c, h)

            act.dma_start(const[:, :], consts).then_inc(s_const, 16)
            act.dma_start(bk_c[:, :], bk).then_inc(s_const, 16)
            act.dma_start(bq_c[:, :], bq).then_inc(s_const, 16)
            for n, (lo, hi) in enumerate(WPARTS):
                act.wait_ge((s_wk, s_wq, s_wv)[n], 16 if n < 2 else 32)
                act.activation(wqkv[:, HI, :, lo:hi], wqkv_f[:, :, lo:hi], ACT.Copy).then_inc(s_whi, 1)
            act.wait_ge(s_const, 48)
            act.wait_ge(s_setup, NSETUP)
            act.activation(tanhs[:, :], gates[:, :], ACT.Tanh).then_inc(s_tanh, 1)
            act.dma_start(we_f[:, :, :], we).then_inc(s_wload, 16)
            for k in range(PI):
                item(0, 0, k)
            run_batches(act, body)
            exps(B - 1, 1, H - 1)
            phi(B - 1, H - 2)
            phi(B - 1, H - 1)
            out_lo(B - 1)
            ditem(B - 1, D_XT)
            weigh(B - 1)
            ditem(B - 1, D_CWT)

        @block.vector
        def _(dve):
            settled = (s_zero, 4)

            def stats_x(c):
                need(dve, s_xload, 16, c, 16)
                dve.bn_stats(bns[:, :], x_in[:, :]).then_inc(s_stats, 1)
                need(dve, s_stats, 2, c, 1, settled)
                dve.bn_aggr(mv[:, :], bns[:, :]).then_inc(s_stats, 1)

            def norm_x(c):
                need(dve, s_rstd, 1, c, 1)
                need(dve, s_item, PI, c, 0)
                dve.tensor_scalar(xn[:, :], x_in[:, :], mv[:, 0:1], rstd[:, 0:1], ALU.subtract, ALU.mult).then_inc(s_xn, 1)

            def norm_x1(c):
                need(dve, s_rstd1, 1, c, 1)
                need(dve, s_ditem, DI, c, 0)
                dve.tensor_scalar(xn1[:, :], x1[:, :], mv1[:, 0:1], rstd1[:, 0:1], ALU.subtract, ALU.mult).then_inc(s_xn1, 1)

            def item(c, par, k):
                ps = ps_i[k % 3]
                if k == P_Q:
                    need(dve, s_item, PI, c, k + 1)
                    need(dve, s_qlo, 1, c, 0)
                    dve.tensor_tensor(q_f[:, :].rearrange("p (g n) -> p g n", g=GROUPS),
                                      ps[:, 0:GROUPS * T].rearrange("p (g n) -> p g n", g=GROUPS),
                                      bq_c[:, :].unsqueeze(2).to_broadcast([128, GROUPS, T]), ALU.add).then_inc(s_ifree, 1)
                    return
                need(dve, s_ihi, 6, c, k + 1 if k < P_Q else k)
                if k == P_XT:
                    dve.tensor_tensor(xT[:, LO, :, :], ps[:, 0:KT * T].rearrange("p (t n) -> p t n", t=KT), xT[:, HI, :, :], ALU.subtract).then_inc(s_ifree, 1)
                elif k < P_Q:
                    j = k - P_K
                    dve.scalar_tensor_tensor(k_s[:, LO, j, :], ps[:, 0:C], bk_c[:, j:j + 1], k_s[:, HI, j, :],
                                             ALU.add, ALU.subtract).then_inc(s_ifree, 1)
                else:
                    j = k - P_V
                    dve.tensor_tensor(v_s[par][0:KB0, j, :, LO, :],
                                      ps[0:KB0, 0:D].rearrange("p (h d) -> p h d", h=H),
                                      v_s[par][0:KB0, j, :, HI, :], ALU.subtract).then_inc(s_ifree, 1)

            def maxima(b, par, h):
                need_all(dve, settled, (s_score, H, b, h + 1), (s_tr, H, b, h - RING + 1), *([(s_keep, 1, b, 1)] if h == 0 else []))
                dve.tensor_tensor_reduce(prob[:, h % RING, :], ps_s[h % 2][0:T, 0:C], keep[par][:, :], -SCALE0, 3e38,
                                         ALU.add, ALU.min, top[:, h % RING:h % RING + 1]).then_inc(s_max, 1)

            def plo(b, h):
                need(dve, s_phi, H, b, h + 1)
                dve.tensor_tensor(pT[0:KB0, h % RING, LO, :, 0:T],
                                  ps_t[h % 2][0:KB0, 0:NB0 * T].rearrange("p (j n) -> p j n", j=NB0),
                                  pT[0:KB0, h % RING, HI, :, 0:T], ALU.subtract).then_inc(s_plo, 1)

            def read_out(c, par):
                need(dve, s_exp, H, c, H)
                dve.reciprocal(rsum[:, :], sums[par][:, :]).then_inc(s_rsum, 1)
                need(dve, s_olo, 1, c, 1)
                dve.tensor_tensor(o_f[:, :, :], ps_o[0:T, :].rearrange("p (h s d) -> p h s d", h=H, s=2)[:, :, HI, :],
                                  o_lo[:, :, :], ALU.add).then_inc(s_oread, 1)
                need(dve, s_rsum, 1, c, 1)
                dve.tensor_scalar(rsum_t[:, :], rsum[:, :], tanhs[0:T, 0:1], None, ALU.mult).then_inc(s_rsumt, 1)

            def stats_x1(c):
                need(dve, s_x1, 1, c, 1)
                dve.bn_stats(bns1[:, :], x1[:, :]).then_inc(s_stats1, 1)
                need(dve, s_stats1, 2, c, 1, settled)
                dve.bn_aggr(mv1[:, :], bns1[:, :]).then_inc(s_stats1, 1)

            def ditem(c, k):
                ps = ps_d[k % 3]
                if k == D_XT:
                    need(dve, s_dhi, 2, c, 1)
                    dve.tensor_tensor(x1T[:, LO, :, :], ps[:, 0:KT * T].rearrange("p (t n) -> p t n", t=KT), x1T[:, HI, :, :], ALU.subtract).then_inc(s_dfree, 1)
                elif k == D_GATE:
                    need(dve, s_ditem, DI, c, k + 1)
                    dve.tensor_copy(logit[:, :], ps[0:T, 0:E]).then_inc(s_dfree, 1)
                    need(dve, s_dfree, DI, c, k + 1, settled)
                    dve.max(best[:, :], logit[:, :]).then_inc(s_route, 1)
                    need(dve, s_route, ROUTE, c, 1, settled)
                    dve.max_index(place[:, :], best[:, :], logit[:, :]).then_inc(s_route, 1)
                    need(dve, s_route, ROUTE, c, 2)
                    dve.tensor_copy(place_f[:, :], place[:, :]).then_inc(s_route, 1)
                    dve.tensor_tensor(gap[:, :], best[:, 1:2], best[:, 0:1], ALU.subtract).then_inc(s_route, 1)
                elif k == D_CWT:
                    need(dve, s_dhi, 2, c, 2)
                    dve.tensor_tensor(cwT[:, LO, :], ps[:, 0:T], cwT[:, HI, :], ALU.subtract).then_inc(s_dfree, 1)
                elif k == D_BIAS:
                    need(dve, s_ditem, DI, c, k + 1)
                    need(dve, s_dfree, DI, c, k)
                    dve.tensor_tensor(acc[:, :], ps[0:T, 0:D], acc[:, :], ALU.add).then_inc(s_dfree, 1)
                else:
                    j = D_PAIRS.index(k)
                    need(dve, s_ditem, DI, c, k + 1)
                    if j == 0:
                        need(dve, s_route, ROUTE, c, ROUTE)
                        need(dve, s_store, 16, c, 0)
                    need(dve, s_dfree, DI, c, k)
                    dve.scalar_tensor_tensor(acc[:, :], ps[0:T, 0:D], cw[:, 2 * j:2 * j + 1], (acc if j else x1)[:, :],
                                             ALU.mult, ALU.add).then_inc(s_acc, 1)
                    need(dve, s_acc, E // 2, c, j + 1)
                    dve.scalar_tensor_tensor(acc[:, :], ps[0:T, D:2 * D], cw[:, 2 * j + 1:2 * j + 2], acc[:, :],
                                             ALU.mult, ALU.add).then_inc(s_dfree, 1)

            def combine_weights(c):
                need(dve, s_ratio, 1, c, 1)
                dve.tensor_scalar(norm[:, :], ratio[:, :], 1.0, None, ALU.add).then_inc(s_route, 1)
                need(dve, s_route, ROUTE, c, 5)
                dve.reciprocal(share[:, :], norm[:, :]).then_inc(s_route, 1)
                need(dve, s_route, ROUTE, c, 6)
                dve.tensor_scalar(w_top[:, 0:1], share[:, :], tanhs[0:T, 2:3], None, ALU.mult)
                dve.tensor_scalar(w_top[:, 1:2], share[:, :], tanhs[0:T, 2:3], ratio[:, 0:1], ALU.mult, ALU.mult).then_inc(s_route, 1)
                need(dve, s_route, ROUTE, c, 7)
                for n in range(2):
                    last = dve.tensor_scalar(picked[:, n, :], const[0:T, IOTA:IOTA + E], place_f[:, n:n + 1], w_top[:, n:n + 1],
                                             ALU.is_equal, ALU.mult)
                last.then_inc(s_route, 1)
                need(dve, s_route, ROUTE, c, 8)
                dve.tensor_tensor(cw[:, 0:E], picked[:, 0, :], picked[:, 1, :], ALU.add).then_inc(s_route, 1)

            def body(b, par):
                for s in range(H):
                    if not first(b) and s == 8:
                        ditem(b - 1, D_XT)
                    maxima(b, par, s)
                    if ahead(b, 1):
                        if s == 0:
                            stats_x(b + 1)
                        if s == 1:
                            norm_x(b + 1)
                        for k in PSLOT.get(s - 1, []):
                            item(b + 1, 1 - par, k)
                    if not first(b):
                        if s == 4:
                            read_out(b - 1, 1 - par)
                        if s == 10:
                            combine_weights(b - 1)
                        for k in DSLOT.get(s - 1, []):
                            if k != D_XT:
                                ditem(b - 1, k)
                    if not (first(b) and s < 2):
                        c, _, h = heads(s, 2, b, par)
                        plo(c, h)
                    if not first(b):
                        if s == 5:
                            stats_x1(b - 1)
                        if s == 6:
                            norm_x1(b - 1)

            for i in range(2):
                dve.memset(q_masked[i][:, :, :, :], 0.0).then_inc(s_zq, 1)
            dve.wait_ge(s_zero, 4)
            for n, (lo, hi) in enumerate(WPARTS):
                dve.wait_ge(s_whi, n + 1)
                dve.tensor_tensor(wqkv[:, LO, :, lo:hi], wqkv_f[:, :, lo:hi], wqkv[:, HI, :, lo:hi], ALU.subtract).then_inc(s_wlo, 1)
                if n == 0:
                    stats_x(0)
                if n == 1:
                    norm_x(0)
            dve.wait_ge(s_const, 48)
            dve.wait_ge(s_setup, NSETUP)
            dve.wait_ge(s_tanh, 1)
            dve.tensor_scalar(bv_t[:, :], bv_r[0:T, :], tanhs[0:T, 0:1], None, ALU.mult).then_inc(s_bvt, 1)
            for k in range(PI):
                item(0, 0, k)
            run_batches(dve, body)
            plo(B - 1, H - 2)
            plo(B - 1, H - 1)
            read_out(B - 1, 1)
            stats_x1(B - 1)
            norm_x1(B - 1)
            ditem(B - 1, D_XT)
            ditem(B - 1, D_GATE)
            combine_weights(B - 1)
            for k in range(D_PAIRS[0], DI):
                ditem(B - 1, k)

D1 = 64
INNER = H * D1
IT = INNER // 128
NK = C + T
NKP = 488
WKV, WQ, WOUT = KT * 2 * INNER, KT * INNER, IT * D
KB1, NB1 = 122, 4
SCALE1 = D1 ** -0.5
MASKED = 1e30

def phase_attention_large_heads(nc, ctx_tok, mask, g_xattn, g_ffn, g1, b1, g2, b2, wr, br, consts, w_s,
                                x2_dram, x3_dram, x3T_dram, cw_dram):
    with ExitStack() as ctx:
        sb = lambda name, shape, dt: ctx.enter_context(nc.sbuf_tensor("b_" + name, shape, dt))
        sem = lambda name: ctx.enter_context(nc.semaphore("b_" + name))
        bank = lambda name: ctx.enter_context(nc.psum_tensor("b_" + name, [128, 512], F32))

        const = sb("const", [128, NCONST], F32)
        ident = const[:, IDENT:IDENT + 128]
        neg_half = sb("neg_half", [128, 4], F32)
        wkv_s = w_s[:, :, 0:WKV].rearrange("p s (k n) -> p s k n", k=KT)
        wq_s = w_s[:, :, WKV:WKV + WQ].rearrange("p s (k n) -> p s k n", k=KT)
        wout_s = w_s[:, :, WKV + WQ:].rearrange("p s (k n) -> p s k n", k=IT)
        wr_f = sb("wr_f", [128, KT, E], F32)
        wr_s = sb("wr_s", [128, 2, KT, E], F16)
        br_r = sb("br_r", [128, E], F32)
        affine = sb("affine", [128, 4, KT], F32)
        gates = sb("gates", [128, 4], F32)
        tanhs = sb("tanhs", [128, 4], F32)

        ctx_t = sb("ctx_t", [KB0, NB0, D], F32)
        x2_t = sb("x2_t", [T, D], F32)
        bns = sb("bns", [128, 4, 6], F32)
        mv = sb("mv", [128, 4, 2], F32)
        var = sb("var", [128, 4], F32)
        rstd = sb("rstd", [128, 4], F32)
        ctx_n = sb("ctx_n", [KB0, NB0, D], F32)
        x2_n = sb("x2_n", [T, D], F32)
        tok_f = sb("tok_f", [128, KT, NK], F32)
        tok_s = [sb(f"tok_s{i}", [128, 2, KT, NKP], F16) for i in range(2)]
        keep_u = sb("keep_u", [T, C], U8)
        keep = [sb(f"keep{i}", [T, NK], F32) for i in range(2)]

        q_s = sb("q_s", [128, 2, IT, T], F16)
        q_dup = [sb(f"q_dup{i}", [128, 2, H, T], F16) for i in range(2)]
        k_s = sb("k_s", [128, 2, IT, NK], F16)
        k_stack = [sb(f"k_stack{i}", [128, H, NK], F16) for i in range(2)]
        v_s = [sb(f"v_s{i}", [128, 2, NB1, INNER], F16) for i in range(2)]

        RING = 4
        prob = sb("prob", [T, RING, NKP], F32)
        top = sb("top", [T, RING], F32)
        sums = [sb(f"sums{i}", [T, H], F32) for i in range(2)]
        pT = sb("pT", [128, 2, 2, NB1, 128], F16)

        x_res = sb("x_res", [T, D], F32)
        rsum = sb("rsum", [T, H], F32)
        o_n = sb("o_n", [T, H, D1], F32)
        oT = sb("oT", [128, 2, IT, T], F16)
        x3 = sb("x3", [T, D], F32)
        bns3 = sb("bns3", [T, 6], F32)
        mv3 = sb("mv3", [T, 2], F32)
        var3 = sb("var3", [T, 1], F32)
        rstd3 = sb("rstd3", [T, 1], F32)
        xn3 = sb("xn3", [T, D], F32)
        x3T = sb("x3T", [128, 2, KT, T], F16)
        logit = sb("logit", [T, E], F32)
        best = sb("best", [T, 8], F32)
        place = sb("place", [T, 8], U32)
        place_f = sb("place_f", [T, 8], F32)
        gap = sb("gap", [T, 1], F32)
        ratio = sb("ratio", [T, 1], F32)
        norm = sb("norm", [T, 1], F32)
        share = sb("share", [T, 1], F32)
        w_top = sb("w_top", [T, 2], F32)
        picked = sb("picked", [T, 2, E], F32)
        cw = sb("cw", [T, E], F32)

        ps_s = [bank(f"ps_s{i}") for i in range(2)]
        ps_t = [bank(f"ps_t{i}") for i in range(2)]
        ps_o = [bank(f"ps_o{i}") for i in range(2)]
        ps_p = [bank(f"ps_p{i}") for i in range(2)]
        ps_x = ps_o[1]

        s_setup = sem("setup")
        s_zero = sem("zero")
        s_wsplit = sem("wsplit")
        s_tanh = sem("tanh")
        s_cload = sem("cload")
        s_xload = sem("xload")
        s_mload = sem("mload")
        s_rload = sem("rload")
        s_keep = sem("keep")
        s_stats = sem("stats")
        s_var = sem("var")
        s_rstd = sem("rstd")
        s_norm = sem("norm")
        s_nitem = sem("nitem")
        s_nfree = sem("nfree")
        s_tsplit = sem("tsplit")
        s_item = sem("item")
        s_ihi = sem("ihi")
        s_ifree = sem("ifree")
        s_kstack = sem("kstack")
        s_qdup = sem("qdup")
        s_score = sem("score")
        s_max = sem("max")
        s_exp = sem("exp")
        s_tr = sem("tr")
        s_phi = sem("phi")
        s_plo = sem("plo")
        s_pv = sem("pv")
        s_rsum = sem("rsum")
        s_oread = sem("oread")
        s_hitem = sem("hitem")
        s_hhi = sem("hhi")
        s_hfree = sem("hfree")
        s_stats3 = sem("stats3")
        s_var3 = sem("var3")
        s_rstd3 = sem("rstd3")
        s_xn3 = sem("xn3")
        s_route = sem("route")
        s_ratio = sem("ratio")
        s_store = sem("store")

        NSETUP = 16 * 11
        P_K, P_Q, P_V, PI = 0, IT, IT + 2, IT + 2 + 2 * NB1
        N_C, N_L, NI = 0, KT, KT + 1
        H_T, H_O, H_X, H_G, HI_ = 0, 2, 3, 4, 5
        ROUTE = 9
        PSLOT, k = {}, 0
        for s, n in enumerate([2, 2, 2, 2, 1, 1, 0, 1, 1, 1, 1, 1, 1, 1, 1]):
            PSLOT[s] = list(range(k, k + n))
            k += n
        assert k == PI
        XSLOT = {3: ("n", 0), 4: ("h", 0), 5: ("h", 1), 6: ("h", 2), 7: ("n", 1), 8: ("h", 3), 9: ("h", 4), 10: ("n", 2)}

        def lent_before(s):
            n = [XSLOT[t][0] for t in XSLOT if t < s]
            return n.count("h"), n.count("n")

        def behind(s, lag, b, par):
            h = s - lag
            return (b, par, h) if h >= 0 else (b - 1, 1 - par, h + H)

        block = ctx.enter_context(nc.Block())

        @block.sync
        def _(sp):
            settled = (s_zero, 8)

            def load(c):
                need(sp, s_norm, 2, c, 0, settled)
                sp.dma_start(ctx_t[:, :, :], ctx_tok[c].rearrange("(j p) d -> p j d", p=KB0)).then_inc(s_cload, 16)
                sp.dma_start(x2_t[:, :], x2_dram[c]).then_inc(s_xload, 16)
                need(sp, s_keep, 1, c, 0, settled)
                sp.dma_start(keep_u[:, :], mask[c].partition_broadcast(T)).then_inc(s_mload, 16)

            def stack(c, par):
                need_all(sp, settled, (s_ihi, PI, c, P_Q), (s_ifree, PI, c, P_Q), (s_score, H, c - 1, 1))
                for a in range(2):
                    for part in (HI, LO):
                        src = k_s[64 * a:64 * a + 64, part, :, :]
                        rows = part if a == 0 else 1 - part
                        sp.dma_start(k_stack[par][64 * rows:64 * rows + 64, a::2, :], src).then_inc(s_kstack, 16)
                need_all(sp, settled, (s_ihi, PI, c, P_V), (s_ifree, PI, c, P_V))
                for a in range(2):
                    for rows in range(2):
                        for part in (HI, LO):
                            sp.dma_start(q_dup[par][64 * rows:64 * rows + 64, part, a::2, :],
                                         q_s[64 * a:64 * a + 64, part, :, :]).then_inc(s_qdup, 16)

            def residual(c):
                need(sp, s_hfree, HI_, c, 0, settled)
                sp.dma_start(x_res[:, :], x2_dram[c]).then_inc(s_rload, 16)

            def store(c):
                need(sp, s_hfree, HI_, c, H_X + 1, settled)
                sp.dma_start(x3_dram[c], x3[:, :]).then_inc(s_store, 16)
                sp.dma_start(x3T_dram[c], x3T[:, :, :, :]).then_inc(s_store, 16)
                need(sp, s_route, ROUTE, c, ROUTE, settled)
                sp.dma_start(cw_dram[c], cw[:, :]).then_inc(s_store, 16)

            def body(b, par):
                if not first(b):
                    residual(b - 1)
                if ahead(b, 2):
                    load(b + 2)
                if ahead(b, 1):
                    stack(b + 1, 1 - par)
                if not first(b):
                    store(b - 1)

            load(0)
            sp.dma_start(const[:, :], consts).then_inc(s_setup, 16)
            for n, v in enumerate((g1, b1, g2, b2)):
                sp.dma_start(affine[:, n, :], v).then_inc(s_setup, 16)
            sp.dma_start(wr_f[:, :, :], wr).then_inc(s_setup, 16)
            sp.dma_start(br_r[:, :], br.partition_broadcast(128)).then_inc(s_setup, 16)
            sp.dma_start(gates[:, 0:2], g_xattn.partition_broadcast(128)).then_inc(s_setup, 16)
            sp.dma_start(gates[:, 2:4], g_ffn.partition_broadcast(128)).then_inc(s_setup, 16)

            load(1)
            stack(0, 0)
            run_batches(sp, body)
            residual(B - 1)
            store(B - 1)
            sp.wait_ge(s_store, 3 * 16 * B)

        @block.gpsimd
        def _(pool):
            pool.memset(neg_half[:, :], -0.5).then_inc(s_zero, 1)
            pool.memset(mv[:, :, :], 0.0).then_inc(s_zero, 1)
            for i in range(2):
                pool.memset(tok_s[i][:, :, :, NK:NKP], 0.0).then_inc(s_zero, 1)
                pool.memset(keep[i][:, C:NK], 0.0).then_inc(s_zero, 1)
            pool.memset(prob[:, :, NK:NKP], 0.0).then_inc(s_zero, 1)
            pool.memset(pT[:, :, :, :, T:128], 0.0).then_inc(s_zero, 1)

            settled = (s_zero, 8)

            def deviation(c):
                need(pool, s_stats, 8, c, 8, settled)
                pool.tensor_scalar(var[:, 0:NB0], mv[:, 0:NB0, 1], 1.0, EPS, ALU.mult, ALU.add).then_inc(s_var, 1)
                pool.tensor_scalar(var[:, NB0:NB0 + 1], mv[:, NB0:NB0 + 1, 1], 1.0 + EPS, EPS * EPS, ALU.mult, ALU.add).then_inc(s_var, 1)
                need(pool, s_var, 2, c, 2)
                pool.tensor_tensor(rstd[:, :], var[:, :], neg_half[:, :], ALU.pow).then_inc(s_rstd, 1)

            def deviation3(c):
                need(pool, s_stats3, 2, c, 2, settled)
                pool.tensor_scalar(var3[:, :], mv3[:, 1:2], 1.0, EPS, ALU.mult, ALU.add).then_inc(s_var3, 1)
                need(pool, s_var3, 1, c, 1)
                pool.tensor_tensor(rstd3[:, :], var3[:, :], neg_half[0:T, 0:1], ALU.pow).then_inc(s_rstd3, 1)

            def mask_bias(c, par):
                need_all(pool, settled, (s_mload, 16, c, 16), (s_max, H, c - 1, 0))
                pool.tensor_scalar(keep[par][:, 0:C], keep_u[:, :], -1.0, MASKED, ALU.add, ALU.mult).then_inc(s_keep, 1)

            def split_tokens(c, par):
                for k in range(KT):
                    need_all(pool, settled, (s_nfree, NI, c, k + 1), *([(s_item, PI, c - 1, 0)] if k == 0 else []))
                    pool.tensor_copy(tok_s[par][:, HI, k, 0:C], tok_f[:, k, 0:C]).then_inc(s_tsplit, 1)
                    need(pool, s_tsplit, 6, c, 2 * k + 1)
                    pool.tensor_tensor(tok_s[par][:, LO, k, 0:C], tok_f[:, k, 0:C], tok_s[par][:, HI, k, 0:C], ALU.subtract).then_inc(s_tsplit, 1)
                need(pool, s_nfree, NI, c, NI, settled)
                pool.tensor_copy(tok_s[par][:, HI, :, C:NK], tok_f[:, :, C:NK]).then_inc(s_tsplit, 1)
                need(pool, s_tsplit, 6, c, 5)
                pool.tensor_tensor(tok_s[par][:, LO, :, C:NK], tok_f[:, :, C:NK], tok_s[par][:, HI, :, C:NK], ALU.subtract).then_inc(s_tsplit, 1)

            def body(b, par):
                if ahead(b, 2):
                    deviation(b + 2)
                if not first(b):
                    deviation3(b - 1)
                if ahead(b, 2):
                    split_tokens(b + 2, par)
                    mask_bias(b + 2, par)

            pool.wait_ge(s_zero, 8)
            deviation(0)
            mask_bias(0, 0)
            split_tokens(0, 0)
            deviation(1)
            mask_bias(1, 1)
            split_tokens(1, 1)
            pool.wait_ge(s_setup, 16 * 9)
            pool.tensor_copy(wr_s[:, HI, :, :], wr_f[:, :, :]).then_inc(s_wsplit, 1)
            pool.wait_ge(s_wsplit, 1)
            pool.tensor_tensor(wr_s[:, LO, :, :], wr_f[:, :, :], wr_s[:, HI, :, :], ALU.subtract).then_inc(s_wsplit, 1)
            run_batches(pool, body)
            deviation3(B - 1)

        @block.tensor
        def _(pe):
            def product(out, sta, mov, tiles=KT):
                for k in range(tiles):
                    for n, (a, m) in enumerate(PASSES):
                        last = pe.matmul(out, sta(a, k), mov(m, k), start=(k == 0 and n == 0),
                                         stop=(k == tiles - 1 and n == 2))
                return last

            def item(c, par, k):
                ps = ps_p[k % 2]
                need(pe, s_ifree, PI, c, max(k - 1, 0))
                if k == 0:
                    need(pe, s_tsplit, 6, c, 6)
                tok = tok_s[par]
                if k < P_Q:
                    last = product(ps[:, 0:NK], lambda a, t: wkv_s[:, a, t, k * 128:(k + 1) * 128],
                                   lambda a, t: tok[:, a, t, 0:NK])
                elif k < P_V:
                    for n in range(4):
                        j = 4 * (k - P_Q) + n
                        last = product(ps[:, n * T:(n + 1) * T], lambda a, t: wq_s[:, a, t, j * 128:(j + 1) * 128],
                                       lambda a, t: tok[:, a, t, C:NK])
                else:
                    j, half = (k - P_V) // 2, (k - P_V) % 2
                    last = product(ps[0:KB1, :], lambda a, t: tok[:, a, t, j * KB1:(j + 1) * KB1],
                                   lambda a, t: wkv_s[:, a, t, INNER + half * 512:INNER + (half + 1) * 512])
                last.then_inc(s_item, 1)

            def nitem(c, k):
                if k == 0:
                    need(pe, s_norm, 2, c, 2)
                if k < N_L:
                    for j in range(NB0):
                        last = pe.transpose(ps_x[:, j * KB0:(j + 1) * KB0], ctx_n[:, j, k * 128:(k + 1) * 128], ident[0:KB0, 0:KB0])
                else:
                    for t in range(KT):
                        last = pe.transpose(ps_x[:, t * T:(t + 1) * T], x2_n[:, t * 128:(t + 1) * 128], ident[0:T, 0:T])
                last.then_inc(s_nitem, 1)

            def hitem(c, k):
                if k < H_O:
                    for n in range(4):
                        j = 4 * k + n
                        last = pe.transpose(ps_x[:, n * T:(n + 1) * T], o_n[:, 2 * j:2 * j + 2, :].rearrange("p h d -> p (h d)"), ident[0:T, 0:T])
                elif k == H_O:
                    need(pe, s_hhi, 3, c, 2)
                    need(pe, s_hfree, HI_, c, 2)
                    last = product(ps_x[0:T, 0:D], lambda a, t: oT[:, a, t, :], lambda a, t: wout_s[:, a, t, :], IT)
                elif k == H_X:
                    need(pe, s_xn3, 1, c, 1)
                    for t in range(KT):
                        last = pe.transpose(ps_x[:, t * T:(t + 1) * T], xn3[:, t * 128:(t + 1) * 128], ident[0:T, 0:T])
                else:
                    need(pe, s_hhi, 3, c, 3)
                    need(pe, s_hfree, HI_, c, H_X + 1)
                    last = product(ps_x[0:T, 0:E], lambda a, t: x3T[:, a, t, :], lambda a, t: wr_s[:, a, t, :])
                last.then_inc(s_hitem, 1)

            def lend(b, s):
                kind, k = XSLOT[s]
                if kind == "h" and first(b) or kind == "n" and not ahead(b, 2):
                    return
                nh, nn = lent_before(s)
                need(pe, s_oread, 2, b, 0)
                if not first(b):
                    need(pe, s_hfree, HI_, b - 1, nh)
                if ahead(b, 2):
                    need(pe, s_nfree, NI, b + 2, nn)
                if kind == "h":
                    hitem(b - 1, k)
                else:
                    nitem(b + 2, k)

            def scores(b, par, h):
                if h == 0:
                    need(pe, s_qdup, 128, b, 128)
                    need(pe, s_kstack, 64, b, 64)
                need(pe, s_max, H, b, h - 1)
                for part in (HI, LO):
                    last = pe.matmul(ps_s[h % 2][0:T, 0:NK], q_dup[par][:, part, h, :], k_stack[par][:, h, :],
                                     start=(part == HI), stop=(part == LO))
                last.then_inc(s_score, 1)

            def transposes(b, h):
                need(pe, s_exp, H, b, h + 1)
                need(pe, s_plo, H, b, h - 1)
                for j in range(NB1):
                    last = pe.transpose(ps_t[h % 2][0:KB1, j * T:(j + 1) * T],
                                        prob[:, h % RING, j * KB1:(j + 1) * KB1], ident[0:T, 0:T])
                last.then_inc(s_tr, 1)

            def values(b, par, h):
                need(pe, s_phi, H, b, h + 1)
                need(pe, s_plo, H, b, h + 1)
                if h == 0:
                    need(pe, s_oread, 2, b, 0)
                    need(pe, s_ihi, PI, b, PI)
                    need(pe, s_ifree, PI, b, PI)
                if h == H // 2:
                    if not first(b):
                        need(pe, s_hfree, HI_, b - 1, HI_)
                    if ahead(b, 2):
                        need(pe, s_nfree, NI, b + 2, NI)
                col = (h % 8) * D1
                for j in range(NB1):
                    for n, (a, m) in enumerate(PASSES):
                        last = pe.matmul(ps_o[h // 8][:, col:col + D1], pT[0:KB1, h % 2, a, j, :],
                                         v_s[par][0:KB1, m, j, h * D1:(h + 1) * D1],
                                         start=(h % 8 == 0 and j == 0 and n == 0),
                                         stop=(j == NB1 - 1 and n == 2), skip_group_check=True)
                last.then_inc(s_pv, 1)

            def body(b, par):
                for s in range(H):
                    scores(b, par, s)
                    if not (first(b) and s < 2):
                        c, _, h = behind(s, 2, b, par)
                        transposes(c, h)
                    if ahead(b, 1):
                        for k in PSLOT.get(s, []):
                            item(b + 1, 1 - par, k)
                    if not (first(b) and s < 3):
                        values(*behind(s, 3, b, par))
                    if s in XSLOT:
                        lend(b, s)

            pe.wait_ge(s_setup, 16 * 9)
            pe.wait_ge(s_zero, 8)
            for c, items in ((0, range(4)), (1, range(4, PI))):
                for k in range(NI):
                    need(pe, s_nfree, NI, c, k)
                    nitem(c, k)
                for k in items:
                    item(0, 0, k)
            pe.wait_ge(s_wsplit, 2)
            run_batches(pe, body)
            transposes(B - 1, H - 2)
            values(B - 1, 1, H - 3)
            transposes(B - 1, H - 1)
            values(B - 1, 1, H - 2)
            values(B - 1, 1, H - 1)
            need(pe, s_oread, 2, B, 0)
            for k in range(HI_):
                need(pe, s_hfree, HI_, B - 1, k)
                hitem(B - 1, k)

        @block.scalar
        def _(act):
            def item(c, par, k):
                ps = ps_p[k % 2]
                need(act, s_item, PI, c, k + 1)
                if k < P_Q:
                    if k == 0:
                        need(act, s_kstack, 64, c, 0)
                    act.activation(k_s[:, HI, k, :], ps[:, 0:NK], ACT.Copy).then_inc(s_ihi, 1)
                elif k < P_V:
                    j = 4 * (k - P_Q)
                    if j == 0:
                        need(act, s_qdup, 128, c, 0)
                    act.activation(q_s[:, HI, j:j + 4, :], ps[:, 0:4 * T].rearrange("p (j n) -> p j n", j=4), ACT.Copy).then_inc(s_ihi, 1)
                else:
                    j, half = (k - P_V) // 2, (k - P_V) % 2
                    need(act, s_pv, H, c - 1, 0)
                    act.activation(v_s[par][0:KB1, HI, j, half * 512:(half + 1) * 512], ps[0:KB1, :], ACT.Copy).then_inc(s_ihi, 1)

            def hitem(c, k):
                if k < H_O:
                    need(act, s_hitem, HI_, c, k + 1)
                    act.activation(oT[:, HI, 4 * k:4 * k + 4, :], ps_x[:, 0:4 * T].rearrange("p (j n) -> p j n", j=4), ACT.Copy).then_inc(s_hhi, 1)
                elif k == H_X:
                    need(act, s_hitem, HI_, c, k + 1)
                    need(act, s_store, 48, c, 0)
                    act.activation(x3T[:, HI, :, :], ps_x[:, 0:KT * T].rearrange("p (t n) -> p t n", t=KT), ACT.Copy).then_inc(s_hhi, 1)

            def exps(b, par, h):
                need(act, s_max, H, b, h + 1)
                act.activation(prob[:, h % RING, 0:NK], prob[:, h % RING, 0:NK], ACT.Exp, bias=top[:, h % RING:h % RING + 1],
                               scale=-1.0, accum_out=sums[par][:, h:h + 1]).then_inc(s_exp, 1)

            def phi(b, h):
                need(act, s_tr, H, b, h + 1)
                need(act, s_pv, H, b, h - 1)
                act.activation(pT[0:KB1, h % 2, HI, :, 0:T],
                               ps_t[h % 2][0:KB1, 0:NB1 * T].rearrange("p (j n) -> p j n", j=NB1), ACT.Copy).then_inc(s_phi, 1)

            def weigh(c):
                need(act, s_route, ROUTE, c, 4)
                act.activation(ratio[:, :], gap[:, :], ACT.Exp).then_inc(s_ratio, 1)

            def body(b, par):
                for s in range(H):
                    if ahead(b, 1):
                        for k in PSLOT.get(s - 1, []):
                            item(b + 1, 1 - par, k)
                    if not first(b):
                        kind, k = XSLOT.get(s - 1, ("", 0))
                        if kind == "h":
                            hitem(b - 1, k)
                        if s == 11:
                            weigh(b - 1)
                    if not (first(b) and s < 1):
                        exps(*behind(s, 1, b, par))
                    if not (first(b) and s < 2):
                        c, _, h = behind(s, 2, b, par)
                        phi(c, h)

            act.wait_ge(s_setup, 16 * 9)
            act.wait_ge(s_zero, 8)
            act.activation(tanhs[:, :], gates[:, :], ACT.Tanh).then_inc(s_tanh, 1)
            for k in range(PI):
                item(0, 0, k)
            run_batches(act, body)
            exps(B - 1, 1, H - 1)
            phi(B - 1, H - 2)
            phi(B - 1, H - 1)
            for k in range(HI_):
                hitem(B - 1, k)
            weigh(B - 1)

        @block.vector
        def _(dve):
            settled = (s_zero, 8)

            def stats(c):
                need(dve, s_cload, 16, c, 16)
                for j in range(NB0):
                    dve.bn_stats(bns[0:KB0, j, :], ctx_t[:, j, :]).then_inc(s_stats, 1)
                need(dve, s_xload, 16, c, 16)
                dve.bn_stats(bns[0:T, NB0, :], x2_t[:, :]).then_inc(s_stats, 1)
                need(dve, s_stats, 8, c, 4, settled)
                for j in range(NB0):
                    dve.bn_aggr(mv[0:KB0, j, :], bns[0:KB0, j, :]).then_inc(s_stats, 1)
                dve.bn_aggr(mv[0:T, NB0, :], bns[0:T, NB0, :]).then_inc(s_stats, 1)

            def normalise(c):
                need(dve, s_rstd, 1, c, 1)
                need(dve, s_nitem, NI, c, 0)
                for j in range(NB0):
                    last = dve.tensor_scalar(ctx_n[:, j, :], ctx_t[:, j, :], mv[0:KB0, j, 0:1], rstd[0:KB0, j:j + 1], ALU.subtract, ALU.mult)
                last.then_inc(s_norm, 1)
                dve.tensor_scalar(x2_n[:, :], x2_t[:, :], mv[0:T, NB0, 0:1], rstd[0:T, NB0:NB0 + 1], ALU.subtract, ALU.mult).then_inc(s_norm, 1)

            def nitem(c, k):
                need(dve, s_nitem, NI, c, k + 1)
                if k == 0:
                    need(dve, s_tsplit, 6, c, 0)
                if k < N_L:
                    dve.tensor_scalar(tok_f[:, k, 0:C], ps_x[:, 0:C], affine[:, 0, k:k + 1], affine[:, 1, k:k + 1], ALU.mult, ALU.add).then_inc(s_nfree, 1)
                else:
                    for t in range(KT):
                        last = dve.tensor_scalar(tok_f[:, t, C:NK], ps_x[:, t * T:(t + 1) * T], affine[:, 2, t:t + 1], affine[:, 3, t:t + 1], ALU.mult, ALU.add)
                    last.then_inc(s_nfree, 1)

            def item(c, par, k):
                ps = ps_p[k % 2]
                need(dve, s_ihi, PI, c, k + 1)
                if k < P_Q:
                    dve.tensor_tensor(k_s[:, LO, k, :], ps[:, 0:NK], k_s[:, HI, k, :], ALU.subtract).then_inc(s_ifree, 1)
                elif k < P_V:
                    j = 4 * (k - P_Q)
                    dve.tensor_tensor(q_s[:, LO, j:j + 4, :], ps[:, 0:4 * T].rearrange("p (j n) -> p j n", j=4), q_s[:, HI, j:j + 4, :], ALU.subtract).then_inc(s_ifree, 1)
                else:
                    j, half = (k - P_V) // 2, (k - P_V) % 2
                    cols = slice(half * 512, (half + 1) * 512)
                    dve.tensor_tensor(v_s[par][0:KB1, LO, j, cols], ps[0:KB1, :], v_s[par][0:KB1, HI, j, cols], ALU.subtract).then_inc(s_ifree, 1)

            def maxima(b, par, h):
                need_all(dve, settled, (s_score, H, b, h + 1), (s_tr, H, b, h - RING + 1), *([(s_keep, 1, b, 1)] if h == 0 else []))
                dve.tensor_tensor_reduce(prob[:, h % RING, 0:NK], ps_s[h % 2][0:T, 0:NK], keep[par][:, :], -SCALE1, 3e38,
                                         ALU.add, ALU.min, top[:, h % RING:h % RING + 1]).then_inc(s_max, 1)

            def plo(b, h):
                need(dve, s_phi, H, b, h + 1)
                dve.tensor_tensor(pT[0:KB1, h % 2, LO, :, 0:T],
                                  ps_t[h % 2][0:KB1, 0:NB1 * T].rearrange("p (j n) -> p j n", j=NB1),
                                  pT[0:KB1, h % 2, HI, :, 0:T], ALU.subtract).then_inc(s_plo, 1)

            def out_heads(c, par):
                need(dve, s_exp, H, c, H)
                dve.reciprocal(rsum[:, :], sums[par][:, :]).then_inc(s_rsum, 1)
                need(dve, s_rsum, 1, c, 1)
                need(dve, s_pv, H, c, H)
                need(dve, s_hitem, HI_, c, 0)
                for i in range(2):
                    dve.tensor_tensor(o_n[:, 8 * i:8 * i + 8, :], ps_o[i][0:T, :].rearrange("p (h d) -> p h d", h=8),
                                      rsum[:, 8 * i:8 * i + 8].unsqueeze(2).to_broadcast([T, 8, D1]), ALU.mult).then_inc(s_oread, 1)

            def hitem(c, k):
                if k < H_O:
                    need(dve, s_hhi, 3, c, k + 1)
                    dve.tensor_tensor(oT[:, LO, 4 * k:4 * k + 4, :], ps_x[:, 0:4 * T].rearrange("p (j n) -> p j n", j=4), oT[:, HI, 4 * k:4 * k + 4, :], ALU.subtract).then_inc(s_hfree, 1)
                elif k == H_O:
                    need(dve, s_hitem, HI_, c, k + 1)
                    need(dve, s_rload, 16, c, 16)
                    need(dve, s_store, 48, c, 0)
                    dve.scalar_tensor_tensor(x3[:, :], ps_x[0:T, 0:D], tanhs[0:T, 1:2], x_res[:, :], ALU.mult, ALU.add).then_inc(s_hfree, 1)
                    need(dve, s_hfree, HI_, c, k + 1)
                    dve.bn_stats(bns3[:, :], x3[:, :]).then_inc(s_stats3, 1)
                    need(dve, s_stats3, 2, c, 1, settled)
                    dve.bn_aggr(mv3[:, :], bns3[:, :]).then_inc(s_stats3, 1)
                elif k == H_X:
                    need(dve, s_hhi, 3, c, 3)
                    dve.tensor_tensor(x3T[:, LO, :, :], ps_x[:, 0:KT * T].rearrange("p (t n) -> p t n", t=KT), x3T[:, HI, :, :], ALU.subtract).then_inc(s_hfree, 1)
                else:
                    need(dve, s_hitem, HI_, c, k + 1)
                    dve.tensor_tensor(logit[:, :], ps_x[0:T, 0:E], br_r[0:T, :], ALU.add).then_inc(s_hfree, 1)
                    need(dve, s_hfree, HI_, c, k + 1, settled)
                    dve.max(best[:, :], logit[:, :]).then_inc(s_route, 1)
                    need(dve, s_route, ROUTE, c, 1, settled)
                    dve.max_index(place[:, :], best[:, :], logit[:, :]).then_inc(s_route, 1)
                    need(dve, s_route, ROUTE, c, 2)
                    dve.tensor_copy(place_f[:, :], place[:, :]).then_inc(s_route, 1)
                    dve.tensor_tensor(gap[:, :], best[:, 1:2], best[:, 0:1], ALU.subtract).then_inc(s_route, 1)

            def norm_x3(c):
                need(dve, s_rstd3, 1, c, 1)
                dve.tensor_scalar(xn3[:, :], x3[:, :], mv3[:, 0:1], rstd3[:, 0:1], ALU.subtract, ALU.mult).then_inc(s_xn3, 1)

            def combine_weights(c):
                need(dve, s_ratio, 1, c, 1)
                dve.tensor_scalar(norm[:, :], ratio[:, :], 1.0, None, ALU.add).then_inc(s_route, 1)
                need(dve, s_route, ROUTE, c, 5)
                dve.reciprocal(share[:, :], norm[:, :]).then_inc(s_route, 1)
                need(dve, s_route, ROUTE, c, 6)
                dve.tensor_scalar(w_top[:, 0:1], share[:, :], tanhs[0:T, 3:4], None, ALU.mult)
                dve.tensor_scalar(w_top[:, 1:2], share[:, :], tanhs[0:T, 3:4], ratio[:, 0:1], ALU.mult, ALU.mult).then_inc(s_route, 1)
                need(dve, s_route, ROUTE, c, 7)
                for n in range(2):
                    last = dve.tensor_scalar(picked[:, n, :], const[0:T, IOTA:IOTA + E], place_f[:, n:n + 1], w_top[:, n:n + 1],
                                             ALU.is_equal, ALU.mult)
                last.then_inc(s_route, 1)
                need(dve, s_route, ROUTE, c, 8)
                dve.tensor_tensor(cw[:, :], picked[:, 0, :], picked[:, 1, :], ALU.add).then_inc(s_route, 1)

            def body(b, par):
                for s in range(H):
                    if ahead(b, 1):
                        for k in PSLOT.get(s - 1, []):
                            item(b + 1, 1 - par, k)
                    if not first(b) and s == 3:
                        out_heads(b - 1, 1 - par)
                    kind, k = XSLOT.get(s - 1, ("", 0))
                    if kind == "h" and not first(b):
                        hitem(b - 1, k)
                    if kind == "n" and ahead(b, 2):
                        nitem(b + 2, k)
                    if not first(b):
                        if s == 8:
                            norm_x3(b - 1)
                        if s == 12:
                            combine_weights(b - 1)
                    if ahead(b, 2):
                        if s == 1:
                            stats(b + 2)
                        if s == 2:
                            normalise(b + 2)
                    maxima(b, par, s)
                    if not (first(b) and s < 2):
                        c, _, h = behind(s, 2, b, par)
                        plo(c, h)

            dve.wait_ge(s_setup, 16 * 9)
            dve.wait_ge(s_zero, 8)
            dve.wait_ge(s_tanh, 1)
            stats(0)
            normalise(0)
            for k in range(NI):
                nitem(0, k)
            stats(1)
            for k in range(2):
                item(0, 0, k)
            normalise(1)
            for k in range(2, 4):
                item(0, 0, k)
            for k in range(NI):
                nitem(1, k)
            for k in range(4, PI):
                item(0, 0, k)
            run_batches(dve, body)
            plo(B - 1, H - 2)
            plo(B - 1, H - 1)
            out_heads(B - 1, 1)
            for k in range(H_X):
                hitem(B - 1, k)
            norm_x3(B - 1)
            hitem(B - 1, H_X)
            hitem(B - 1, H_G)
            combine_weights(B - 1)

F = 512
FT = F // 128
W1N, W2N = KT * 2 * F, FT * D
NG = 4
GB = B // NG
G = GB * T

def phase_experts(nc, w_all, b2, consts, x3_dram, x3T_dram, cw_dram, out):
    with ExitStack() as ctx:
        sb = lambda name, shape, dt: ctx.enter_context(nc.sbuf_tensor("c_" + name, shape, dt))
        sem = lambda name: ctx.enter_context(nc.semaphore("c_" + name))
        bank = lambda name: ctx.enter_context(nc.psum_tensor("c_" + name, [128, 512], F32))

        const = sb("const", [128, NCONST], F32)
        ident = const[:, IDENT:IDENT + 128]
        x_T = sb("x_T", [128, B, 2, KT, T], F16)
        x_s = sb("x_s", [128, 2, KT, B, T], F16)
        x3 = sb("x3", [T, B, D], F32)
        acc = sb("acc", [T, B, D], F32)
        cw = sb("cw", [T, B, E], F32)
        cw_e = [sb(f"cw_e{i}", [T, B], F32) for i in range(2)]
        cwT_f = sb("cwT_f", [128, T], F32)
        cwT_s = sb("cwT_s", [128, 2, T], F16)
        cwT_b = sb("cwT_b", [128, 2, B, T], F16)
        b2_f = sb("b2_f", [128, D], F32)
        b2_s = sb("b2_s", [128, 2, D], F16)
        w_f = [sb(f"w_f{i}", [128, W1N + W2N + 8], F32) for i in range(2)]
        w_s = [sb(f"w_s{i}", [128, 2, W1N + W2N], F16) for i in range(2)]
        b1 = [sb(f"b1{i}", [128, 8], F32) for i in range(2)]
        sil = sb("sil", [128, 2, G], F32)
        act_f = sb("act_f", [128, 2, G], F32)
        act_s = sb("act_s", [128, 2, 2, FT, G], F16)

        ps_a = [bank(f"ps_a{i}") for i in range(2)]
        ps_g = [bank(f"ps_g{i}") for i in range(2)]
        ps_y = [bank(f"ps_y{i}") for i in range(GB)]

        s_setup = sem("setup")
        s_xT = sem("xT")
        s_xs = sem("xs")
        s_cw = sem("cw")
        s_cwT = sem("cwT")
        s_cwf = sem("cwf")
        s_cws = sem("cws")
        s_cwb = sem("cwb")
        s_b2 = sem("b2")
        s_bias = sem("bias")
        s_acc = sem("acc")
        s_wload = sem("wload")
        s_wsplit = sem("wsplit")
        s_cwe = sem("cwe")
        s_a = sem("a")
        s_g = sem("g")
        s_sil = sem("sil")
        s_act = sem("act")
        s_ahi = sem("ahi")
        s_alo = sem("alo")
        s_y = sem("y")
        s_yread = sem("yread")
        s_store = sem("store")

        PAIRS = NG * FT

        def run_experts(eng, body):
            body(0, 0)
            body(1, 1)
            with eng.Fori(1, E // 2) as i:
                body(i * 2, 0)
                body(i * 2 + 1, 1)

        block = ctx.enter_context(nc.Block())

        @block.sync
        def _(sp):
            settled = (s_setup, 32)

            def load(e, par):
                sp.dma_start(w_f[par][:, :], w_all[e]).then_inc(s_wload, 16)

            sp.dma_start(const[:, :], consts).then_inc(s_setup, 16)
            sp.dma_start(cw[:, :, :], cw_dram.rearrange("b t e -> t b e")).then_inc(s_cw, 16)
            load(0, 0)
            sp.dma_start(x_T[:, :, :, :, :], x3T_dram.rearrange("b p s k n -> p b s k n")).then_inc(s_xT, 16)
            sp.dma_start(b2_f[:, :], b2).then_inc(s_b2, 16)
            sp.dma_start(x3[:, :, :], x3_dram.rearrange("b t d -> t b d")).then_inc(s_setup, 16)
            need(sp, s_wsplit, 3, 0, 1)
            load(1, 1)
            with sp.Fori(0, E // 2 - 1) as i:
                for par in range(2):
                    need(sp, s_wsplit, 3, i * 2 + par + 1, 1, settled)
                    load(i * 2 + par + 2, par)
            for g in range(NG):
                need(sp, s_yread, B, E - 1, (g + 1) * GB, settled)
                sp.dma_start(out[g * GB:(g + 1) * GB].rearrange("b t d -> t b d"), acc[:, g * GB:(g + 1) * GB, :]).then_inc(s_store, 16)
            sp.wait_ge(s_store, 16 * NG)

        @block.gpsimd
        def _(pool):
            settled = (s_setup, 32)

            def split_weights(e, par):
                need_all(pool, settled, (s_wload, 16, e, 16), (s_y, B, e - 1, 0), (s_act, PAIRS, e - 1, 0))
                pool.tensor_copy(w_s[par][:, HI, :], w_f[par][:, 0:W1N + W2N]).then_inc(s_wsplit, 1)
                need(pool, s_wsplit, 3, e, 1)
                pool.tensor_tensor(w_s[par][:, LO, :], w_f[par][:, 0:W1N + W2N], w_s[par][:, HI, :], ALU.subtract).then_inc(s_wsplit, 1)
                pool.tensor_copy(b1[par][:, :], w_f[par][:, W1N + W2N:]).then_inc(s_wsplit, 1)

            split_weights(0, 0)
            split_weights(1, 1)
            with pool.Fori(0, E // 2 - 1) as i:
                split_weights(i * 2 + 2, 0)
                split_weights(i * 2 + 3, 1)

        @block.tensor
        def _(pe):
            def product(out_, sta, mov, tiles):
                for k in range(tiles):
                    for n, (a, m) in enumerate(PASSES):
                        last = pe.matmul(out_, sta(a, k), mov(m, k), start=(k == 0 and n == 0),
                                         stop=(k == tiles - 1 and n == 2))
                return last

            def hidden(e, par, g, m):
                n = g * FT + m
                w1 = w_s[par][:, :, 0:W1N].rearrange("p s (k n) -> p s k n", k=KT)
                xg = lambda a, t: x_s[:, a, t, g * GB:(g + 1) * GB, :].rearrange("p b n -> p (b n)")
                need(pe, s_sil, PAIRS, e, n - 1)
                product(ps_a[n % 2][:, 0:G], lambda a, t: w1[:, a, t, m * 128:(m + 1) * 128], xg, KT).then_inc(s_a, 1)
                need(pe, s_act, PAIRS, e, n - 1)
                product(ps_g[n % 2][:, 0:G], lambda a, t: w1[:, a, t, F + m * 128:F + (m + 1) * 128], xg, KT).then_inc(s_g, 1)

            def outputs(e, par, g):
                w2 = w_s[par][:, :, W1N:].rearrange("p s (k n) -> p s k n", k=FT)
                need(pe, s_alo, PAIRS, e, (g + 1) * FT)
                for i in range(GB):
                    need(pe, s_yread, B, e, (g - 1) * GB + i + 1)
                    product(ps_y[i][0:T, 0:D], lambda a, t: act_s[:, g % 2, a, t, i * T:(i + 1) * T],
                            lambda a, t: w2[:, a, t, :], FT).then_inc(s_y, 1)

            def body(e, par):
                need(pe, s_wsplit, 3, e, 2)
                for g in range(NG):
                    for m in range(FT):
                        hidden(e, par, g, m)
                        if m == 1 and g > 0:
                            outputs(e, par, g - 1)
                outputs(e, par, NG - 1)

            pe.wait_ge(s_setup, 16)
            pe.wait_ge(s_cw, 16)
            pe.transpose(ps_a[0][:, 0:T], cw[:, :, :].rearrange("t b e -> t (b e)"), ident[0:T, 0:T]).then_inc(s_cwT, 1)
            pe.wait_ge(s_cwb, 2)
            pe.wait_ge(s_b2, 18)
            for b in range(B):
                if b >= GB:
                    pe.wait_ge(s_acc, b - GB + 1)
                for n, (a, m) in enumerate(PASSES):
                    last = pe.matmul(ps_y[b % GB][0:T, 0:D], cwT_b[:, a, b, :], b2_s[:, m, :], start=(n == 0), stop=(n == 2))
                last.then_inc(s_bias, 1)
            pe.wait_ge(s_acc, B)
            pe.wait_ge(s_xs, 2)
            run_experts(pe, body)

        @block.scalar
        def _(act):
            def silu(e, par, n):
                m = n % FT
                if n == 0:
                    need(act, s_wsplit, 3, e, 3)
                need(act, s_a, PAIRS, e, n + 1)
                need(act, s_act, PAIRS, e, n - 1)
                act.activation(sil[:, n % 2, :], ps_a[n % 2][:, 0:G], ACT.Silu, bias=b1[par][:, m:m + 1]).then_inc(s_sil, 1)

            def high(e, n):
                g, m = n // FT, n % FT
                need(act, s_act, PAIRS, e, n + 1)
                if m == 0:
                    need(act, s_y, B, e, (g - 1) * GB)
                act.activation(act_s[:, g % 2, HI, m, :], act_f[:, n % 2, :], ACT.Copy).then_inc(s_ahi, 1)

            def body(e, par):
                for n in range(PAIRS):
                    silu(e, par, n)
                    if n:
                        high(e, n - 1)
                high(e, PAIRS - 1)

            act.wait_ge(s_cwT, 1)
            act.activation(cwT_f[:, :], ps_a[0][:, 0:T], ACT.Copy).then_inc(s_cwf, 1)
            act.wait_ge(s_xT, 16)
            act.activation(x_s[:, HI, :, :, :].rearrange("p k b n -> p b k n"), x_T[:, :, HI, :, :], ACT.Copy).then_inc(s_xs, 1)
            run_experts(act, body)

        @block.vector
        def _(dve):
            def product_act(e, par, n):
                m = n % FT
                need(dve, s_sil, PAIRS, e, n + 1)
                need(dve, s_g, PAIRS, e, n + 1)
                need(dve, s_alo, PAIRS, e, n - 1)
                dve.scalar_tensor_tensor(act_f[:, n % 2, :], ps_g[n % 2][:, 0:G], b1[par][:, FT + m:FT + m + 1], sil[:, n % 2, :],
                                         ALU.add, ALU.mult).then_inc(s_act, 1)

            def low(e, n):
                g, m = n // FT, n % FT
                need(dve, s_ahi, PAIRS, e, n + 1)
                dve.tensor_tensor(act_s[:, g % 2, LO, m, :], act_f[:, n % 2, :], act_s[:, g % 2, HI, m, :], ALU.subtract).then_inc(s_alo, 1)

            def add(e, par, g):
                for i in range(GB):
                    b = g * GB + i
                    need(dve, s_y, B, e, b + 1)
                    need(dve, s_yread, B, e, 0)
                    dve.scalar_tensor_tensor(acc[:, b, :], ps_y[i][0:T, 0:D], cw_e[par][:, b:b + 1], acc[:, b, :],
                                             ALU.mult, ALU.add).then_inc(s_yread, 1)

            def body(e, par):
                need(dve, s_yread, B, e - 1, 0)
                dve.tensor_copy(cw_e[par][:, :], cw[:, :, bass.ds(e, 1)].rearrange("t b o -> t (b o)")).then_inc(s_cwe, 1)
                need(dve, s_cwe, 1, e, 1)
                for n in range(PAIRS):
                    product_act(e, par, n)
                    if n:
                        low(e, n - 1)
                    if n % FT == 2 and n > FT:
                        add(e, par, n // FT - 1)
                low(e, PAIRS - 1)
                add(e, par, NG - 1)

            dve.wait_ge(s_b2, 16)
            dve.tensor_copy(b2_s[:, HI, :], b2_f[:, :]).then_inc(s_b2, 1)
            dve.wait_ge(s_b2, 17)
            dve.tensor_tensor(b2_s[:, LO, :], b2_f[:, :], b2_s[:, HI, :], ALU.subtract).then_inc(s_b2, 1)
            dve.wait_ge(s_cwf, 1)
            dve.tensor_copy(cwT_s[:, HI, :], cwT_f[:, :]).then_inc(s_cws, 1)
            dve.wait_ge(s_cws, 1)
            dve.tensor_tensor(cwT_s[:, LO, :], cwT_f[:, :], cwT_s[:, HI, :], ALU.subtract).then_inc(s_cws, 1)
            dve.wait_ge(s_cws, 2)
            dve.wait_ge(s_setup, 32)
            for part in (HI, LO):
                dve.tensor_tensor(cwT_b[:, part, :, :], cwT_s[:, part, :].unsqueeze(1).to_broadcast([128, B, T]),
                                  const[:, BATCHMASK:BATCHMASK + B].unsqueeze(2).to_broadcast([128, B, T]), ALU.mult).then_inc(s_cwb, 1)
            dve.wait_ge(s_xT, 16)
            dve.tensor_copy(x_s[:, LO, :, :, :].rearrange("p k b n -> p b k n"), x_T[:, :, LO, :, :]).then_inc(s_xs, 1)
            for b in range(B):
                dve.wait_ge(s_bias, b + 1)
                dve.tensor_tensor(acc[:, b, :], ps_y[b % GB][0:T, 0:D], x3[:, b, :], ALU.add).then_inc(s_acc, 1)
            dve.wait_ge(s_acc, B)
            run_experts(dve, body)

def build_program(nc, a, out):
    x2 = nc.dram_tensor("x2", (B, T, D), F32, kind="Internal").ap()
    x3 = nc.dram_tensor("x3", (B, T, D), F32, kind="Internal").ap()
    x3T = nc.dram_tensor("x3T", (B, 128, 2, KT, T), F16, kind="Internal").ap()
    cw = nc.dram_tensor("cw", (B, T, E), F32, kind="Internal").ap()
    with nc.sbuf_tensor("w1_s", [128, 2, WKV + WQ + WOUT], F16) as w1_s:
        phase_attention_small_heads(nc, a["x"], a["ctxT"], a["mask0"], a["g_xattn"], a["g_ffn"], a["wq0"], a["wk0"],
                                    a["wv0"], a["bq0"], a["bk0"], a["bv0"], a["wg0"], a["we0"], a["be0"], a["consts"],
                                    x2, w1_s, a["w1"])
        phase_attention_large_heads(nc, a["ctx"], a["mask1"], a["g_xattn"], a["g_ffn"], a["g1"], a["b1"], a["g2"],
                                    a["b2"], a["wr1"], a["br1"], a["consts"], w1_s, x2, x3, x3T, cw)
    phase_experts(nc, a["w_experts"], a["b2_experts"], a["consts"], x3, x3T, cw, out)

def kernel(x, ctx_1024, mask_BxSxS2_ff1, mask_BxS2_bk0, g_xattn, g_ffn,
           L0_xattn_Wq, L0_xattn_bq, L0_xattn_Wk, L0_xattn_bk, L0_xattn_Wv, L0_xattn_bv,
           L0_ffn_Wg, L0_ffn_We, L0_ffn_be,
           L1_xattn_g1, L1_xattn_b1, L1_xattn_g2, L1_xattn_b2, L1_xattn_Wq, L1_xattn_Wkv, L1_xattn_Wout,
           L1_ffn_W1, L1_ffn_b1, L1_ffn_W2, L1_ffn_b2, L1_ffn_Wr, L1_ffn_br):
    import numpy as np
    import concourse.bacc as bacc
    from concourse.bass_utils import run_bass_kernel_spmd

    rows = lambda w: w.reshape(-1, 128, w.shape[-1]).transpose(1, 0, 2)
    column = lambda v: v.reshape(-1, 128).T
    twice = lambda w: np.concatenate([w, w], -1)

    p = np.arange(128)
    consts = np.zeros((128, NCONST), np.float32)
    consts[:, IDENT:IDENT + 128] = np.eye(128)
    consts[:, HEADMASK:HEADMASK + 4] = (p[:, None] // D0) % 4 == np.arange(4)
    consts[:, IOTA:IOTA + E] = np.arange(E)
    consts[:, BATCHMASK:BATCHMASK + B] = p[:, None] // E == np.arange(B)

    as_np = np.asarray
    experts = [as_np(L1_ffn_W1).reshape(E, KT, 128, 2 * F).transpose(0, 2, 1, 3).reshape(E, 128, W1N),
               as_np(L1_ffn_W2).reshape(E, FT, 128, D).transpose(0, 2, 1, 3).reshape(E, 128, W2N),
               as_np(L1_ffn_b1).reshape(E, 2 * FT, 128).transpose(0, 2, 1)]
    arrays = {
        "x": as_np(x), "ctx": as_np(ctx_1024), "consts": consts,
        "ctxT": as_np(ctx_1024).reshape(B, C, KT, 128).transpose(0, 3, 2, 1),
        "mask0": as_np(mask_BxSxS2_ff1), "mask1": as_np(mask_BxS2_bk0),
        "g_xattn": as_np(g_xattn), "g_ffn": as_np(g_ffn),
        "wq0": rows(twice(as_np(L0_xattn_Wq).T.reshape(D, GROUPS, 64)).reshape(D, 128 * GROUPS)),
        "bq0": twice(as_np(L0_xattn_bq).reshape(GROUPS, 64)).T,
        "wk0": rows(as_np(L0_xattn_Wk).T), "bk0": column(as_np(L0_xattn_bk)),
        "wv0": rows(as_np(L0_xattn_Wv).T), "bv0": as_np(L0_xattn_bv),
        "wg0": rows(as_np(L0_ffn_Wg).T), "we0": rows(as_np(L0_ffn_We).transpose(2, 0, 1).reshape(D, E * D)),
        "be0": as_np(L0_ffn_be),
        "g1": column(as_np(L1_xattn_g1)), "b1": column(as_np(L1_xattn_b1)),
        "g2": column(as_np(L1_xattn_g2)), "b2": column(as_np(L1_xattn_b2)),
        "w1": np.concatenate([rows(as_np(w)).reshape(128, -1) for w in (L1_xattn_Wkv, L1_xattn_Wq, L1_xattn_Wout)], 1),
        "wr1": rows(as_np(L1_ffn_Wr)), "br1": as_np(L1_ffn_br),
        "w_experts": np.concatenate(experts, 2), "b2_experts": np.tile(as_np(L1_ffn_b2), (B, 1)),
    }
    nc = bacc.Bacc("TRN2", target_bir_lowering=False, num_devices=1)
    inputs, aps = {}, {}
    for name, array in arrays.items():
        array = np.ascontiguousarray(array)
        inputs[f"in_{name}"] = array
        aps[name] = nc.dram_tensor(f"in_{name}", array.shape, mybir.dt.from_np(array.dtype), kind="ExternalInput").ap()
    out = nc.dram_tensor("out", (B, T, D), F32, kind="ExternalOutput").ap()
    build_program(nc, aps, out)
    result = run_bass_kernel_spmd(nc, [inputs], core_ids=[0])
    return result.results[0]["out"]
```

```python
from contextlib import ExitStack

import concourse.bass as bass
from concourse import mybir

ALU = mybir.AluOpType
ACT = mybir.ActivationFunctionType
F32 = mybir.dt.float32
F16 = mybir.dt.float16
U32 = mybir.dt.uint32
U8 = mybir.dt.uint8

B = 16
T = 112
C = 375
D = 256
KT = D // 128
E = 8
H = 16
EPS = 1e-5
HI, LO = 0, 1
PASSES = ((HI, HI), (HI, LO), (LO, HI))

D0 = D // H
KB0, NB0 = 125, 3
SCALE0 = D0 ** -0.5
GROUPS = 4

IDENT, IOTA, TILEMASK, NCONST = 0, 128, 136, 150

def need(eng, sem, per, batch, count, met=None):
    need_all(eng, met, (sem, per, batch, count))

def need_all(eng, met, *conditions):
    values = [(sem, batch * per + count) for sem, per, batch, count in conditions]
    values = [(sem, v) for sem, v in values if not isinstance(v, int) or v > 0]
    if met and any(not isinstance(v, int) for _, v in values):
        values = [(sem, v if isinstance(v, int) else eng.to_reg(v)) for sem, v in values]
        eng.wait_ge(*met)
    for sem, v in values:
        eng.wait_ge(sem, v)

def run_batches(eng, body):
    body(0, 0)
    body(1, 1)
    with eng.Fori(1, B // 2 - 1) as i:
        body(i * 2, 0)
        body(i * 2 + 1, 1)
    body(B - 2, 0)
    body(B - 1, 1)

def first(b):
    return isinstance(b, int) and b == 0

def ahead(b, n):
    return not (isinstance(b, int) and b + n > B - 1)

def phase_attention_small_heads(nc, x, ctxT, mask, g_xattn, g_ffn, wq, wk, wv, bq, bk, bv, wg, we, be, consts,
                                x2_dram, next_w, next_w_dram):
    with ExitStack() as ctx:
        sb = lambda name, shape, dt: ctx.enter_context(nc.sbuf_tensor("a_" + name, shape, dt))
        sem = lambda name: ctx.enter_context(nc.semaphore("a_" + name))
        bank = lambda name: ctx.enter_context(nc.psum_tensor("a_" + name, [128, 512], F32))

        const = sb("const", [128, NCONST], F32)
        ident = const[:, IDENT:IDENT + 128]
        neg_half = sb("neg_half", [128, 1], F32)
        wqkv_f = sb("wqkv_f", [128, KT, 512 + 512 + E], F32)
        wqkv = sb("wqkv", [128, 2, KT, 512 + 512 + E], F16)
        we_s = sb("we_s", [128, 2, KT, E * D], F16)
        NEXT = next_w_dram.shape[1] // H
        NLOAD = next_w_dram.shape[1] // 8
        WE = E * D // (H // 2)
        next_f = sb("next_f", [128, next_w_dram.shape[1]], F32)
        we_f = next_f[:, 0:KT * E * D].rearrange("p (k n) -> p k n", k=KT)
        be_f = sb("be_f", [128, D], F32)
        be_s = sb("be_s", [128, 2, D], F16)
        wq_s = wqkv[:, :, :, 0:512].rearrange("p s k (g m) -> p s k g m", g=GROUPS)
        wk_s = wqkv[:, :, :, 512:768]
        wv_s = wqkv[:, :, :, 768:1024]
        wg_s = wqkv[:, :, :, 1024:1024 + E]
        bq_c = sb("bq_c", [128, GROUPS], F32)
        bk_c = sb("bk_c", [128, KT], F32)
        bv_r = sb("bv_r", [128, D], F32)
        bv_t = sb("bv_t", [T, D], F32)
        gates = sb("gates", [128, 4], F32)
        tanhs = sb("tanhs", [128, 4], F32)

        x_in = sb("x_in", [T, D], F32)
        ctx_f = sb("ctx_f", [128, KT, C], F32)
        ctx_s = sb("ctx_s", [128, 2, KT, C], F16)
        keep = [sb(f"keep{i}", [T, C], F32) for i in range(2)]
        bns = sb("bns", [T, 6], F32)
        mv = sb("mv", [T, 2], F32)
        var = sb("var", [T, 1], F32)
        rstd = sb("rstd", [T, 1], F32)
        xn = sb("xn", [T, D], F32)
        xT = sb("xT", [128, 2, KT, T], F16)
        q_f = sb("q_f", [128, GROUPS * T], F32)
        q_s = sb("q_s", [128, 2, GROUPS * T], F16)
        q_masked = [sb(f"q_masked{i}", [128, 2, 4, GROUPS * T], F16) for i in range(2)]
        k_s = sb("k_s", [128, 2, 2, C], F16)
        k_stack = [sb(f"k_stack{i}", [128, GROUPS, C], F16) for i in range(2)]
        v_s = [sb(f"v_s{i}", [128, NB0, H, 2, D0], F16) for i in range(2)]

        RING = 4
        prob = sb("prob", [T, RING, C], F32)
        top = sb("top", [T, RING], F32)
        sums = [sb(f"sums{i}", [T, H], F32) for i in range(2)]
        pT = sb("pT", [128, RING, 2, NB0, 128], F16)

        x_res = sb("x_res", [T, D], F32)
        o_lo = sb("o_lo", [T, H, D0], F32)
        rsum = sb("rsum", [T, H], F32)
        rsum_t = sb("rsum_t", [T, H], F32)
        x_b = sb("x_b", [T, D], F32)
        o_f = sb("o_f", [T, H, D0], F32)
        o_n = sb("o_n", [T, H, D0], F32)
        x1 = sb("x1", [T, D], F32)
        bns1 = sb("bns1", [T, 6], F32)
        mv1 = sb("mv1", [T, 2], F32)
        var1 = sb("var1", [T, 1], F32)
        rstd1 = sb("rstd1", [T, 1], F32)
        xn1 = sb("xn1", [T, D], F32)
        x1T = sb("x1T", [128, 2, KT, T], F16)
        logit = sb("logit", [T, E], F32)
        best = sb("best", [T, 8], F32)
        place = sb("place", [T, 8], U32)
        place_f = sb("place_f", [T, 8], F32)
        gap = sb("gap", [T, 1], F32)
        ratio = sb("ratio", [T, 1], F32)
        norm = sb("norm", [T, 1], F32)
        share = sb("share", [T, 1], F32)
        w_top = sb("w_top", [T, 2], F32)
        picked = sb("picked", [T, 2, E], F32)
        cw = sb("cw", [T, 128], F32)
        cwT = sb("cwT", [128, 2, T], F16)
        acc = sb("acc", [T, D], F32)
        scaled = [sb(f"scaled{i}", [T, D], F32) for i in range(2)]
        acc_odd = sb("acc_odd", [T, D], F32)
        x2 = sb("x2", [T, D], F32)

        ps_s = [bank(f"ps_s{i}") for i in range(2)]
        ps_t = [bank(f"ps_t{i}") for i in range(2)]
        ps_o = bank("ps_o")
        ps_p = [bank(f"ps_p{i}") for i in range(3)]

        s_setup = sem("setup")
        s_const = sem("const")
        s_wk = sem("wk")
        s_wq = sem("wq")
        s_wv = sem("wv")
        s_wload = sem("wload")
        s_nload = sem("nload")
        s_nhi = sem("nhi")
        s_nlo = sem("nlo")
        s_bvt = sem("bvt")
        s_xb = sem("xb")
        s_zero = sem("zero")
        s_zq = sem("zq")
        s_besplit = sem("besplit")
        s_whi = sem("whi")
        s_wlo = sem("wlo")
        s_wehi = sem("wehi")
        s_welo = sem("welo")
        s_tanh = sem("tanh")
        s_xload = sem("xload")
        s_cload = sem("cload")
        s_mload = sem("mload")
        s_rload = sem("rload")
        s_keep = sem("keep")
        s_csplit = sem("csplit")
        s_stats = sem("stats")
        s_var = sem("var")
        s_rstd = sem("rstd")
        s_xn = sem("xn")
        s_item = sem("item")
        s_ihi = sem("ihi")
        s_ifree = sem("ifree")
        s_qhi = sem("qhi")
        s_qlo = sem("qlo")
        s_qmask = sem("qmask")
        s_kstack = sem("kstack")
        s_score = sem("score")
        s_max = sem("max")
        s_exp = sem("exp")
        s_tr = sem("tr")
        s_phi = sem("phi")
        s_plo = sem("plo")
        s_pv = sem("pv")
        s_olo = sem("olo")
        s_rsum = sem("rsum")
        s_oread = sem("oread")
        s_on = sem("on")
        s_rsumt = sem("rsumt")
        s_x1 = sem("x1")
        s_stats1 = sem("stats1")
        s_var1 = sem("var1")
        s_rstd1 = sem("rstd1")
        s_xn1 = sem("xn1")
        s_ditem = sem("ditem")
        s_dhi = sem("dhi")
        s_dfree = sem("dfree")
        s_route = sem("route")
        s_ratio = sem("ratio")
        s_scaled = sem("scaled")
        s_odd = sem("odd")
        s_x2 = sem("x2")
        s_store = sem("store")

        PI = 7
        P_K, P_XT, P_Q, P_V = 0, 2, 3, 4
        NSETUP = 16 * 4
        QMASK = 16 * 8
        DI = 8
        D_XT, D_GATE, D_CWT, D_PAIRS, D_BIAS = 0, 1, 4, (2, 3, 5, 6), 7
        ROUTE = 9
        PSLOT = {0: [P_K], 1: [P_K + 1], 2: [P_XT], 4: [P_Q], 5: [P_V], 6: [P_V + 1], 7: [P_V + 2]}
        DSLOT = {7: [D_XT], 8: [D_GATE], 9: [D_PAIRS[0]], 10: [D_PAIRS[1]], 11: [D_CWT], 12: [D_PAIRS[2]],
                 13: [D_PAIRS[3]], 14: [D_BIAS]}
        DREAD = {8: [D_XT], 9: [D_GATE], 11: [D_PAIRS[0]], 12: [D_PAIRS[1], D_CWT], 13: [D_PAIRS[2]],
                 14: [D_PAIRS[3]], 15: [D_BIAS]}
        WPARTS = ((512, 768), (0, 512), (768, 1024 + E))

        def heads(s, lag, b, par):
            h = s - lag
            return (b, par, h) if h >= 0 else (b - 1, 1 - par, h + H)

        ps_i = (ps_p[0], ps_p[1], ps_p[2])
        ps_d = (ps_p[1], ps_p[2], ps_p[0])

        block = ctx.enter_context(nc.Block())

        @block.sync
        def _(sp):
            sp.dma_start(ctx_f[:, :, :], ctxT[0]).then_inc(s_cload, 16)
            sp.dma_start(wqkv_f[:, :, 512:768], wk).then_inc(s_wk, 16)
            sp.dma_start(x_in[:, :], x[0]).then_inc(s_xload, 16)
            sp.dma_start(wqkv_f[:, :, 0:512], wq).then_inc(s_wq, 16)
            sp.dma_start(wqkv_f[:, :, 768:1024], wv).then_inc(s_wv, 16)
            sp.dma_start(wqkv_f[:, :, 1024:1024 + E], wg).then_inc(s_wv, 16)
            sp.dma_start(keep[0][:, :], mask[0]).then_inc(s_mload, 16)
            sp.dma_start(bv_r[:, :], bv.partition_broadcast(128)).then_inc(s_setup, 16)
            sp.dma_start(gates[:, 0:2], g_xattn.partition_broadcast(128)).then_inc(s_setup, 16)
            sp.dma_start(gates[:, 2:4], g_ffn.partition_broadcast(128)).then_inc(s_setup, 16)
            sp.wait_ge(s_zero, 1)
            sp.dma_start(be_f[0:E, :], be).then_inc(s_setup, 16)

            settled = (s_zero, 1)

            def load_tokens(c):
                need(sp, s_xn, 1, c, 0, settled)
                sp.dma_start(x_in[:, :], x[c]).then_inc(s_xload, 16)
                need(sp, s_csplit, 2, c, 0, settled)
                sp.dma_start(ctx_f[:, :, :], ctxT[c]).then_inc(s_cload, 16)

            def load_mask(c, par):
                need_all(sp, settled, (s_max, H, c - 1, 0), (s_keep, 1, c, 0))
                sp.dma_start(keep[par][:, :], mask[c]).then_inc(s_mload, 16)

            def load_residual(c):
                need(sp, s_xb, 1, c, 0, settled)
                sp.dma_start(x_res[:, :], x[c]).then_inc(s_rload, 16)

            def stack_keys(c, par):
                need_all(sp, settled, (s_ihi, 6, c, P_K + 2), (s_ifree, PI, c, P_K + 2), (s_score, H, c - 1, 1))
                for a in range(2):
                    for part in (HI, LO):
                        sp.dma_start(k_stack[par][64 * part:64 * part + 64, a::2, :],
                                     k_s[64 * a:64 * a + 64, part, :, :]).then_inc(s_kstack, 16)

            def mask_queries(c, par):
                need_all(sp, settled, (s_qlo, 1, c, 1), (s_score, H, c - 1, 1))
                for m in range(4):
                    for row in (D0 * m, 64 + D0 * m):
                        sp.dma_start(q_masked[par][row:row + D0, :, m, :], q_s[row:row + D0, :, :]).then_inc(s_qmask, 16)

            def store(c):
                need(sp, s_x2, 1, c, 1, settled)
                sp.dma_start(x2_dram[c], x2[:, :]).then_inc(s_store, 16)

            def body(b, par):
                if ahead(b, 1):
                    load_mask(b + 1, 1 - par)
                if not first(b):
                    load_residual(b - 1)
                if ahead(b, 2):
                    load_tokens(b + 2)
                if ahead(b, 1):
                    stack_keys(b + 1, 1 - par)
                    mask_queries(b + 1, 1 - par)
                if not ahead(b, 1):
                    load_residual(b)
                if not first(b):
                    store(b - 1)

            load_tokens(1)
            stack_keys(0, 0)
            sp.wait_ge(s_zq, 2)
            mask_queries(0, 0)
            run_batches(sp, body)
            store(B - 1)
            sp.wait_ge(s_store, 16 * B)
            sp.wait_ge(s_nlo, H)

        @block.gpsimd
        def _(pool):
            pool.memset(be_f[:, :], 0.0).then_inc(s_zero, 1)
            pool.memset(neg_half[:, :], -0.5).then_inc(s_zero, 1)
            pool.memset(cw[:, :], 0.0).then_inc(s_zero, 1)
            pool.memset(pT[:, :, :, :, T:128], 0.0).then_inc(s_zero, 1)

            settled = (s_zero, 4)

            def split_context(c):
                need_all(pool, settled, (s_cload, 16, c, 16), (s_item, PI, c, 0))
                pool.tensor_copy(ctx_s[:, HI, :, :], ctx_f[:, :, :]).then_inc(s_csplit, 1)
                need(pool, s_csplit, 2, c, 1)
                pool.tensor_tensor(ctx_s[:, LO, :, :], ctx_f[:, :, :], ctx_s[:, HI, :, :], ALU.subtract).then_inc(s_csplit, 1)

            def deviation(c, s_in, s_mid, s_out, stat, mid, out):
                need(pool, s_in, 2, c, 2, settled)
                pool.tensor_scalar(mid[:, :], stat[:, 1:2], 1.0, EPS, ALU.mult, ALU.add).then_inc(s_mid, 1)
                need(pool, s_mid, 1, c, 1)
                pool.tensor_tensor(out[:, :], mid[:, :], neg_half[0:T, :], ALU.pow).then_inc(s_out, 1)

            def deviation_x(c):
                deviation(c, s_stats, s_var, s_rstd, mv, var, rstd)

            def deviation_x1(c):
                deviation(c, s_stats1, s_var1, s_rstd1, mv1, var1, rstd1)

            def mask_bias(c, par):
                need(pool, s_mload, 16, c, 16, settled)
                pool.tensor_scalar(keep[par][:, :], keep[par][:, :], -1.0, 10000.0 / SCALE0, ALU.add, ALU.mult).then_inc(s_keep, 1)

            def split_queries(c):
                need_all(pool, settled, (s_ifree, PI, c, P_Q + 1), (s_qmask, QMASK, c, 0))
                pool.tensor_copy(q_s[:, HI, :], q_f[:, :]).then_inc(s_qhi, 1)
                need(pool, s_qhi, 1, c, 1)
                pool.tensor_tensor(q_s[:, LO, :], q_f[:, :], q_s[:, HI, :], ALU.subtract).then_inc(s_qlo, 1)

            def residual(c):
                need(pool, s_rload, 16, c, 16)
                pool.tensor_tensor(x_b[:, :], x_res[:, :], bv_t[:, :], ALU.add).then_inc(s_xb, 1)
                need(pool, s_rsumt, 1, c, 1)
                need(pool, s_oread, 1, c, 1)
                pool.tensor_tensor(o_n[:, :, :], o_f[:, :, :], rsum_t[:, :].unsqueeze(2).to_broadcast([T, H, D0]), ALU.mult).then_inc(s_on, 1)
                need(pool, s_on, 1, c, 1)
                need(pool, s_xb, 1, c, 1)
                need(pool, s_odd, E // 2, c, 0)
                pool.tensor_tensor(x1[:, :], o_n[:, :, :].rearrange("p h d -> p (h d)"), x_b[:, :], ALU.add).then_inc(s_x1, 1)

            def experts_low(n):
                pool.wait_ge(s_wehi, n + 1)
                cols = slice(n * WE, (n + 1) * WE)
                pool.tensor_tensor(we_s[:, LO, :, cols], we_f[:, :, cols], we_s[:, HI, :, cols], ALU.subtract).then_inc(s_welo, 1)

            def next_low(n):
                pool.wait_ge(s_nhi, n + 1)
                cols = slice(n * NEXT, (n + 1) * NEXT)
                pool.tensor_tensor(next_w[:, LO, cols], next_f[:, cols], next_w[:, HI, cols], ALU.subtract).then_inc(s_nlo, 1)

            def sum_experts(c, alone=True):
                for j in range(E // 2):
                    if not alone:
                        for n in range(2):
                            next_low((c - (B - 3)) * 8 + 2 * j + n)
                    need(pool, s_scaled, E // 2, c, j + 1)
                    need(pool, s_odd if j else s_x2, E // 2 if j else 1, c, j)
                    pool.tensor_tensor(acc_odd[:, :], scaled[j % 2][:, :], (acc_odd if j else x1)[:, :], ALU.add).then_inc(s_odd, 1)
                need(pool, s_odd, E // 2, c, E // 2)
                need(pool, s_dfree, DI, c, DI)
                need(pool, s_store, 16, c, 0)
                pool.tensor_tensor(x2[:, :], acc_odd[:, :], acc[:, :], ALU.add).then_inc(s_x2, 1)

            def body(b, par):
                if ahead(b, 1):
                    deviation_x(b + 1)
                if not first(b):
                    residual(b - 1)
                    deviation_x1(b - 1)
                if ahead(b, 1):
                    mask_bias(b + 1, 1 - par)
                    split_queries(b + 1)
                if ahead(b, 2):
                    split_context(b + 2)
                if not first(b):
                    sum_experts(b - 1, ahead(b, 2))
                if first(b):
                    for n in range(H // 2):
                        experts_low(n)

            split_context(0)
            mask_bias(0, 0)
            deviation_x(0)
            split_queries(0)
            split_context(1)
            pool.wait_ge(s_setup, NSETUP)
            pool.tensor_copy(be_s[:, HI, :], be_f[:, :]).then_inc(s_besplit, 1)
            pool.wait_ge(s_besplit, 1)
            pool.tensor_tensor(be_s[:, LO, :], be_f[:, :], be_s[:, HI, :], ALU.subtract).then_inc(s_besplit, 1)
            pool.wait_ge(s_bvt, 1)
            run_batches(pool, body)
            residual(B - 1)
            deviation_x1(B - 1)
            sum_experts(B - 1)

        @block.tensor
        def _(pe):
            def product(out, sta, mov):
                for k in range(KT):
                    for n, (a, m) in enumerate(PASSES):
                        last = pe.matmul(out, sta(a, k), mov(m, k), start=(k == 0 and n == 0),
                                         stop=(k == KT - 1 and n == 2))
                return last

            def pe_wait_weights(c, n):
                if first(c):
                    pe.wait_ge(s_whi, n)
                    pe.wait_ge(s_wlo, n)

            def item(c, par, k):
                ps = ps_i[k % 3]
                if k < 3 and isinstance(c, int) and c < 3:
                    need(pe, s_ifree, PI, c, 0)
                elif k < 3:
                    need(pe, s_dfree, DI, c - 2, k - 2)
                else:
                    need(pe, s_ifree, PI, c, k - 2)
                if k == P_XT:
                    need(pe, s_xn, 1, c, 1)
                    for t in range(KT):
                        last = pe.transpose(ps[:, t * T:(t + 1) * T], xn[:, t * 128:(t + 1) * 128], ident[0:T, 0:T])
                elif P_K <= k < P_Q:
                    j = k - P_K
                    pe_wait_weights(c, 1)
                    need(pe, s_csplit, 2, c, 2)
                    last = product(ps[:, 0:C], lambda a, t: wk_s[:, a, t, j * 128:(j + 1) * 128],
                                   lambda a, t: ctx_s[:, a, t, :])
                elif k == P_Q:
                    pe_wait_weights(c, 2)
                    need(pe, s_ihi, 6, c, P_XT + 1)
                    need(pe, s_ifree, PI, c, P_XT + 1)
                    for g in range(GROUPS):
                        last = product(ps[:, g * T:(g + 1) * T], lambda a, t: wq_s[:, a, t, g, :],
                                       lambda a, t: xT[:, a, t, :])
                else:
                    j = k - P_V
                    pe_wait_weights(c, 3)
                    last = product(ps[0:KB0, 0:D], lambda a, t: ctx_s[:, a, t, j * KB0:(j + 1) * KB0],
                                   lambda a, t: wv_s[:, a, t, :])
                last.then_inc(s_item, 1)

            def ditem(c, k):
                ps = ps_d[k % 3]
                if k >= 3:
                    need(pe, s_dfree, DI, c, k - 2)
                elif ahead(c, 2):
                    need(pe, s_ifree, PI, c + 2, P_V + 1 + k)
                if k == D_XT:
                    need(pe, s_xn1, 1, c, 1)
                    for t in range(KT):
                        last = pe.transpose(ps[:, t * T:(t + 1) * T], xn1[:, t * 128:(t + 1) * 128], ident[0:T, 0:T])
                elif k == D_GATE:
                    need(pe, s_dhi, 2, c, 1)
                    need(pe, s_dfree, DI, c, D_XT + 1)
                    last = product(ps[0:T, 0:E], lambda a, t: x1T[:, a, t, :], lambda a, t: wg_s[:, a, t, :])
                elif k == D_CWT:
                    need(pe, s_route, ROUTE, c, ROUTE)
                    last = pe.transpose(ps[:, 0:T], cw[:, :], ident[0:T, 0:T])
                elif k == D_BIAS:
                    if first(c):
                        pe.wait_ge(s_besplit, 2)
                    need(pe, s_dhi, 2, c, 2)
                    need(pe, s_dfree, DI, c, D_CWT + 1)
                    for n, (a, m) in enumerate(PASSES):
                        last = pe.matmul(ps[0:T, 0:D], cwT[:, a, :], be_s[:, m, :], start=(n == 0), stop=(n == 2))
                else:
                    j = D_PAIRS.index(k)
                    if first(c):
                        pe.wait_ge(s_welo, H // 2)
                    last = product(ps[0:T, :], lambda a, t: x1T[:, a, t, :],
                                   lambda a, t: we_s[:, a, t, j * 512:(j + 1) * 512])
                last.then_inc(s_ditem, 1)

            def scores(b, par, h):
                g, m = h // 4, h % 4
                if h == 0:
                    need(pe, s_qmask, QMASK, b, QMASK)
                    need(pe, s_kstack, 64, b, 64)
                need(pe, s_max, H, b, h - 1)
                for part in (HI, LO):
                    last = pe.matmul(ps_s[h % 2][0:T, 0:C], q_masked[par][:, part, m, g * T:(g + 1) * T],
                                     k_stack[par][:, g, :], start=(part == HI), stop=(part == LO))
                last.then_inc(s_score, 1)

            def transposes(b, h):
                need(pe, s_exp, H, b, h + 1)
                need(pe, s_plo, H, b, h - 1)
                for j in range(NB0):
                    last = pe.transpose(ps_t[h % 2][0:KB0, j * T:(j + 1) * T],
                                        prob[:, h % RING, j * KB0:(j + 1) * KB0], ident[0:T, 0:T])
                last.then_inc(s_tr, 1)

            def values(b, par, h):
                need(pe, s_phi, H, b, h + 1)
                need(pe, s_plo, H, b, h + 1)
                if h == 0:
                    need(pe, s_oread, 1, b, 0)
                    need(pe, s_ihi, 6, b, 6)
                    need(pe, s_ifree, PI, b, PI)
                for j in range(NB0):
                    for part in (HI, LO):
                        last = pe.matmul(ps_o[:, 32 * h:32 * h + 32], pT[0:KB0, h % RING, part, j, :],
                                         v_s[par][0:KB0, j, h, :, :], start=(h == 0 and j == 0 and part == HI),
                                         stop=(j == NB0 - 1 and part == LO), skip_group_check=True)
                last.then_inc(s_pv, 1)

            def drain(b, par):
                for s in range(4):
                    for lag, stage in ((2, transposes), (4, values)):
                        h = H + s - lag
                        if h < H:
                            stage(b, h) if lag == 2 else stage(b, par, h)

            def body(b, par):
                for s in range(H):
                    scores(b, par, s)
                    if not (first(b) and s < 2):
                        c, _, h = heads(s, 2, b, par)
                        transposes(c, h)
                    if s == 5:
                        values(b, par, 0)
                    if s != 4 and not (first(b) and s < 4):
                        values(*heads(s, 4, b, par))
                    if ahead(b, 1):
                        for k in PSLOT.get(s, []):
                            item(b + 1, 1 - par, k)
                    if not first(b):
                        for k in DSLOT.get(s, []):
                            ditem(b - 1, k)

            pe.wait_ge(s_zero, 4)
            for k in range(PI):
                if k == P_XT:
                    pe.wait_ge(s_const, 48)
                item(0, 0, k)
            run_batches(pe, body)
            drain(B - 1, 1)
            for k in range(DI):
                ditem(B - 1, k)

        @block.scalar
        def _(act):
            def item(c, par, k):
                ps = ps_i[k % 3]
                need(act, s_item, PI, c, k + 1)
                if k == P_Q:
                    need(act, s_qlo, 1, c, 0)
                    for g in range(GROUPS):
                        last = act.activation(q_f[:, g * T:(g + 1) * T], ps[:, g * T:(g + 1) * T], ACT.Identity, bias=bq_c[:, g:g + 1])
                    last.then_inc(s_ifree, 1)
                elif k == P_XT:
                    act.activation(xT[:, HI, :, :], ps[:, 0:KT * T].rearrange("p (t n) -> p t n", t=KT), ACT.Copy).then_inc(s_ihi, 1)
                elif k < P_Q:
                    j = k - P_K
                    if j == 0:
                        need(act, s_kstack, 64, c, 0)
                    act.activation(k_s[:, HI, j, :], ps[:, 0:C], ACT.Identity, bias=bk_c[:, j:j + 1]).then_inc(s_ihi, 1)
                else:
                    j = k - P_V
                    need(act, s_pv, H, c - 1, 0)
                    act.activation(v_s[par][0:KB0, j, :, HI, :],
                                   ps[0:KB0, 0:D].rearrange("p (h d) -> p h d", h=H), ACT.Copy).then_inc(s_ihi, 1)

            def ditem(c, k):
                if k == D_XT:
                    need(act, s_ditem, DI, c, 1)
                    act.activation(x1T[:, HI, :, :], ps_d[0][:, 0:KT * T].rearrange("p (t n) -> p t n", t=KT), ACT.Copy).then_inc(s_dhi, 1)
                elif k == D_CWT:
                    need(act, s_ditem, DI, c, D_CWT + 1)
                    act.activation(cwT[:, HI, :], ps_d[D_CWT % 3][:, 0:T], ACT.Copy).then_inc(s_dhi, 1)
                elif k in D_PAIRS:
                    j = D_PAIRS.index(k)
                    need(act, s_ditem, DI, c, k + 1)
                    if j == 0:
                        need(act, s_route, ROUTE, c, ROUTE)
                    need(act, s_odd, E // 2, c, j - 1)
                    act.activation(scaled[j % 2][:, :], ps_d[k % 3][0:T, D:2 * D], ACT.Identity,
                                   scale=cw[:, 2 * j + 1:2 * j + 2]).then_inc(s_scaled, 1)

            def exps(b, par, h):
                need(act, s_max, H, b, h + 1)
                act.activation(prob[:, h % RING, :], prob[:, h % RING, :], ACT.Exp, bias=top[:, h % RING:h % RING + 1],
                               scale=-1.0, accum_out=sums[par][:, h:h + 1]).then_inc(s_exp, 1)

            def phi(b, h):
                need(act, s_tr, H, b, h + 1)
                need(act, s_pv, H, b, h - RING + 1)
                act.activation(pT[0:KB0, h % RING, HI, :, 0:T],
                               ps_t[h % 2][0:KB0, 0:NB0 * T].rearrange("p (j n) -> p j n", j=NB0), ACT.Copy).then_inc(s_phi, 1)

            def out_lo(c):
                need(act, s_pv, H, c, H)
                act.activation(o_lo[:, :, :], ps_o[0:T, :].rearrange("p (h s d) -> p h s d", h=H, s=2)[:, :, LO, :], ACT.Copy).then_inc(s_olo, 1)

            def experts_high(n):
                act.wait_ge(s_wload, 16)
                act.activation(we_s[:, HI, :, n * WE:(n + 1) * WE], we_f[:, :, n * WE:(n + 1) * WE], ACT.Copy).then_inc(s_wehi, 1)

            def load_next(col):
                act.wait_ge(s_welo, H // 2)
                act.dma_start(next_f[:, bass.ds(col, NLOAD)], next_w_dram[:, bass.ds(col, NLOAD)]).then_inc(s_nload, 16)

            def next_high(n):
                if n == 0:
                    act.wait_ge(s_nload, 16 * 8)
                act.activation(next_w[:, HI, n * NEXT:(n + 1) * NEXT], next_f[:, n * NEXT:(n + 1) * NEXT], ACT.Copy).then_inc(s_nhi, 1)

            def weigh(c):
                need(act, s_route, ROUTE, c, 4)
                act.activation(ratio[:, :], gap[:, :], ACT.Exp).then_inc(s_ratio, 1)

            def body(b, par):
                for s in range(H):
                    if ahead(b, 1):
                        for k in PSLOT.get(s - 1, []):
                            if k != P_Q:
                                item(b + 1, 1 - par, k)
                    if not first(b):
                        if s == 4:
                            out_lo(b - 1)
                        if s == 10:
                            weigh(b - 1)
                        for k in DREAD.get(s, []):
                            if k != D_PAIRS[0]:
                                ditem(b - 1, k)
                    if first(b) and s >= H // 2:
                        experts_high(s - H // 2)
                    if par == 0 and not first(b) and s == 0:
                        load_next(b * (NLOAD // 2) - NLOAD)
                    if isinstance(b, int) and b == B - 2 and s == H // 4:
                        load_next(b * (NLOAD // 2))
                    if not ahead(b, 2) and (s >= H // 2) == ahead(b, 1):
                        next_high((s + H // 2) % H)
                    if not (first(b) and s < 1):
                        exps(*heads(s, 1, b, par))
                    if not first(b) and D_PAIRS[0] in DREAD.get(s, []):
                        ditem(b - 1, D_PAIRS[0])
                    if not (first(b) and s < 2):
                        c, _, h = heads(s, 2, b, par)
                        phi(c, h)
                    if ahead(b, 1) and P_Q in PSLOT.get(s - 1, []):
                        item(b + 1, 1 - par, P_Q)

            act.dma_start(const[:, :], consts).then_inc(s_const, 16)
            act.dma_start(bk_c[:, :], bk).then_inc(s_const, 16)
            act.dma_start(bq_c[:, :], bq).then_inc(s_const, 16)
            for n, (lo, hi) in enumerate(WPARTS):
                act.wait_ge((s_wk, s_wq, s_wv)[n], 16 if n < 2 else 32)
                act.activation(wqkv[:, HI, :, lo:hi], wqkv_f[:, :, lo:hi], ACT.Copy).then_inc(s_whi, 1)
            act.wait_ge(s_const, 48)
            act.wait_ge(s_setup, NSETUP)
            act.activation(tanhs[:, :], gates[:, :], ACT.Tanh).then_inc(s_tanh, 1)
            act.dma_start(we_f[:, :, :], we).then_inc(s_wload, 16)
            for k in range(PI):
                item(0, 0, k)
            run_batches(act, body)
            exps(B - 1, 1, H - 1)
            phi(B - 1, H - 2)
            phi(B - 1, H - 1)
            out_lo(B - 1)
            ditem(B - 1, D_XT)
            weigh(B - 1)
            for k in range(D_PAIRS[0], DI):
                ditem(B - 1, k)

        @block.vector
        def _(dve):
            settled = (s_zero, 4)

            def stats_x(c):
                need(dve, s_xload, 16, c, 16)
                dve.bn_stats(bns[:, :], x_in[:, :]).then_inc(s_stats, 1)

            def moments_x(c):
                need(dve, s_stats, 2, c, 1, settled)
                dve.bn_aggr(mv[:, :], bns[:, :]).then_inc(s_stats, 1)

            def norm_x(c):
                need(dve, s_rstd, 1, c, 1)
                need(dve, s_item, PI, c, 0)
                dve.tensor_scalar(xn[:, :], x_in[:, :], mv[:, 0:1], rstd[:, 0:1], ALU.subtract, ALU.mult).then_inc(s_xn, 1)

            def norm_x1(c):
                need(dve, s_rstd1, 1, c, 1)
                need(dve, s_ditem, DI, c, 0)
                dve.tensor_scalar(xn1[:, :], x1[:, :], mv1[:, 0:1], rstd1[:, 0:1], ALU.subtract, ALU.mult).then_inc(s_xn1, 1)

            def item(c, par, k):
                ps = ps_i[k % 3]
                if k == P_Q:
                    return
                need(dve, s_ihi, 6, c, k + 1 if k < P_Q else k)
                if k == P_XT:
                    dve.tensor_tensor(xT[:, LO, :, :], ps[:, 0:KT * T].rearrange("p (t n) -> p t n", t=KT), xT[:, HI, :, :], ALU.subtract).then_inc(s_ifree, 1)
                elif k < P_Q:
                    j = k - P_K
                    dve.scalar_tensor_tensor(k_s[:, LO, j, :], ps[:, 0:C], bk_c[:, j:j + 1], k_s[:, HI, j, :],
                                             ALU.add, ALU.subtract).then_inc(s_ifree, 1)
                else:
                    j = k - P_V
                    dve.tensor_tensor(v_s[par][0:KB0, j, :, LO, :],
                                      ps[0:KB0, 0:D].rearrange("p (h d) -> p h d", h=H),
                                      v_s[par][0:KB0, j, :, HI, :], ALU.subtract).then_inc(s_ifree, 1)

            def maxima(b, par, h):
                need_all(dve, settled, (s_score, H, b, h + 1), (s_tr, H, b, h - RING + 1), *([(s_keep, 1, b, 1)] if h == 0 else []))
                dve.tensor_tensor_reduce(prob[:, h % RING, :], ps_s[h % 2][0:T, 0:C], keep[par][:, :], -SCALE0, 3e38,
                                         ALU.add, ALU.min, top[:, h % RING:h % RING + 1]).then_inc(s_max, 1)

            def plo(b, h):
                need(dve, s_phi, H, b, h + 1)
                dve.tensor_tensor(pT[0:KB0, h % RING, LO, :, 0:T],
                                  ps_t[h % 2][0:KB0, 0:NB0 * T].rearrange("p (j n) -> p j n", j=NB0),
                                  pT[0:KB0, h % RING, HI, :, 0:T], ALU.subtract).then_inc(s_plo, 1)

            def read_out(c, par):
                need(dve, s_exp, H, c, H)
                dve.reciprocal(rsum[:, :], sums[par][:, :]).then_inc(s_rsum, 1)
                need(dve, s_olo, 1, c, 1)
                dve.tensor_tensor(o_f[:, :, :], ps_o[0:T, :].rearrange("p (h s d) -> p h s d", h=H, s=2)[:, :, HI, :],
                                  o_lo[:, :, :], ALU.add).then_inc(s_oread, 1)
                need(dve, s_rsum, 1, c, 1)
                dve.tensor_scalar(rsum_t[:, :], rsum[:, :], tanhs[0:T, 0:1], None, ALU.mult).then_inc(s_rsumt, 1)

            def stats_x1(c):
                need(dve, s_x1, 1, c, 1)
                dve.bn_stats(bns1[:, :], x1[:, :]).then_inc(s_stats1, 1)
                need(dve, s_stats1, 2, c, 1, settled)
                dve.bn_aggr(mv1[:, :], bns1[:, :]).then_inc(s_stats1, 1)

            def ditem(c, k):
                ps = ps_d[k % 3]
                if k == D_XT:
                    need(dve, s_dhi, 2, c, 1)
                    dve.tensor_tensor(x1T[:, LO, :, :], ps[:, 0:KT * T].rearrange("p (t n) -> p t n", t=KT), x1T[:, HI, :, :], ALU.subtract).then_inc(s_dfree, 1)
                elif k == D_GATE:
                    need(dve, s_ditem, DI, c, k + 1)
                    dve.tensor_copy(logit[:, :], ps[0:T, 0:E]).then_inc(s_dfree, 1)
                elif k == D_CWT:
                    need(dve, s_dhi, 2, c, 2)
                    dve.tensor_tensor(cwT[:, LO, :], ps[:, 0:T], cwT[:, HI, :], ALU.subtract).then_inc(s_dfree, 1)
                elif k == D_BIAS:
                    need(dve, s_ditem, DI, c, k + 1)
                    need(dve, s_dfree, DI, c, k)
                    dve.tensor_tensor(acc[:, :], ps[0:T, 0:D], acc[:, :], ALU.add).then_inc(s_dfree, 1)
                else:
                    j = D_PAIRS.index(k)
                    need(dve, s_scaled, E // 2, c, j + 1)
                    if j == 0:
                        need(dve, s_route, ROUTE, c, ROUTE)
                        need(dve, s_x2, 1, c, 0)
                        dve.tensor_scalar(acc[:, :], ps[0:T, 0:D], cw[:, 0:1], None, ALU.mult).then_inc(s_dfree, 1)
                    else:
                        need(dve, s_dfree, DI, c, k)
                        dve.scalar_tensor_tensor(acc[:, :], ps[0:T, 0:D], cw[:, 2 * j:2 * j + 1], acc[:, :],
                                                 ALU.mult, ALU.add).then_inc(s_dfree, 1)

            def rank_experts(c):
                need(dve, s_dfree, DI, c, D_GATE + 1, settled)
                dve.max(best[:, :], logit[:, :]).then_inc(s_route, 1)
                need(dve, s_route, ROUTE, c, 1, settled)
                dve.max_index(place[:, :], best[:, :], logit[:, :]).then_inc(s_route, 1)
                need(dve, s_route, ROUTE, c, 2)
                dve.tensor_copy(place_f[:, :], place[:, :]).then_inc(s_route, 1)
                dve.tensor_tensor(gap[:, :], best[:, 1:2], best[:, 0:1], ALU.subtract).then_inc(s_route, 1)

            def combine_weights(c):
                need(dve, s_ratio, 1, c, 1)
                dve.tensor_scalar(norm[:, :], ratio[:, :], 1.0, None, ALU.add).then_inc(s_route, 1)
                need(dve, s_route, ROUTE, c, 5)
                dve.reciprocal(share[:, :], norm[:, :]).then_inc(s_route, 1)
                need(dve, s_route, ROUTE, c, 6)
                dve.tensor_scalar(w_top[:, 0:1], share[:, :], tanhs[0:T, 2:3], None, ALU.mult)
                dve.tensor_scalar(w_top[:, 1:2], share[:, :], tanhs[0:T, 2:3], ratio[:, 0:1], ALU.mult, ALU.mult).then_inc(s_route, 1)
                need(dve, s_route, ROUTE, c, 7)
                for n in range(2):
                    last = dve.tensor_scalar(picked[:, n, :], const[0:T, IOTA:IOTA + E], place_f[:, n:n + 1], w_top[:, n:n + 1],
                                             ALU.is_equal, ALU.mult)
                last.then_inc(s_route, 1)
                need(dve, s_route, ROUTE, c, 8)
                dve.tensor_tensor(cw[:, 0:E], picked[:, 0, :], picked[:, 1, :], ALU.add).then_inc(s_route, 1)

            def body(b, par):
                for s in range(H):
                    if not first(b) and s == 8:
                        ditem(b - 1, D_XT)
                    maxima(b, par, s)
                    if ahead(b, 1):
                        if s == 0:
                            stats_x(b + 1)
                        for k in PSLOT.get(s - 1, []):
                            item(b + 1, 1 - par, k)
                    if not first(b):
                        if s == 4:
                            read_out(b - 1, 1 - par)
                        if s == 10:
                            combine_weights(b - 1)
                        for k in DREAD.get(s, []):
                            if k != D_XT:
                                ditem(b - 1, k)
                    if not (first(b) and s < 2):
                        c, _, h = heads(s, 2, b, par)
                        plo(c, h)
                    if ahead(b, 1) and s == 0:
                        moments_x(b + 1)
                    if ahead(b, 1) and s == 1:
                        norm_x(b + 1)
                    if not first(b):
                        if s == 9:
                            rank_experts(b - 1)
                        if s == 5:
                            stats_x1(b - 1)
                        if s == 6:
                            norm_x1(b - 1)

            for i in range(2):
                dve.memset(q_masked[i][:, :, :, :], 0.0).then_inc(s_zq, 1)
            dve.wait_ge(s_zero, 4)
            for n, (lo, hi) in enumerate(WPARTS):
                dve.wait_ge(s_whi, n + 1)
                dve.tensor_tensor(wqkv[:, LO, :, lo:hi], wqkv_f[:, :, lo:hi], wqkv[:, HI, :, lo:hi], ALU.subtract).then_inc(s_wlo, 1)
                if n == 0:
                    stats_x(0)
                    moments_x(0)
                if n == 1:
                    norm_x(0)
            dve.wait_ge(s_const, 48)
            dve.wait_ge(s_setup, NSETUP)
            dve.wait_ge(s_tanh, 1)
            dve.tensor_scalar(bv_t[:, :], bv_r[0:T, :], tanhs[0:T, 0:1], None, ALU.mult).then_inc(s_bvt, 1)
            for k in range(PI):
                item(0, 0, k)
            run_batches(dve, body)
            plo(B - 1, H - 2)
            plo(B - 1, H - 1)
            read_out(B - 1, 1)
            stats_x1(B - 1)
            norm_x1(B - 1)
            ditem(B - 1, D_XT)
            ditem(B - 1, D_GATE)
            rank_experts(B - 1)
            combine_weights(B - 1)
            for k in range(D_PAIRS[0], DI):
                ditem(B - 1, k)

D1 = 64
INNER = H * D1
IT = INNER // 128
NK = C + T
NKP = 488
WKV, WQ, WOUT = KT * 2 * INNER, KT * INNER, IT * D
KB1, NB1 = 122, 4
SCALE1 = D1 ** -0.5
MASKED = 1e30

def phase_attention_large_heads(nc, ctx_tok, mask, g_xattn, g_ffn, g1, b1, g2, b2, wr, br, consts, w_s,
                                x2_dram, x3_dram, x3T_dram, cw_dram, w_next, w_next_dram, s_w_next):
    with ExitStack() as ctx:
        sb = lambda name, shape, dt: ctx.enter_context(nc.sbuf_tensor("b_" + name, shape, dt))
        sem = lambda name: ctx.enter_context(nc.semaphore("b_" + name))
        bank = lambda name: ctx.enter_context(nc.psum_tensor("b_" + name, [128, 512], F32))

        const = sb("const", [128, NCONST], F32)
        ident = const[:, IDENT:IDENT + 128]
        neg_half = sb("neg_half", [128, 4], F32)
        wkv_s = w_s[:, :, 0:WKV].rearrange("p s (k n) -> p s k n", k=KT)
        wq_s = w_s[:, :, WKV:WKV + WQ].rearrange("p s (k n) -> p s k n", k=KT)
        wout_s = w_s[:, :, WKV + WQ:].rearrange("p s (k n) -> p s k n", k=IT)
        wr_f = sb("wr_f", [128, KT, E], F32)
        wr_s = sb("wr_s", [128, 2, KT, E], F16)
        br_r = sb("br_r", [128, E], F32)
        affine = sb("affine", [128, 4, KT], F32)
        gates = sb("gates", [128, 4], F32)
        tanhs = sb("tanhs", [128, 4], F32)

        ctx_t = sb("ctx_t", [KB0, NB0, D], F32)
        x2_t = sb("x2_t", [T, D], F32)
        bns = sb("bns", [128, 4, 6], F32)
        mv = sb("mv", [128, 4, 2], F32)
        var = sb("var", [128, 4], F32)
        rstd = sb("rstd", [128, 4], F32)
        ctx_n = sb("ctx_n", [KB0, NB0, D], F32)
        x2_n = sb("x2_n", [T, D], F32)
        tok_f = sb("tok_f", [128, KT, NK], F32)
        tok_s = [sb(f"tok_s{i}", [128, 2, KT, NKP], F16) for i in range(2)]
        keep_u = sb("keep_u", [T, C], U8)
        keep = [sb(f"keep{i}", [T, NK], F32) for i in range(2)]

        q_s = sb("q_s", [128, 2, IT, T], F16)
        q_dup = [sb(f"q_dup{i}", [128, 2, H, T], F16) for i in range(2)]
        k_s = sb("k_s", [128, 2, IT, NK], F16)
        k_stack = [sb(f"k_stack{i}", [128, H, NK], F16) for i in range(2)]
        v_s = [sb(f"v_s{i}", [128, 2, NB1, INNER], F16) for i in range(2)]

        RING = 4
        prob = sb("prob", [T, RING, NKP], F32)
        top = sb("top", [T, RING], F32)
        sums = [sb(f"sums{i}", [T, H], F32) for i in range(2)]
        pT = sb("pT", [128, 2, 2, NB1, 128], F16)

        x_res = sb("x_res", [T, D], F32)
        rsum = sb("rsum", [T, H], F32)
        o_n = sb("o_n", [T, H, D1], F32)
        oT = sb("oT", [128, 2, IT, T], F16)
        x3 = sb("x3", [T, D], F32)
        bns3 = sb("bns3", [T, 6], F32)
        mv3 = sb("mv3", [T, 2], F32)
        var3 = sb("var3", [T, 1], F32)
        rstd3 = sb("rstd3", [T, 1], F32)
        xn3 = sb("xn3", [T, D], F32)
        x3T = sb("x3T", [128, 2, KT, T], F16)
        logit = sb("logit", [T, E], F32)
        best = sb("best", [T, 8], F32)
        place = sb("place", [T, 8], U32)
        place_f = sb("place_f", [T, 8], F32)
        gap = sb("gap", [T, 1], F32)
        ratio = sb("ratio", [T, 1], F32)
        norm = sb("norm", [T, 1], F32)
        share = sb("share", [T, 1], F32)
        w_top = sb("w_top", [T, 2], F32)
        picked = sb("picked", [T, 2, E], F32)
        cw = sb("cw", [T, E], F32)

        ps_s = [bank(f"ps_s{i}") for i in range(2)]
        ps_t = [bank(f"ps_t{i}") for i in range(2)]
        ps_o = [bank(f"ps_o{i}") for i in range(2)]
        ps_p = [bank(f"ps_p{i}") for i in range(2)]
        ps_x = ps_o[1]

        s_setup = sem("setup")
        s_zero = sem("zero")
        s_wsplit = sem("wsplit")
        s_tanh = sem("tanh")
        s_cload = sem("cload")
        s_xload = sem("xload")
        s_mload = sem("mload")
        s_rload = sem("rload")
        s_keep = sem("keep")
        s_stats = sem("stats")
        s_var = sem("var")
        s_rstd = sem("rstd")
        s_norm = sem("norm")
        s_nitem = sem("nitem")
        s_nfree = sem("nfree")
        s_tsplit = sem("tsplit")
        s_thi = sem("thi")
        s_item = sem("item")
        s_ihi = sem("ihi")
        s_ifree = sem("ifree")
        s_kstack = sem("kstack")
        s_qdup = sem("qdup")
        s_score = sem("score")
        s_max = sem("max")
        s_exp = sem("exp")
        s_tr = sem("tr")
        s_phi = sem("phi")
        s_plo = sem("plo")
        s_pv = sem("pv")
        s_rsum = sem("rsum")
        s_oread = sem("oread")
        s_hitem = sem("hitem")
        s_hhi = sem("hhi")
        s_hfree = sem("hfree")
        s_stats3 = sem("stats3")
        s_var3 = sem("var3")
        s_rstd3 = sem("rstd3")
        s_xn3 = sem("xn3")
        s_route = sem("route")
        s_ratio = sem("ratio")
        s_store = sem("store")

        NSETUP = 16 * 11
        P_K, P_Q, P_V, PI = 0, IT, IT + 2, IT + 2 + 2 * NB1
        N_C, N_L, NI = 0, KT, KT + 1
        H_T, H_O, H_X, H_G, HI_ = 0, 2, 3, 4, 5
        ROUTE = 9
        TOK = [(0, slice(0, C)), (1, slice(0, C)), (slice(None), slice(C, NK))]
        PSLOT, k = {}, 0
        for s, n in enumerate([2, 2, 2, 2, 1, 1, 0, 1, 1, 1, 1, 1, 1, 1, 1]):
            PSLOT[s] = list(range(k, k + n))
            k += n
        assert k == PI
        XSLOT = {3: ("n", 0), 4: ("h", 0), 5: ("h", 1), 6: ("n", 1), 7: ("h", 2), 8: ("n", 2), 9: ("h", 3), 10: ("h", 4)}

        def lent_before(s):
            n = [XSLOT[t][0] for t in XSLOT if t < s]
            return n.count("h"), n.count("n")

        def behind(s, lag, b, par):
            h = s - lag
            return (b, par, h) if h >= 0 else (b - 1, 1 - par, h + H)

        block = ctx.enter_context(nc.Block())

        @block.sync
        def _(sp):
            settled = (s_zero, 8)

            def load(c):
                need(sp, s_norm, 2, c, 0, settled)
                sp.dma_start(ctx_t[:, :, :], ctx_tok[c].rearrange("(j p) d -> p j d", p=KB0)).then_inc(s_cload, 16)
                sp.dma_start(x2_t[:, :], x2_dram[c]).then_inc(s_xload, 16)
                need(sp, s_keep, 1, c, 0, settled)
                sp.dma_start(keep_u[:, :], mask[c].partition_broadcast(T)).then_inc(s_mload, 16)

            def stack(c, par):
                need_all(sp, settled, (s_ihi, PI, c, P_Q), (s_ifree, PI, c, P_Q), (s_score, H, c - 1, 1))
                for a in range(2):
                    for part in (HI, LO):
                        src = k_s[64 * a:64 * a + 64, part, :, :]
                        rows = part if a == 0 else 1 - part
                        sp.dma_start(k_stack[par][64 * rows:64 * rows + 64, a::2, :], src).then_inc(s_kstack, 16)
                need_all(sp, settled, (s_ihi, PI, c, P_V), (s_ifree, PI, c, P_V))
                for a in range(2):
                    for rows in range(2):
                        for part in (HI, LO):
                            sp.dma_start(q_dup[par][64 * rows:64 * rows + 64, part, a::2, :],
                                         q_s[64 * a:64 * a + 64, part, :, :]).then_inc(s_qdup, 16)

            def residual(c):
                need(sp, s_hfree, HI_, c, 0, settled)
                sp.dma_start(x_res[:, :], x2_dram[c]).then_inc(s_rload, 16)

            def store(c):
                need(sp, s_hfree, HI_, c, H_X + 1, settled)
                sp.dma_start(x3_dram[c], x3[:, :]).then_inc(s_store, 16)
                sp.dma_start(x3T_dram[c], x3T[:, :, :, :]).then_inc(s_store, 16)
                need(sp, s_route, ROUTE, c, ROUTE, settled)
                sp.dma_start(cw_dram[c], cw[:, :]).then_inc(s_store, 16)

            def body(b, par):
                if not first(b):
                    residual(b - 1)
                if ahead(b, 2):
                    load(b + 2)
                if ahead(b, 1):
                    stack(b + 1, 1 - par)
                if not first(b):
                    store(b - 1)

            load(0)
            load(1)
            stack(0, 0)
            sp.dma_start(w_next[:, :], w_next_dram).then_inc(s_w_next, 16)
            run_batches(sp, body)
            residual(B - 1)
            store(B - 1)
            sp.wait_ge(s_store, 3 * 16 * B)

        @block.gpsimd
        def _(pool):
            pool.memset(neg_half[:, :], -0.5).then_inc(s_zero, 1)
            pool.memset(mv[:, :, :], 0.0).then_inc(s_zero, 1)
            for i in range(2):
                pool.memset(tok_s[i][:, :, :, NK:NKP], 0.0).then_inc(s_zero, 1)
                pool.memset(keep[i][:, C:NK], 0.0).then_inc(s_zero, 1)
            pool.memset(prob[:, :, NK:NKP], 0.0).then_inc(s_zero, 1)
            pool.memset(pT[:, :, :, :, T:128], 0.0).then_inc(s_zero, 1)

            settled = (s_zero, 8)

            def deviation(c):
                need(pool, s_stats, 8, c, 8, settled)
                pool.tensor_scalar(var[:, 0:NB0], mv[:, 0:NB0, 1], 1.0, EPS, ALU.mult, ALU.add).then_inc(s_var, 1)
                pool.tensor_scalar(var[:, NB0:NB0 + 1], mv[:, NB0:NB0 + 1, 1], 1.0 + EPS, EPS * EPS, ALU.mult, ALU.add).then_inc(s_var, 1)
                need(pool, s_var, 2, c, 2)
                pool.tensor_tensor(rstd[:, :], var[:, :], neg_half[:, :], ALU.pow).then_inc(s_rstd, 1)

            def deviation3(c):
                need(pool, s_stats3, 2, c, 2, settled)
                pool.tensor_scalar(var3[:, :], mv3[:, 1:2], 1.0, EPS, ALU.mult, ALU.add).then_inc(s_var3, 1)
                need(pool, s_var3, 1, c, 1)
                pool.tensor_tensor(rstd3[:, :], var3[:, :], neg_half[0:T, 0:1], ALU.pow).then_inc(s_rstd3, 1)

            def mask_bias(c, par):
                need_all(pool, settled, (s_mload, 16, c, 16), (s_max, H, c - 1, 0))
                pool.tensor_scalar(keep[par][:, 0:C], keep_u[:, :], -1.0, MASKED, ALU.add, ALU.mult).then_inc(s_keep, 1)

            def split_tokens(c, par):
                for k, cols in enumerate(TOK):
                    need_all(pool, settled, (s_nfree, NI, c, k + 1), *([(s_item, PI, c - 1, 0)] if k == 0 else []))
                    if first(c):
                        pool.wait_ge(s_thi, k + 1)
                    else:
                        pool.tensor_copy(tok_s[par][(slice(None), HI) + cols], tok_f[(slice(None),) + cols]).then_inc(s_tsplit, 1)
                        need(pool, s_tsplit, 6, c, 2 * k + 1)
                    pool.tensor_tensor(tok_s[par][(slice(None), LO) + cols], tok_f[(slice(None),) + cols],
                                       tok_s[par][(slice(None), HI) + cols], ALU.subtract).then_inc(s_tsplit, 2 if first(c) else 1)

            def body(b, par):
                if ahead(b, 2):
                    deviation(b + 2)
                if not first(b):
                    deviation3(b - 1)
                if ahead(b, 2):
                    split_tokens(b + 2, par)
                    mask_bias(b + 2, par)

            pool.wait_ge(s_zero, 8)
            deviation(0)
            mask_bias(0, 0)
            split_tokens(0, 0)
            deviation(1)
            mask_bias(1, 1)
            split_tokens(1, 1)
            pool.wait_ge(s_setup, 16 * 9)
            pool.tensor_copy(wr_s[:, HI, :, :], wr_f[:, :, :]).then_inc(s_wsplit, 1)
            pool.wait_ge(s_wsplit, 1)
            pool.tensor_tensor(wr_s[:, LO, :, :], wr_f[:, :, :], wr_s[:, HI, :, :], ALU.subtract).then_inc(s_wsplit, 1)
            run_batches(pool, body)
            deviation3(B - 1)

        @block.tensor
        def _(pe):
            def product(out, sta, mov, tiles=KT):
                for k in range(tiles):
                    for n, (a, m) in enumerate(PASSES):
                        last = pe.matmul(out, sta(a, k), mov(m, k), start=(k == 0 and n == 0),
                                         stop=(k == tiles - 1 and n == 2))
                return last

            def item(c, par, k):
                ps = ps_p[k % 2]
                need(pe, s_ifree, PI, c, max(k - 1, 0))
                if k == 0:
                    need(pe, s_tsplit, 6, c, 6)
                tok = tok_s[par]
                if k < P_Q:
                    last = product(ps[:, 0:NK], lambda a, t: wkv_s[:, a, t, k * 128:(k + 1) * 128],
                                   lambda a, t: tok[:, a, t, 0:NK])
                elif k < P_V:
                    for n in range(4):
                        j = 4 * (k - P_Q) + n
                        last = product(ps[:, n * T:(n + 1) * T], lambda a, t: wq_s[:, a, t, j * 128:(j + 1) * 128],
                                       lambda a, t: tok[:, a, t, C:NK])
                else:
                    j, half = (k - P_V) // 2, (k - P_V) % 2
                    last = product(ps[0:KB1, :], lambda a, t: tok[:, a, t, j * KB1:(j + 1) * KB1],
                                   lambda a, t: wkv_s[:, a, t, INNER + half * 512:INNER + (half + 1) * 512])
                last.then_inc(s_item, 1)

            def nitem(c, k):
                if k == 0:
                    need(pe, s_norm, 2, c, 2)
                if k < N_L:
                    for j in range(NB0):
                        last = pe.transpose(ps_x[:, j * KB0:(j + 1) * KB0], ctx_n[:, j, k * 128:(k + 1) * 128], ident[0:KB0, 0:KB0])
                else:
                    for t in range(KT):
                        last = pe.transpose(ps_x[:, t * T:(t + 1) * T], x2_n[:, t * 128:(t + 1) * 128], ident[0:T, 0:T])
                last.then_inc(s_nitem, 1)

            def hitem(c, k):
                if k < H_O:
                    for n in range(4):
                        j = 4 * k + n
                        last = pe.transpose(ps_x[:, n * T:(n + 1) * T], o_n[:, 2 * j:2 * j + 2, :].rearrange("p h d -> p (h d)"), ident[0:T, 0:T])
                elif k == H_O:
                    need(pe, s_hhi, 3, c, 2)
                    need(pe, s_hfree, HI_, c, 2)
                    last = product(ps_x[0:T, 0:D], lambda a, t: oT[:, a, t, :], lambda a, t: wout_s[:, a, t, :], IT)
                elif k == H_X:
                    need(pe, s_xn3, 1, c, 1)
                    for t in range(KT):
                        last = pe.transpose(ps_x[:, t * T:(t + 1) * T], xn3[:, t * 128:(t + 1) * 128], ident[0:T, 0:T])
                else:
                    need(pe, s_hhi, 3, c, 3)
                    need(pe, s_hfree, HI_, c, H_X + 1)
                    last = product(ps_x[0:T, 0:E], lambda a, t: x3T[:, a, t, :], lambda a, t: wr_s[:, a, t, :])
                last.then_inc(s_hitem, 1)

            def lend(b, s):
                kind, k = XSLOT[s]
                if kind == "h" and first(b) or kind == "n" and not ahead(b, 2):
                    return
                nh, nn = lent_before(s)
                need(pe, s_oread, 2, b, 0)
                if not first(b):
                    need(pe, s_hfree, HI_, b - 1, nh)
                if ahead(b, 2):
                    need(pe, s_nfree, NI, b + 2, nn)
                if kind == "h":
                    hitem(b - 1, k)
                else:
                    nitem(b + 2, k)

            def scores(b, par, h):
                if h == 0:
                    need(pe, s_qdup, 128, b, 128)
                    need(pe, s_kstack, 64, b, 64)
                need(pe, s_max, H, b, h - 1)
                for part in (HI, LO):
                    last = pe.matmul(ps_s[h % 2][0:T, 0:NK], q_dup[par][:, part, h, :], k_stack[par][:, h, :],
                                     start=(part == HI), stop=(part == LO))
                last.then_inc(s_score, 1)

            def transposes(b, h):
                need(pe, s_exp, H, b, h + 1)
                need(pe, s_plo, H, b, h - 1)
                for j in range(NB1):
                    last = pe.transpose(ps_t[h % 2][0:KB1, j * T:(j + 1) * T],
                                        prob[:, h % RING, j * KB1:(j + 1) * KB1], ident[0:T, 0:T])
                last.then_inc(s_tr, 1)

            def values(b, par, h):
                need(pe, s_phi, H, b, h + 1)
                need(pe, s_plo, H, b, h + 1)
                if h == 0:
                    need(pe, s_oread, 2, b, 0)
                    need(pe, s_ihi, PI, b, PI)
                    need(pe, s_ifree, PI, b, PI)
                if h == H // 2:
                    if not first(b):
                        need(pe, s_hfree, HI_, b - 1, HI_)
                    if ahead(b, 2):
                        need(pe, s_nfree, NI, b + 2, NI)
                col = (h % 8) * D1
                for j in range(NB1):
                    for n, (a, m) in enumerate(PASSES):
                        last = pe.matmul(ps_o[h // 8][:, col:col + D1], pT[0:KB1, h % 2, a, j, :],
                                         v_s[par][0:KB1, m, j, h * D1:(h + 1) * D1],
                                         start=(h % 8 == 0 and j == 0 and n == 0),
                                         stop=(j == NB1 - 1 and n == 2), skip_group_check=True)
                last.then_inc(s_pv, 1)

            def body(b, par):
                for s in range(H):
                    scores(b, par, s)
                    if not (first(b) and s < 2):
                        c, _, h = behind(s, 2, b, par)
                        transposes(c, h)
                    if ahead(b, 1):
                        for k in PSLOT.get(s, []):
                            item(b + 1, 1 - par, k)
                    if not (first(b) and s < 3):
                        values(*behind(s, 3, b, par))
                    if s in XSLOT:
                        lend(b, s)

            pe.wait_ge(s_setup, 16 * 9)
            pe.wait_ge(s_zero, 8)
            for c, items in ((0, range(4)), (1, range(4, PI))):
                for k in range(NI):
                    need(pe, s_nfree, NI, c, k)
                    nitem(c, k)
                for k in items:
                    item(0, 0, k)
            pe.wait_ge(s_wsplit, 2)
            run_batches(pe, body)
            transposes(B - 1, H - 2)
            values(B - 1, 1, H - 3)
            transposes(B - 1, H - 1)
            values(B - 1, 1, H - 2)
            values(B - 1, 1, H - 1)
            need(pe, s_oread, 2, B, 0)
            for k in range(HI_):
                need(pe, s_hfree, HI_, B - 1, k)
                hitem(B - 1, k)

        @block.scalar
        def _(act):
            def item(c, par, k):
                ps = ps_p[k % 2]
                need(act, s_item, PI, c, k + 1)
                if k < P_Q:
                    if k == 0:
                        need(act, s_kstack, 64, c, 0)
                    act.activation(k_s[:, HI, k, :], ps[:, 0:NK], ACT.Copy).then_inc(s_ihi, 1)
                elif k < P_V:
                    j = 4 * (k - P_Q)
                    if j == 0:
                        need(act, s_qdup, 128, c, 0)
                    act.activation(q_s[:, HI, j:j + 4, :], ps[:, 0:4 * T].rearrange("p (j n) -> p j n", j=4), ACT.Copy).then_inc(s_ihi, 1)
                else:
                    j, half = (k - P_V) // 2, (k - P_V) % 2
                    need(act, s_pv, H, c - 1, 0)
                    act.activation(v_s[par][0:KB1, HI, j, half * 512:(half + 1) * 512], ps[0:KB1, :], ACT.Copy).then_inc(s_ihi, 1)

            def hitem(c, k):
                if k < H_O:
                    need(act, s_hitem, HI_, c, k + 1)
                    act.activation(oT[:, HI, 4 * k:4 * k + 4, :], ps_x[:, 0:4 * T].rearrange("p (j n) -> p j n", j=4), ACT.Copy).then_inc(s_hhi, 1)
                elif k == H_X:
                    need(act, s_hitem, HI_, c, k + 1)
                    need(act, s_store, 48, c, 0)
                    act.activation(x3T[:, HI, :, :], ps_x[:, 0:KT * T].rearrange("p (t n) -> p t n", t=KT), ACT.Copy).then_inc(s_hhi, 1)

            def exps(b, par, h):
                need(act, s_max, H, b, h + 1)
                act.activation(prob[:, h % RING, 0:NK], prob[:, h % RING, 0:NK], ACT.Exp, bias=top[:, h % RING:h % RING + 1],
                               scale=-1.0, accum_out=sums[par][:, h:h + 1]).then_inc(s_exp, 1)

            def phi(b, h):
                need(act, s_tr, H, b, h + 1)
                need(act, s_pv, H, b, h - 1)
                act.activation(pT[0:KB1, h % 2, HI, :, 0:T],
                               ps_t[h % 2][0:KB1, 0:NB1 * T].rearrange("p (j n) -> p j n", j=NB1), ACT.Copy).then_inc(s_phi, 1)

            def weigh(c):
                need(act, s_route, ROUTE, c, 4)
                act.activation(ratio[:, :], gap[:, :], ACT.Exp).then_inc(s_ratio, 1)

            def body(b, par):
                for s in range(H):
                    if ahead(b, 1):
                        for k in PSLOT.get(s - 1, []):
                            item(b + 1, 1 - par, k)
                    if not first(b):
                        kind, k = XSLOT.get(s - 1, ("", 0))
                        if kind == "h":
                            hitem(b - 1, k)
                        if s == 12:
                            weigh(b - 1)
                    if not (first(b) and s < 1):
                        exps(*behind(s, 1, b, par))
                    if not (first(b) and s < 2):
                        c, _, h = behind(s, 2, b, par)
                        phi(c, h)

            act.dma_start(const[:, :], consts).then_inc(s_setup, 16)
            for n, v in enumerate((g1, b1, g2, b2)):
                act.dma_start(affine[:, n, :], v).then_inc(s_setup, 16)
            act.dma_start(wr_f[:, :, :], wr).then_inc(s_setup, 16)
            act.dma_start(br_r[:, :], br.partition_broadcast(128)).then_inc(s_setup, 16)
            act.dma_start(gates[:, 0:2], g_xattn.partition_broadcast(128)).then_inc(s_setup, 16)
            act.dma_start(gates[:, 2:4], g_ffn.partition_broadcast(128)).then_inc(s_setup, 16)

            act.wait_ge(s_setup, 16 * 9)
            act.wait_ge(s_zero, 8)
            act.activation(tanhs[:, :], gates[:, :], ACT.Tanh).then_inc(s_tanh, 1)
            for k, cols in enumerate(TOK):
                act.wait_ge(s_nfree, k + 1)
                act.activation(tok_s[0][(slice(None), HI) + cols], tok_f[(slice(None),) + cols], ACT.Copy).then_inc(s_thi, 1)
            for k in range(PI):
                item(0, 0, k)
            run_batches(act, body)
            exps(B - 1, 1, H - 1)
            phi(B - 1, H - 2)
            phi(B - 1, H - 1)
            for k in range(HI_):
                hitem(B - 1, k)
            weigh(B - 1)

        @block.vector
        def _(dve):
            settled = (s_zero, 8)

            def stats(c):
                need(dve, s_cload, 16, c, 16)
                for j in range(NB0):
                    dve.bn_stats(bns[0:KB0, j, :], ctx_t[:, j, :]).then_inc(s_stats, 1)
                need(dve, s_xload, 16, c, 16)
                dve.bn_stats(bns[0:T, NB0, :], x2_t[:, :]).then_inc(s_stats, 1)
                need(dve, s_stats, 8, c, 4, settled)
                for j in range(NB0):
                    dve.bn_aggr(mv[0:KB0, j, :], bns[0:KB0, j, :]).then_inc(s_stats, 1)
                dve.bn_aggr(mv[0:T, NB0, :], bns[0:T, NB0, :]).then_inc(s_stats, 1)

            def normalise(c):
                need(dve, s_rstd, 1, c, 1)
                need(dve, s_nitem, NI, c, 0)
                for j in range(NB0):
                    last = dve.tensor_scalar(ctx_n[:, j, :], ctx_t[:, j, :], mv[0:KB0, j, 0:1], rstd[0:KB0, j:j + 1], ALU.subtract, ALU.mult)
                last.then_inc(s_norm, 1)
                dve.tensor_scalar(x2_n[:, :], x2_t[:, :], mv[0:T, NB0, 0:1], rstd[0:T, NB0:NB0 + 1], ALU.subtract, ALU.mult).then_inc(s_norm, 1)

            def nitem(c, k):
                need(dve, s_nitem, NI, c, k + 1)
                if k == 0:
                    need(dve, s_tsplit, 6, c, 0)
                if k < N_L:
                    dve.tensor_scalar(tok_f[:, k, 0:C], ps_x[:, 0:C], affine[:, 0, k:k + 1], affine[:, 1, k:k + 1], ALU.mult, ALU.add).then_inc(s_nfree, 1)
                else:
                    for t in range(KT):
                        last = dve.tensor_scalar(tok_f[:, t, C:NK], ps_x[:, t * T:(t + 1) * T], affine[:, 2, t:t + 1], affine[:, 3, t:t + 1], ALU.mult, ALU.add)
                    last.then_inc(s_nfree, 1)

            def item(c, par, k):
                ps = ps_p[k % 2]
                need(dve, s_ihi, PI, c, k + 1)
                if k < P_Q:
                    dve.tensor_tensor(k_s[:, LO, k, :], ps[:, 0:NK], k_s[:, HI, k, :], ALU.subtract).then_inc(s_ifree, 1)
                elif k < P_V:
                    j = 4 * (k - P_Q)
                    dve.tensor_tensor(q_s[:, LO, j:j + 4, :], ps[:, 0:4 * T].rearrange("p (j n) -> p j n", j=4), q_s[:, HI, j:j + 4, :], ALU.subtract).then_inc(s_ifree, 1)
                else:
                    j, half = (k - P_V) // 2, (k - P_V) % 2
                    cols = slice(half * 512, (half + 1) * 512)
                    dve.tensor_tensor(v_s[par][0:KB1, LO, j, cols], ps[0:KB1, :], v_s[par][0:KB1, HI, j, cols], ALU.subtract).then_inc(s_ifree, 1)

            def maxima(b, par, h):
                need_all(dve, settled, (s_score, H, b, h + 1), (s_tr, H, b, h - RING + 1), *([(s_keep, 1, b, 1)] if h == 0 else []))
                dve.tensor_tensor_reduce(prob[:, h % RING, 0:NK], ps_s[h % 2][0:T, 0:NK], keep[par][:, :], -SCALE1, 3e38,
                                         ALU.add, ALU.min, top[:, h % RING:h % RING + 1]).then_inc(s_max, 1)

            def plo(b, h):
                need(dve, s_phi, H, b, h + 1)
                dve.tensor_tensor(pT[0:KB1, h % 2, LO, :, 0:T],
                                  ps_t[h % 2][0:KB1, 0:NB1 * T].rearrange("p (j n) -> p j n", j=NB1),
                                  pT[0:KB1, h % 2, HI, :, 0:T], ALU.subtract).then_inc(s_plo, 1)

            def out_heads(c, par):
                need(dve, s_exp, H, c, H)
                dve.reciprocal(rsum[:, :], sums[par][:, :]).then_inc(s_rsum, 1)
                need(dve, s_rsum, 1, c, 1)
                need(dve, s_pv, H, c, H)
                need(dve, s_hitem, HI_, c, 0)
                for i in range(2):
                    dve.tensor_tensor(o_n[:, 8 * i:8 * i + 8, :], ps_o[i][0:T, :].rearrange("p (h d) -> p h d", h=8),
                                      rsum[:, 8 * i:8 * i + 8].unsqueeze(2).to_broadcast([T, 8, D1]), ALU.mult).then_inc(s_oread, 1)

            def hitem(c, k):
                if k < H_O:
                    need(dve, s_hhi, 3, c, k + 1)
                    dve.tensor_tensor(oT[:, LO, 4 * k:4 * k + 4, :], ps_x[:, 0:4 * T].rearrange("p (j n) -> p j n", j=4), oT[:, HI, 4 * k:4 * k + 4, :], ALU.subtract).then_inc(s_hfree, 1)
                elif k == H_O:
                    need(dve, s_hitem, HI_, c, k + 1)
                    need(dve, s_rload, 16, c, 16)
                    need(dve, s_store, 48, c, 0)
                    dve.scalar_tensor_tensor(x3[:, :], ps_x[0:T, 0:D], tanhs[0:T, 1:2], x_res[:, :], ALU.mult, ALU.add).then_inc(s_hfree, 1)
                    need(dve, s_hfree, HI_, c, k + 1)
                    dve.bn_stats(bns3[:, :], x3[:, :]).then_inc(s_stats3, 1)
                    need(dve, s_stats3, 2, c, 1, settled)
                    dve.bn_aggr(mv3[:, :], bns3[:, :]).then_inc(s_stats3, 1)
                elif k == H_X:
                    need(dve, s_hhi, 3, c, 3)
                    dve.tensor_tensor(x3T[:, LO, :, :], ps_x[:, 0:KT * T].rearrange("p (t n) -> p t n", t=KT), x3T[:, HI, :, :], ALU.subtract).then_inc(s_hfree, 1)
                else:
                    need(dve, s_hitem, HI_, c, k + 1)
                    dve.tensor_tensor(logit[:, :], ps_x[0:T, 0:E], br_r[0:T, :], ALU.add).then_inc(s_hfree, 1)
                    need(dve, s_hfree, HI_, c, k + 1, settled)
                    dve.max(best[:, :], logit[:, :]).then_inc(s_route, 1)
                    need(dve, s_route, ROUTE, c, 1, settled)
                    dve.max_index(place[:, :], best[:, :], logit[:, :]).then_inc(s_route, 1)
                    need(dve, s_route, ROUTE, c, 2)
                    dve.tensor_copy(place_f[:, :], place[:, :]).then_inc(s_route, 1)
                    dve.tensor_tensor(gap[:, :], best[:, 1:2], best[:, 0:1], ALU.subtract).then_inc(s_route, 1)

            def norm_x3(c):
                need(dve, s_rstd3, 1, c, 1)
                dve.tensor_scalar(xn3[:, :], x3[:, :], mv3[:, 0:1], rstd3[:, 0:1], ALU.subtract, ALU.mult).then_inc(s_xn3, 1)

            def combine_weights(c):
                need(dve, s_ratio, 1, c, 1)
                dve.tensor_scalar(norm[:, :], ratio[:, :], 1.0, None, ALU.add).then_inc(s_route, 1)
                need(dve, s_route, ROUTE, c, 5)
                dve.reciprocal(share[:, :], norm[:, :]).then_inc(s_route, 1)
                need(dve, s_route, ROUTE, c, 6)
                dve.tensor_scalar(w_top[:, 0:1], share[:, :], tanhs[0:T, 3:4], None, ALU.mult)
                dve.tensor_scalar(w_top[:, 1:2], share[:, :], tanhs[0:T, 3:4], ratio[:, 0:1], ALU.mult, ALU.mult).then_inc(s_route, 1)
                need(dve, s_route, ROUTE, c, 7)
                for n in range(2):
                    last = dve.tensor_scalar(picked[:, n, :], const[0:T, IOTA:IOTA + E], place_f[:, n:n + 1], w_top[:, n:n + 1],
                                             ALU.is_equal, ALU.mult)
                last.then_inc(s_route, 1)
                need(dve, s_route, ROUTE, c, 8)
                dve.tensor_tensor(cw[:, :], picked[:, 0, :], picked[:, 1, :], ALU.add).then_inc(s_route, 1)

            def body(b, par):
                for s in range(H):
                    if ahead(b, 1):
                        for k in PSLOT.get(s - 1, []):
                            item(b + 1, 1 - par, k)
                    if not first(b) and s == 3:
                        out_heads(b - 1, 1 - par)
                    kind, k = XSLOT.get(s - 1, ("", 0))
                    if kind == "h" and not first(b):
                        hitem(b - 1, k)
                    if kind == "n" and ahead(b, 2):
                        nitem(b + 2, k)
                    if not first(b):
                        if s == 9:
                            norm_x3(b - 1)
                        if s == 13:
                            combine_weights(b - 1)
                    if ahead(b, 2):
                        if s == 1:
                            stats(b + 2)
                        if s == 2:
                            normalise(b + 2)
                    maxima(b, par, s)
                    if not (first(b) and s < 2):
                        c, _, h = behind(s, 2, b, par)
                        plo(c, h)

            dve.wait_ge(s_zero, 8)
            stats(0)
            normalise(0)
            dve.wait_ge(s_setup, 16 * 9)
            dve.wait_ge(s_tanh, 1)
            for k in range(NI):
                nitem(0, k)
            stats(1)
            for k in range(2):
                item(0, 0, k)
            normalise(1)
            for k in range(2, 4):
                item(0, 0, k)
            for k in range(NI):
                nitem(1, k)
            for k in range(4, PI):
                item(0, 0, k)
            run_batches(dve, body)
            plo(B - 1, H - 2)
            plo(B - 1, H - 1)
            out_heads(B - 1, 1)
            for k in range(H_X):
                hitem(B - 1, k)
            norm_x3(B - 1)
            hitem(B - 1, H_X)
            hitem(B - 1, H_G)
            combine_weights(B - 1)

F = 512
FT = F // 128
W1N, W2N = KT * 2 * F, FT * D
NG = 4
GB = B // NG
G = GB * T
NT = B * T // 128
YB = 4
TILES = [range(g * G // 128, (g + 1) * G // 128) for g in range(NG)]

def phase_experts(nc, w_all, w_f0, s_w0, b2, consts, x3_dram, x3T_dram, cw_dram, out):
    with ExitStack() as ctx:
        sb = lambda name, shape, dt: ctx.enter_context(nc.sbuf_tensor("c_" + name, shape, dt))
        sem = lambda name: ctx.enter_context(nc.semaphore("c_" + name))
        bank = lambda name: ctx.enter_context(nc.psum_tensor("c_" + name, [128, 512], F32))

        const = sb("const", [128, NCONST], F32)
        ident = const[:, IDENT:IDENT + 128]
        x_T = sb("x_T", [128, B, 2, KT, T], F16)
        x3 = sb("x3", [128, NT, D], F32)
        acc = sb("acc", [128, NT, D], F32)
        cw = sb("cw", [128, NT, E], F32)
        cw_e = [sb(f"cw_e{i}", [128, NT], F32) for i in range(2)]
        cwT_f = sb("cwT_f", [NT * E, 128], F32)
        cwT_s = sb("cwT_s", [NT * E, 2, 128], F16)
        cwT_b = sb("cwT_b", [NT * E, 2, NT, 128], F16)
        b2_f = sb("b2_f", [128, D], F32)
        b2_s = sb("b2_s", [128, 2, D], F16)
        w_f = [w_f0, sb("w_f1", [128, W1N + W2N + 8], F32)]
        w_s = [sb(f"w_s{i}", [128, 2, W1N + W2N], F16) for i in range(2)]
        b1 = [sb(f"b1{i}", [128, 8], F32) for i in range(2)]
        sil = sb("sil", [128, 2, G], F32)
        act_f = sb("act_f", [128, 2, G], F32)
        act_s = sb("act_s", [128, 2, FT, 2 * G], F16)

        ps_a = [bank(f"ps_a{i}") for i in range(2)]
        ps_g = [bank(f"ps_g{i}") for i in range(2)]
        ps_y = [bank(f"ps_y{i}") for i in range(YB)]

        s_setup = sem("setup")
        s_xT = sem("xT")
        s_x3 = sem("x3")
        s_xw = sem("xw")
        s_whi = sem("whi")
        s_cw = sem("cw")
        s_cwT = sem("cwT")
        s_cwf = sem("cwf")
        s_cws = sem("cws")
        s_cwb = sem("cwb")
        s_b2 = sem("b2")
        s_bias = sem("bias")
        s_acc = sem("acc")
        s_wload = sem("wload")
        s_wsplit = sem("wsplit")
        s_cwe = sem("cwe")
        s_a = sem("a")
        s_g = sem("g")
        s_sil = sem("sil")
        s_act = sem("act")
        s_ahi = sem("ahi")
        s_alo = sem("alo")
        s_y = sem("y")
        s_yread = sem("yread")
        s_store = sem("store")

        BIAS_G = 1
        PAIRS = NG * FT

        def run_experts(eng, body):
            body(0, 0)
            body(1, 1)
            with eng.Fori(1, E // 2) as i:
                body(i * 2, 0)
                body(i * 2 + 1, 1)

        block = ctx.enter_context(nc.Block())

        @block.sync
        def _(sp):
            settled = (s_setup, 16)

            def load(e, par):
                sp.dma_start(w_f[par][:, :], w_all[e]).then_inc(s_wload, 16)

            for g in range(NG):
                sp.dma_start(x_T[:, g * GB:(g + 1) * GB, :, :, :],
                             x3T_dram[g * GB:(g + 1) * GB].rearrange("b p s k n -> p b s k n")).then_inc(s_xw if g else s_xT, 16)
                if g == 0:
                    sp.dma_start(cw[:, :, :], cw_dram.rearrange("b t e -> (b t) e").rearrange("(j p) e -> p j e", p=128)).then_inc(s_cw, 16)
                    sp.dma_start(const[:, :], consts).then_inc(s_setup, 16)
                    sp.dma_start(b2_f[:, :], b2).then_inc(s_b2, 16)
            sp.dma_start(x3[:, :, :], x3_dram.rearrange("b t d -> (b t) d").rearrange("(j p) d -> p j d", p=128)).then_inc(s_x3, 16)
            load(1, 1)
            with sp.Fori(0, E // 2 - 1) as i:
                for par in range(2):
                    need(sp, s_wsplit, 3, i * 2 + par + 1, 1, settled)
                    load(i * 2 + par + 2, par)
            out_tiles = out.rearrange("b t d -> (b t) d").rearrange("(j p) d -> p j d", p=128)
            for g in range(NG):
                lo, hi = TILES[g][0], TILES[g][-1] + 1
                need(sp, s_yread, NT, E - 1, hi)
                sp.dma_start(out_tiles[:, lo:hi, :], acc[:, lo:hi, :]).then_inc(s_store, 16)
            sp.wait_ge(s_store, 16 * NG)

        @block.gpsimd
        def _(pool):
            settled = (s_setup, 16)

            def split_weights(e, par):
                need_all(pool, settled, (s_wload, 16, e, 0), (s_y, NT, e - 1, 0), (s_act, PAIRS, e - 1, 0))
                pool.tensor_copy(w_s[par][:, HI, :], w_f[par][:, 0:W1N + W2N]).then_inc(s_wsplit, 1)
                need(pool, s_wsplit, 3, e, 1)
                pool.tensor_tensor(w_s[par][:, LO, :], w_f[par][:, 0:W1N + W2N], w_s[par][:, HI, :], ALU.subtract).then_inc(s_wsplit, 1)
                pool.tensor_copy(b1[par][:, :], w_f[par][:, W1N + W2N:]).then_inc(s_wsplit, 1)

            pool.wait_ge(s_b2, 16)
            pool.tensor_copy(b2_s[:, HI, :], b2_f[:, :]).then_inc(s_b2, 1)
            pool.wait_ge(s_b2, 17)
            pool.tensor_tensor(b2_s[:, LO, :], b2_f[:, :], b2_s[:, HI, :], ALU.subtract).then_inc(s_b2, 1)
            pool.wait_ge(s_cwf, 1)
            pool.tensor_copy(cwT_s[:, HI, :], cwT_f[:, :]).then_inc(s_cws, 1)
            pool.wait_ge(s_cws, 1)
            pool.tensor_tensor(cwT_s[:, LO, :], cwT_f[:, :], cwT_s[:, HI, :], ALU.subtract).then_inc(s_cws, 1)
            pool.wait_ge(s_cws, 2)
            pool.wait_ge(s_setup, 16)
            for part in (HI, LO):
                pool.tensor_tensor(cwT_b[:, part, :, :], cwT_s[:, part, :].unsqueeze(1).to_broadcast([NT * E, NT, 128]),
                                   const[0:NT * E, TILEMASK:TILEMASK + NT].unsqueeze(2).to_broadcast([NT * E, NT, 128]), ALU.mult).then_inc(s_cwb, 1)
            split_weights(1, 1)
            with pool.Fori(0, E // 2 - 1) as i:
                split_weights(i * 2 + 2, 0)
                split_weights(i * 2 + 3, 1)

        @block.tensor
        def _(pe):
            def product(out_, sta, mov, tiles):
                for k in range(tiles):
                    for n, (a, m) in enumerate(PASSES):
                        last = pe.matmul(out_, sta(a, k), mov(m, k), start=(k == 0 and n == 0),
                                         stop=(k == tiles - 1 and n == 2))
                return last

            def hidden(e, par, g, m):
                n = g * FT + m
                w1 = w_s[par][:, :, 0:W1N].rearrange("p s (k n) -> p s k n", k=KT)
                xg = lambda a, t: x_T[:, g * GB:(g + 1) * GB, a, t, :]
                need(pe, s_sil, PAIRS, e, n - 1)
                product(ps_a[n % 2][:, 0:G], lambda a, t: w1[:, a, t, m * 128:(m + 1) * 128], xg, KT).then_inc(s_a, 1)
                need(pe, s_act, PAIRS, e, n - 1)
                product(ps_g[n % 2][:, 0:G], lambda a, t: w1[:, a, t, F + m * 128:F + (m + 1) * 128], xg, KT).then_inc(s_g, 1)

            def outputs(e, par, g):
                w2 = w_s[par][:, :, W1N:].rearrange("p s (k n) -> p s k n", k=FT)
                need(pe, s_alo, PAIRS, e, (g + 1) * FT)
                for j in TILES[g]:
                    if j >= YB or not first(e):
                        need(pe, s_yread, NT, e, max(j - YB + 1, 0))
                    at = j * 128 % (2 * G)
                    product(ps_y[j % YB][:, 0:D], lambda a, t: act_s[:, a, t, at:at + 128],
                            lambda a, t: w2[:, a, t, :], FT).then_inc(s_y, 1)

            def biases():
                pe.wait_ge(s_cwb, 2)
                for j in range(NT):
                    if j >= YB:
                        pe.wait_ge(s_acc, j - YB + 1)
                    for n, (a, m) in enumerate(PASSES):
                        last = pe.matmul(ps_y[j % YB][:, 0:D], cwT_b[:, a, j, :], b2_s[0:NT * E, m, :], start=(n == 0), stop=(n == 2))
                    last.then_inc(s_bias, 1)

            def body(e, par):
                if first(e):
                    pe.wait_ge(s_wsplit, 1)
                else:
                    need(pe, s_wsplit, 3, e, 2)
                for g in range(NG):
                    if first(e):
                        if g:
                            pe.wait_ge(s_xw, 16 * (NG - 1))
                        else:
                            pe.wait_ge(s_xT, 16)
                    for m in range(FT):
                        hidden(e, par, g, m)
                        if first(e) and g == 0 and m == 1:
                            pe.wait_ge(s_cw, 16)
                            pe.wait_ge(s_setup, 16)
                            pe.transpose(ps_y[0][0:NT * E, 0:128], cw[:, :, :].rearrange("p j e -> p (j e)"), ident[:, :]).then_inc(s_cwT, 1)
                        if first(e) and g == BIAS_G and m == 1:
                            biases()
                            pe.wait_ge(s_acc, NT)
                            pe.wait_ge(s_wsplit, 2)
                        if m == 1 and g > 0:
                            outputs(e, par, g - 1)
                        if m == 1 and g == 0 and not first(e):
                            outputs(e - 1, 1 - par, NG - 1)

            run_experts(pe, body)
            outputs(E - 1, 1, NG - 1)

        @block.scalar
        def _(act):
            def silu(e, par, n):
                m = n % FT
                if n == 0:
                    need(act, s_wsplit, 3, e, 3)
                need(act, s_a, PAIRS, e, n + 1)
                need(act, s_act, PAIRS, e, n - 1)
                act.activation(sil[:, n % 2, :], ps_a[n % 2][:, 0:G], ACT.Silu, bias=b1[par][:, m:m + 1]).then_inc(s_sil, 1)

            def high(e, n):
                g, m = n // FT, n % FT
                need(act, s_act, PAIRS, e, n + 1)
                if m == 0:
                    if g >= 2:
                        need(act, s_y, NT, e, (g - 1) * G // 128 + ((g - 1) * G % 128 > 0))
                    else:
                        need(act, s_y, NT, e - 1, (NG + g - 1) * G // 128 + ((g - 1) * G % 128 > 0))
                act.activation(act_s[:, HI, m, g % 2 * G:(g % 2 + 1) * G], act_f[:, n % 2, :], ACT.Copy).then_inc(s_ahi, 1)

            def body(e, par):
                for n in range(PAIRS):
                    silu(e, par, n)
                    if n:
                        high(e, n - 1)
                    if first(e) and n == 1:
                        act.wait_ge(s_cwT, 1)
                        act.activation(cwT_f[:, :], ps_y[0][0:NT * E, 0:128], ACT.Copy).then_inc(s_cwf, 1)
                high(e, PAIRS - 1)

            act.wait_ge(s_w0, 16)
            act.activation(w_s[0][:, HI, 0:W1N], w_f[0][:, 0:W1N], ACT.Copy).then_inc(s_whi, 1)
            act.activation(w_s[0][:, HI, W1N:], w_f[0][:, W1N:W1N + W2N], ACT.Copy).then_inc(s_whi, 1)
            run_experts(act, body)

        @block.vector
        def _(dve):
            def product_act(e, par, n):
                m = n % FT
                need(dve, s_sil, PAIRS, e, n + 1)
                need(dve, s_g, PAIRS, e, n + 1)
                need(dve, s_alo, PAIRS, e, n - 1)
                dve.scalar_tensor_tensor(act_f[:, n % 2, :], ps_g[n % 2][:, 0:G], b1[par][:, FT + m:FT + m + 1], sil[:, n % 2, :],
                                         ALU.add, ALU.mult).then_inc(s_act, 1)

            def low(e, n):
                g, m = n // FT, n % FT
                need(dve, s_ahi, PAIRS, e, n + 1)
                half = slice(g % 2 * G, (g % 2 + 1) * G)
                dve.tensor_tensor(act_s[:, LO, m, half], act_f[:, n % 2, :], act_s[:, HI, m, half], ALU.subtract).then_inc(s_alo, 1)

            def add(e, par, g):
                for j in TILES[g]:
                    need(dve, s_y, NT, e, j + 1)
                    need(dve, s_yread, NT, e, 0)
                    dve.scalar_tensor_tensor(acc[:, j, :], ps_y[j % YB][:, 0:D], cw_e[par][:, j:j + 1], acc[:, j, :],
                                             ALU.mult, ALU.add).then_inc(s_yread, 1)

            def start_sums():
                dve.wait_ge(s_x3, 16)
                for j in range(NT):
                    dve.wait_ge(s_bias, j + 1)
                    dve.tensor_tensor(acc[:, j, :], ps_y[j % YB][:, 0:D], x3[:, j, :], ALU.add).then_inc(s_acc, 1)
                dve.wait_ge(s_acc, NT)

            def body(e, par):
                need(dve, s_yread, NT, e - 1, 0)
                dve.tensor_copy(cw_e[par][:, :], cw[:, :, bass.ds(e, 1)].rearrange("p j o -> p (j o)")).then_inc(s_cwe, 1)
                need(dve, s_cwe, 1, e, 1)
                for n in range(PAIRS):
                    product_act(e, par, n)
                    if n:
                        low(e, n - 1)
                    if first(e) and n == BIAS_G * FT + 1:
                        start_sums()
                    if n % FT == 2 and n > FT:
                        add(e, par, n // FT - 1)
                    if n == 2 and not first(e):
                        add(e - 1, 1 - par, NG - 1)
                low(e, PAIRS - 1)

            dve.wait_ge(s_w0, 16)
            for n, cols in enumerate((slice(0, W1N), slice(W1N, W1N + W2N))):
                dve.wait_ge(s_whi, n + 1)
                dve.tensor_tensor(w_s[0][:, LO, cols], w_f[0][:, cols], w_s[0][:, HI, cols], ALU.subtract).then_inc(s_wsplit, 1)
            dve.tensor_copy(b1[0][:, :], w_f[0][:, W1N + W2N:]).then_inc(s_wsplit, 1)
            dve.wait_ge(s_cw, 16)
            run_experts(dve, body)
            add(E - 1, 1, NG - 1)

def build_program(nc, a, out):
    x2 = nc.dram_tensor("x2", (B, T, D), F32, kind="Internal").ap()
    x3 = nc.dram_tensor("x3", (B, T, D), F32, kind="Internal").ap()
    x3T = nc.dram_tensor("x3T", (B, 128, 2, KT, T), F16, kind="Internal").ap()
    cw = nc.dram_tensor("cw", (B, T, E), F32, kind="Internal").ap()
    with nc.sbuf_tensor("w_e0", [128, W1N + W2N + 8], F32) as w_e0, nc.semaphore("w_e0_load") as s_w_e0:
        with nc.sbuf_tensor("w1_s", [128, 2, WKV + WQ + WOUT], F16) as w1_s:
            phase_attention_small_heads(nc, a["x"], a["ctxT"], a["mask0"], a["g_xattn"], a["g_ffn"], a["wq0"], a["wk0"],
                                        a["wv0"], a["bq0"], a["bk0"], a["bv0"], a["wg0"], a["we0"], a["be0"], a["consts"],
                                        x2, w1_s, a["w1"])
            phase_attention_large_heads(nc, a["ctx"], a["mask1"], a["g_xattn"], a["g_ffn"], a["g1"], a["b1"], a["g2"],
                                        a["b2"], a["wr1"], a["br1"], a["consts"], w1_s, x2, x3, x3T, cw,
                                        w_e0, a["w_experts"][0], s_w_e0)
        phase_experts(nc, a["w_experts"], w_e0, s_w_e0, a["b2_experts"], a["consts"], x3, x3T, cw, out)

def kernel(x, ctx_1024, mask_BxSxS2_ff1, mask_BxS2_bk0, g_xattn, g_ffn,
           L0_xattn_Wq, L0_xattn_bq, L0_xattn_Wk, L0_xattn_bk, L0_xattn_Wv, L0_xattn_bv,
           L0_ffn_Wg, L0_ffn_We, L0_ffn_be,
           L1_xattn_g1, L1_xattn_b1, L1_xattn_g2, L1_xattn_b2, L1_xattn_Wq, L1_xattn_Wkv, L1_xattn_Wout,
           L1_ffn_W1, L1_ffn_b1, L1_ffn_W2, L1_ffn_b2, L1_ffn_Wr, L1_ffn_br):
    import numpy as np
    import concourse.bacc as bacc
    from concourse.bass_utils import run_bass_kernel_spmd

    rows = lambda w: w.reshape(-1, 128, w.shape[-1]).transpose(1, 0, 2)
    column = lambda v: v.reshape(-1, 128).T
    twice = lambda w: np.concatenate([w, w], -1)

    p = np.arange(128)
    consts = np.zeros((128, NCONST), np.float32)
    consts[:, IDENT:IDENT + 128] = np.eye(128)
    consts[:, IOTA:IOTA + E] = np.arange(E)
    consts[:, TILEMASK:TILEMASK + NT] = p[:, None] // E == np.arange(NT)

    as_np = np.asarray
    experts = [as_np(L1_ffn_W1).reshape(E, KT, 128, 2 * F).transpose(0, 2, 1, 3).reshape(E, 128, W1N),
               as_np(L1_ffn_W2).reshape(E, FT, 128, D).transpose(0, 2, 1, 3).reshape(E, 128, W2N),
               as_np(L1_ffn_b1).reshape(E, 2 * FT, 128).transpose(0, 2, 1)]
    arrays = {
        "x": as_np(x), "ctx": as_np(ctx_1024), "consts": consts,
        "ctxT": as_np(ctx_1024).reshape(B, C, KT, 128).transpose(0, 3, 2, 1),
        "mask0": as_np(mask_BxSxS2_ff1), "mask1": as_np(mask_BxS2_bk0),
        "g_xattn": as_np(g_xattn), "g_ffn": as_np(g_ffn),
        "wq0": rows(twice(as_np(L0_xattn_Wq).T.reshape(D, GROUPS, 64)).reshape(D, 128 * GROUPS)),
        "bq0": twice(as_np(L0_xattn_bq).reshape(GROUPS, 64)).T,
        "wk0": rows(as_np(L0_xattn_Wk).T), "bk0": column(as_np(L0_xattn_bk)),
        "wv0": rows(as_np(L0_xattn_Wv).T), "bv0": as_np(L0_xattn_bv),
        "wg0": rows(as_np(L0_ffn_Wg).T), "we0": rows(as_np(L0_ffn_We).transpose(2, 0, 1).reshape(D, E * D)),
        "be0": as_np(L0_ffn_be),
        "g1": column(as_np(L1_xattn_g1)), "b1": column(as_np(L1_xattn_b1)),
        "g2": column(as_np(L1_xattn_g2)), "b2": column(as_np(L1_xattn_b2)),
        "w1": np.concatenate([rows(as_np(w)).reshape(128, -1) for w in (L1_xattn_Wkv, L1_xattn_Wq, L1_xattn_Wout)], 1),
        "wr1": rows(as_np(L1_ffn_Wr)), "br1": as_np(L1_ffn_br),
        "w_experts": np.concatenate(experts, 2), "b2_experts": np.tile(as_np(L1_ffn_b2), (B, 1)),
    }
    nc = bacc.Bacc("TRN2", target_bir_lowering=False, num_devices=1)
    inputs, aps = {}, {}
    for name, array in arrays.items():
        array = np.ascontiguousarray(array)
        inputs[f"in_{name}"] = array
        aps[name] = nc.dram_tensor(f"in_{name}", array.shape, mybir.dt.from_np(array.dtype), kind="ExternalInput").ap()
    out = nc.dram_tensor("out", (B, T, D), F32, kind="ExternalOutput").ap()
    build_program(nc, aps, out)
    result = run_bass_kernel_spmd(nc, [inputs], core_ids=[0])
    return result.results[0]["out"]
```
